# Optimizing a Trainium2 kernel written in Bass

```python
import numpy as np
import jax
import jax.numpy as jnp

def _softmax(x, axis=-1):
    return jax.nn.softmax(x, axis=axis)
def _gelu(x):
    return jax.nn.gelu(x, approximate=True)
def _silu(x):
    return jax.nn.silu(x)
def _sigmoid(x):
    return jax.nn.sigmoid(x)
def _layernorm(x, axis=-1, eps=1e-5):
    m = jnp.mean(x, axis=axis, keepdims=True)
    v = jnp.var(x, axis=axis, keepdims=True)
    return (x - m) / jnp.sqrt(v + eps)
def _scatter_add(tgt, idx, src, axis=0):
    return tgt.at[idx].add(src)
def _segment_sum(src, seg, n):
    return jax.ops.segment_sum(src, seg, n)

kernel_name = 'mk_metaformer_d1_conv_nchw256_cc0a94'

def setup_inputs(seed: int = 0):
    np.random.seed(seed)
    _w = jnp.asarray
    def _rec_inputs():
        import jax
        import jax.numpy as jnp
        _gk = jax.random.key(seed)
        x = 7.22e-05 + 1 * jax.random.normal(jax.random.fold_in(_gk, 1), (8, 256, 64, 64), jnp.float32)
        return x
    x = _rec_inputs()
    def _L0_conv_setup():
        import jax, jax.numpy as jnp
        import numpy as np
        N, C, H, W = (8, 256, 64, 64)
        G, K_, DIL, STRIDE, PAD, OFFSET_SCALE = (8, 3, 1, 1, 1, 1.0)
        P = K_ * K_
        OM_DIM = int(np.ceil(G * P * 3 / 8) * 8)

        def _dcn_core(v, offset, mask):
            n, h, w, c = v.shape
            gc = c // G
            vp = jnp.pad(v, ((0, 0), (PAD, PAD), (PAD, PAD), (0, 0)))
            Hin, Win = (h + 2 * PAD, w + 2 * PAD)
            Ho = (Hin - (DIL * (K_ - 1) + 1)) // STRIDE + 1
            Wo = (Win - (DIL * (K_ - 1) + 1)) // STRIDE + 1
            Lo = Ho * Wo
            ry = (DIL * (K_ - 1) // 2 + 0.5 + jnp.arange(Ho, dtype=jnp.float32) * STRIDE) / Hin
            rx = (DIL * (K_ - 1) // 2 + 0.5 + jnp.arange(Wo, dtype=jnp.float32) * STRIDE) / Win
            ref = jnp.stack(jnp.broadcast_arrays(rx[None, :], ry[:, None]), -1)
            wl = jnp.arange(K_, dtype=jnp.float32) * DIL - DIL * (K_ - 1) // 2
            gx = jnp.repeat(wl, K_) / Win
            gy = jnp.tile(wl, K_) / Hin
            gp = jnp.stack([gx, gy], -1)
            loc = ref[:, :, None, None, :] + gp[None, None, None, :, :] * OFFSET_SCALE
            off = offset.reshape(n, Ho, Wo, G, P, 2)
            norm = jnp.array([Win, Hin], jnp.float32)
            samp = loc[None] + off * OFFSET_SCALE / norm
            sg = 2.0 * samp - 1.0
            ix = ((sg[..., 0] + 1.0) * Win - 1.0) / 2.0
            iy = ((sg[..., 1] + 1.0) * Hin - 1.0) / 2.0
            ix = ix.reshape(n, Lo, G, P).transpose(0, 2, 1, 3).reshape(n, G, Lo * P)
            iy = iy.reshape(n, Lo, G, P).transpose(0, 2, 1, 3).reshape(n, G, Lo * P)
            x0f = jnp.floor(ix)
            y0f = jnp.floor(iy)
            wx1 = ix - x0f
            wx0 = 1.0 - wx1
            wy1 = iy - y0f
            wy0 = 1.0 - wy1
            x0 = x0f.astype(jnp.int32)
            y0 = y0f.astype(jnp.int32)
            x1 = x0 + 1
            y1 = y0 + 1
            vin = vp.reshape(n, Hin * Win, G, gc).transpose(0, 2, 1, 3)

            def corner(yc, xc, wgt):
                valid = (xc >= 0) & (xc < Win) & (yc >= 0) & (yc < Hin)
                idx = jnp.clip(yc, 0, Hin - 1) * Win + jnp.clip(xc, 0, Win - 1)
                vals = jnp.take_along_axis(vin, idx[..., None], axis=2)
                return vals * (wgt * valid.astype(wgt.dtype))[..., None]
            acc = corner(y0, x0, wy0 * wx0)
            acc = acc + corner(y0, x1, wy0 * wx1)
            acc = acc + corner(y1, x0, wy1 * wx0)
            acc = acc + corner(y1, x1, wy1 * wx1)
            acc = acc.reshape(n, G, Lo, P, gc)
            m = mask.reshape(n, Lo, G, P).transpose(0, 2, 1, 3)
            out = jnp.einsum('nglpc,nglp->nglc', acc, m)
            return out.transpose(0, 2, 1, 3).reshape(n, Ho, Wo, c)
        key = jax.random.key(seed)
        ks = jax.random.split(key, 9)
        x = jax.random.normal(ks[0], (N, C, H, W), jnp.float32)
        dw_w = jax.random.normal(ks[1], (C, 1, 3, 3), jnp.float32) * 0.1
        dw_b = jax.random.normal(ks[2], (C,), jnp.float32) * 0.01
        om_w = jax.random.normal(ks[3], (OM_DIM, C), jnp.float32) * 0.02
        om_b = jax.random.normal(ks[4], (OM_DIM,), jnp.float32) * 0.01
        sc = 1.0 / np.sqrt(C)
        vp_w = jax.random.normal(ks[5], (C, C), jnp.float32) * sc
        vp_b = jnp.zeros((C,), jnp.float32)
        op_w = jax.random.normal(ks[6], (C, C), jnp.float32) * sc
        op_b = jnp.zeros((C,), jnp.float32)
        return {'x': x, 'dw_w': dw_w, 'dw_b': dw_b, 'om_w': om_w, 'om_b': om_b, 'vp_w': vp_w, 'vp_b': vp_b, 'op_w': op_w, 'op_b': op_b}
    _L0_conv_all = _L0_conv_setup()
    _L0_conv_in = {k: v for k, v in _L0_conv_all.items() if k in ('dw_w', 'dw_b', 'om_w', 'om_b', 'vp_w', 'vp_b', 'op_w', 'op_b', )}
    del _L0_conv_all

    def _L0_ffn_setup():
        import math
        import jax, jax.numpy as jnp
        import numpy as np
        CAPACITY_FACTOR = 1.25
        key = jax.random.key(seed)
        ks = jax.random.split(key, 5)
        B, L, D, F, E = (8, 8192, 256, 1024, 8)
        h = jax.random.normal(ks[0], (B, L, D), dtype=jnp.float32)
        gate_w = jax.random.normal(ks[1], (D, E), dtype=jnp.float32) * 0.02
        gate_b = jnp.zeros((E,), dtype=jnp.float32)
        w1 = jax.random.normal(ks[2], (E, D, F), dtype=jnp.float32) * (1.0 / math.sqrt(D))
        b1 = jnp.zeros((E, F), dtype=jnp.float32)
        w2 = jax.random.normal(ks[3], (E, F, D), dtype=jnp.float32) * (1.0 / math.sqrt(F))
        b2 = jnp.zeros((E, D), dtype=jnp.float32)
        return {'h': h, 'gate_w': gate_w, 'gate_b': gate_b, 'w1': w1, 'b1': b1, 'w2': w2, 'b2': b2}
    _L0_ffn_all = _L0_ffn_setup()
    _L0_ffn_in = {k: v for k, v in _L0_ffn_all.items() if k in ('gate_w', 'gate_b', 'w1', 'b1', 'w2', 'b2', )}
    del _L0_ffn_all

    return {
        "x": x,
        "L0_conv_dw_w": _L0_conv_in["dw_w"],
        "L0_conv_dw_b": _L0_conv_in["dw_b"],
        "L0_conv_om_w": _L0_conv_in["om_w"],
        "L0_conv_om_b": _L0_conv_in["om_b"],
        "L0_conv_vp_w": _L0_conv_in["vp_w"],
        "L0_conv_vp_b": _L0_conv_in["vp_b"],
        "L0_conv_op_w": _L0_conv_in["op_w"],
        "L0_conv_op_b": _L0_conv_in["op_b"],
        "L0_ffn_gate_w": _L0_ffn_in["gate_w"],
        "L0_ffn_gate_b": _L0_ffn_in["gate_b"],
        "L0_ffn_w1": _L0_ffn_in["w1"],
        "L0_ffn_b1": _L0_ffn_in["b1"],
        "L0_ffn_w2": _L0_ffn_in["w2"],
        "L0_ffn_b2": _L0_ffn_in["b2"],
    }

def reference(x, L0_conv_dw_w, L0_conv_dw_b, L0_conv_om_w, L0_conv_om_b, L0_conv_vp_w, L0_conv_vp_b, L0_conv_op_w, L0_conv_op_b, L0_ffn_gate_w, L0_ffn_gate_b, L0_ffn_w1, L0_ffn_b1, L0_ffn_w2, L0_ffn_b2):
    import jax
    import jax.numpy as jnp
    def _L0_conv_ref(x, dw_w, dw_b, om_w, om_b, vp_w, vp_b, op_w, op_b):
        import jax, jax.numpy as jnp
        import numpy as np
        N, C, H, W = (8, 256, 64, 64)
        G, K_, DIL, STRIDE, PAD, OFFSET_SCALE = (8, 3, 1, 1, 1, 1.0)
        P = K_ * K_
        OM_DIM = int(np.ceil(G * P * 3 / 8) * 8)

        def _dcn_core(v, offset, mask):
            n, h, w, c = v.shape
            gc = c // G
            vp = jnp.pad(v, ((0, 0), (PAD, PAD), (PAD, PAD), (0, 0)))
            Hin, Win = (h + 2 * PAD, w + 2 * PAD)
            Ho = (Hin - (DIL * (K_ - 1) + 1)) // STRIDE + 1
            Wo = (Win - (DIL * (K_ - 1) + 1)) // STRIDE + 1
            Lo = Ho * Wo
            ry = (DIL * (K_ - 1) // 2 + 0.5 + jnp.arange(Ho, dtype=jnp.float32) * STRIDE) / Hin
            rx = (DIL * (K_ - 1) // 2 + 0.5 + jnp.arange(Wo, dtype=jnp.float32) * STRIDE) / Win
            ref = jnp.stack(jnp.broadcast_arrays(rx[None, :], ry[:, None]), -1)
            wl = jnp.arange(K_, dtype=jnp.float32) * DIL - DIL * (K_ - 1) // 2
            gx = jnp.repeat(wl, K_) / Win
            gy = jnp.tile(wl, K_) / Hin
            gp = jnp.stack([gx, gy], -1)
            loc = ref[:, :, None, None, :] + gp[None, None, None, :, :] * OFFSET_SCALE
            off = offset.reshape(n, Ho, Wo, G, P, 2)
            norm = jnp.array([Win, Hin], jnp.float32)
            samp = loc[None] + off * OFFSET_SCALE / norm
            sg = 2.0 * samp - 1.0
            ix = ((sg[..., 0] + 1.0) * Win - 1.0) / 2.0
            iy = ((sg[..., 1] + 1.0) * Hin - 1.0) / 2.0
            ix = ix.reshape(n, Lo, G, P).transpose(0, 2, 1, 3).reshape(n, G, Lo * P)
            iy = iy.reshape(n, Lo, G, P).transpose(0, 2, 1, 3).reshape(n, G, Lo * P)
            x0f = jnp.floor(ix)
            y0f = jnp.floor(iy)
            wx1 = ix - x0f
            wx0 = 1.0 - wx1
            wy1 = iy - y0f
            wy0 = 1.0 - wy1
            x0 = x0f.astype(jnp.int32)
            y0 = y0f.astype(jnp.int32)
            x1 = x0 + 1
            y1 = y0 + 1
            vin = vp.reshape(n, Hin * Win, G, gc).transpose(0, 2, 1, 3)

            def corner(yc, xc, wgt):
                valid = (xc >= 0) & (xc < Win) & (yc >= 0) & (yc < Hin)
                idx = jnp.clip(yc, 0, Hin - 1) * Win + jnp.clip(xc, 0, Win - 1)
                vals = jnp.take_along_axis(vin, idx[..., None], axis=2)
                return vals * (wgt * valid.astype(wgt.dtype))[..., None]
            acc = corner(y0, x0, wy0 * wx0)
            acc = acc + corner(y0, x1, wy0 * wx1)
            acc = acc + corner(y1, x0, wy1 * wx0)
            acc = acc + corner(y1, x1, wy1 * wx1)
            acc = acc.reshape(n, G, Lo, P, gc)
            m = mask.reshape(n, Lo, G, P).transpose(0, 2, 1, 3)
            out = jnp.einsum('nglpc,nglp->nglc', acc, m)
            return out.transpose(0, 2, 1, 3).reshape(n, Ho, Wo, c)
        n, c, h, w = x.shape
        L = h * w
        xh = jnp.transpose(x, (0, 2, 3, 1)).reshape(n, L, c)
        v = (xh @ vp_w.T + vp_b).reshape(n, h, w, c)
        om_in = jnp.transpose(x.reshape(n, h, w, c), (0, 3, 1, 2))
        dw = jax.lax.conv_general_dilated(om_in, dw_w, (1, 1), ((1, 1), (1, 1)), feature_group_count=c, dimension_numbers=('NCHW', 'OIHW', 'NCHW'))
        dw = dw + dw_b[None, :, None, None]
        omf = jnp.transpose(dw, (0, 2, 3, 1)).reshape(n, L, c)
        om = (omf @ om_w.T + om_b).reshape(n, h, w, -1)[..., :G * P * 3]
        om = om.reshape(n, h, w, G, P * 3)
        offset = om[..., :2 * P].reshape(n, h, w, G * 2 * P)
        mask = om[..., 2 * P:3 * P].reshape(n, h, w, G * P)
        out = _dcn_core(v, offset, mask)
        out = out.reshape(n, L, c) @ op_w.T + op_b
        return jnp.transpose(out.reshape(n, h, w, c), (0, 3, 1, 2))

    def _L0_ffn_ref(h, gate_w, gate_b, w1, b1, w2, b2):
        import math
        import jax, jax.numpy as jnp
        import numpy as np
        CAPACITY_FACTOR = 1.25
        B, L, D = h.shape
        E = gate_w.shape[1]
        T = B * L
        C = max(1, math.ceil(CAPACITY_FACTOR * T / E))
        x = h.reshape(T, D)
        logits = x @ gate_w + gate_b
        probs = jax.nn.softmax(logits, axis=-1)
        idx = jnp.argmax(probs, axis=-1)
        prb = jnp.take_along_axis(probs, idx[:, None], axis=1)[:, 0]
        one_hot = jax.nn.one_hot(idx, E, dtype=jnp.float32)
        pos = (jnp.cumsum(one_hot, axis=0) * one_hot).sum(-1).astype(jnp.int32) - 1
        kept = pos < C
        pos_safe = jnp.where(kept, pos, C)
        buf = jnp.zeros((E, C, D), dtype=h.dtype).at[idx, pos_safe].set(x, mode='drop')
        hmid = jax.nn.relu(jnp.einsum('ecd,edf->ecf', buf, w1) + b1[:, None, :])
        ybuf = jnp.einsum('ecf,efd->ecd', hmid, w2) + b2[:, None, :]
        pos_g = jnp.minimum(pos, C - 1)
        y_tok = ybuf[idx, pos_g] * (prb * kept)[:, None]
        y = y_tok.reshape(B, L, D)
        y = jnp.nan_to_num(y, nan=0.0, posinf=10000.0, neginf=-10000.0)
        return y

    def _gn(v, G=32, eps=1e-5):
        B_, C_, H_, W_ = v.shape
        g = v.reshape(B_, G, C_ // G, H_, W_)
        m = jnp.mean(g, axis=(2, 3, 4), keepdims=True)
        s = jnp.var(g, axis=(2, 3, 4), keepdims=True)
        return ((g - m) / jnp.sqrt(s + eps)).reshape(v.shape)

    def _ln_c(v, eps=1e-6):
        m = jnp.mean(v, axis=1, keepdims=True)
        s = jnp.var(v, axis=1, keepdims=True)
        return (v - m) / jnp.sqrt(s + eps)

    def _ln_t(v, eps=1e-5):
        m = jnp.mean(v, axis=-1, keepdims=True)
        s = jnp.var(v, axis=-1, keepdims=True)
        return (v - m) / jnp.sqrt(s + eps)

    def _to_tokens(v):
        B_, C_, H_, W_ = v.shape
        return v.reshape(B_, C_, H_ * W_).transpose(0, 2, 1)
    def _from_tokens(t, like):
        B_, C_, H_, W_ = like.shape
        return t.transpose(0, 2, 1).reshape(B_, C_, H_, W_)

    x = x + _L0_conv_ref(_ln_c(x), L0_conv_dw_w, L0_conv_dw_b, L0_conv_om_w, L0_conv_om_b, L0_conv_vp_w, L0_conv_vp_b, L0_conv_op_w, L0_conv_op_b)
    t = _to_tokens(x)
    t = t + _L0_ffn_ref(_ln_t(t), L0_ffn_gate_w, L0_ffn_gate_b, L0_ffn_w1, L0_ffn_b1, L0_ffn_w2, L0_ffn_b2)
    x = _from_tokens(t, x)
    return x


_drawn_inputs = setup_inputs


def setup_inputs(seed=0):
    import zlib

    import numpy as np

    out = dict(_drawn_inputs(seed))
    spreads = {'L0_conv_vp_b': (0.0, 0.1),
     'L0_conv_op_b': (0.0, 0.1),
     'L0_ffn_gate_b': (0.0, 0.1),
     'L0_ffn_b1': (0.0, 0.629),
     'L0_ffn_b2': (0.0, 0.445)}
    factors = {'L0_conv_dw_b': 3.943}
    for name, (base, spread) in spreads.items():
        noise = np.random.default_rng([zlib.crc32(name.encode()), seed]).standard_normal(out[name].shape)
        drawn = base * np.exp(spread * noise) if base else spread * noise
        out[name] = jnp.asarray(drawn.astype(out[name].dtype))
    for name, factor in factors.items():
        out[name] = (out[name] * factor).astype(out[name].dtype)
    return out
```

```python
from contextlib import ExitStack

import concourse.bass as bass
from concourse import mybir

ALU = mybir.AluOpType
ACT = mybir.ActivationFunctionType
AX = mybir.AxisListType
F32 = mybir.dt.float32
I32 = mybir.dt.int32
U32 = mybir.dt.uint32

P = 128
TM = 512
G, PT = 8, 9
HALO = 2
BH, BW = 6, 8
RH, RW = BH + 2 * HALO, BW + 2 * HALO
Q = RH * RW
NPOS = BH * BW
TAPS = 25
TAPP = 32


def conv_features(nc, x, dw_w, dw_b, om_w, om_b, vp_w, vp_b, ident_d, mean_d,
                  xn, v_pad, om_raw, taps_t, routed_x, room):
    B, C, HW = x.shape
    W = 64
    H = HW // W
    KC = C // P
    RC = 512 // W
    N = RC * W
    NCH = HW // N
    NT = N // P
    OM = om_w.shape[1]
    TG = NT * G
    WP = W + 2 * HALO
    VR = v_pad.shape[1]
    ZB = 2048
    with ExitStack() as ctx:
        def sb(name, shape):
            return ctx.enter_context(nc.sbuf_tensor(name, shape, F32))

        def ps(name, shape):
            return ctx.enter_context(nc.psum_tensor(name, shape, F32))

        def sem(name):
            return ctx.enter_context(nc.semaphore(name))

        ident = sb("p1_ident", [P, P])
        mean_w = sb("mean_w", [P, P])
        dw_sb = sb("dw_sb", [P, KC, 9])
        dwb_sb = sb("dwb_sb", [P, KC])
        om_sb = sb("om_sb", [P, KC, OM])
        vp_sb = sb("vp_sb", [P, KC, C])
        omb_bc = sb("omb_bc", [P, OM])
        vpb_bc = sb("vpb_bc", [P, C])
        X = sb("X", [P, 2, KC, N])
        SQ = sb("SQ", [P, KC, N])
        eps = sb("eps", [P, 1])
        ones = sb("ones", [P, P])
        STD = sb("STD", [P, NT])
        RSTD = sb("RSTD", [P, NT])
        RDIAG = sb("RDIAG", [P, NT, P])
        XL = sb("XL", [P, KC, H + 2, W + 2])
        TK = sb("TK", [P, 2, NT, C])
        F = sb("F", [P, KC, N])
        OMS = sb("OMS", [P, NT, OM])
        VS = sb("VS", [P, 2, NT, C])
        TENT = sb("TENT", [P, 3, TG, 2 * PT])
        MTX = sb("MTX", [P, TG, 3, PT])
        RM = sb("RM", [P, 3, TG, 3, PT])
        K = sb("K", [P, TG, TAPP])
        KS = sb("KS", [P, 2, N])
        zero = sb("zero", [P, ZB])
        psM = ps("psM", [P, N])
        psR = ps("psR", [P, N])
        psVal = ps("psVal", [P, NT, C])
        psX = psVal[:].rearrange("p t c -> p (t c)").rearrange("p (h w) -> p h w", h=KC)
        psO = ps("psO", [P, 2, 512])
        psV = psO[:, 0, 2 * OM:2 * OM + NT]
        psK = ps("psK", [P, 2, N])

        const_in = sem("const_in")
        zeroed = sem("zeroed")
        passed = sem("p1_passed")
        x_in = [sem(f"x_in{i}") for i in range(2)]
        mean_done, sub_done, sq_done, var_done = sem("mean_done"), sem("sub_done"), sem("sq_done"), sem("var_done")
        diag_done, spread_mm = sem("diag_done"), sem("spread_mm")
        xn_st = [sem(f"xn_st{i}") for i in range(2)]
        tk_in = [sem(f"tk_in{i}") for i in range(2)]
        tk_turned = sem("tk_turned")
        xl_done, std_done = sem("xl_done"), sem("std_done")
        rstd_done, norm_done, dw_step, om_mm = sem("rstd_done"), sem("norm_done"), sem("dw_step"), sem("om_mm")
        v_mm, v_raw, v_ready = sem("v_mm"), sem("v_raw"), sem("v_ready")
        v_st = [sem(f"v_st{i}") for i in range(2)]
        om_evac, om_ready, om_st, tent_done = sem("om_evac"), sem("om_ready"), sem("om_st"), sem("tent_done")
        tent_step = sem("tent_step")
        mtx_done, rm_done, k_clr, k_add, tr_mm = sem("mtx_done"), sem("rm_done"), sem("k_clr"), sem("k_add"), sem("tr_mm")
        ks_ready, ks_st, red_done, fill_st = sem("ks_ready"), sem("ks_st"), sem("red_done"), sem("fill_st")
        block = ctx.enter_context(nc.Block())

        def chunks(step, lag):
            return [step - lag] if 0 <= step - lag < NCH else []

        def images(eng, pair):
            pair(0, None)
            if B > 1:
                with eng.Fori(1, B) as n:
                    pair(n, n - 1)
            pair(None, B - 1)

        @block.sync
        def _(sp):
            loads = [(ident[:], ident_d), (mean_w[:], mean_d),
                     (dw_sb[:], dw_w.rearrange("(h p) t -> p h t", p=P)), (dwb_sb[:], dw_b),
                     (om_sb[:], om_w.rearrange("(h p) o -> p h o", p=P)),
                     (vp_sb[:], vp_w.rearrange("(h p) o -> p h o", p=P)),
                     (omb_bc[:], om_b.partition_broadcast(P)), (vpb_bc[:], vp_b.partition_broadcast(P))]
            for dst, src in loads:
                sp.dma_start(dst, src).then_inc(const_in, 16)
            xn_rows = xn.rearrange("n c w -> n (c w)").rearrange("n (l c) -> n l c", c=C)

            def columns(ap, n, c):
                return ap[n, :, N * c:N * (c + 1)].rearrange("(h p) w -> p h w", p=P)

            def load_x(n, c):
                sp.dma_start(X[:, c % 2], columns(x, n, c)).then_inc(x_in[c % 2], 16)

            def load_tk(j, c):
                sp.wait_ge(tk_turned, j * NCH + max(c - 1, 0))
                sp.dma_start(TK[:, c % 2], xn_rows[j, N * c:N * (c + 1)].rearrange("(t p) c -> p t c", p=P)) \
                    .then_inc(tk_in[c % 2], 16)

            def pair(n, j):
                if n is not None:
                    for c in range(2):
                        sp.wait_ge(v_mm, n * NCH)
                        sp.sem_inc(passed, 1)
                        sp.wait_ge(xn_st[c], n * (8 * NCH))
                        load_x(n, c)
                if j is not None:
                    for i in range(2):
                        sp.wait_ge(xn_st[i], j * (8 * NCH) + 8 * NCH)
                        sp.sem_inc(passed, 1)
                    load_tk(j, 0)
                for s in range(NCH + 2):
                    if n is not None:
                        for c in chunks(s, 0):
                            sp.wait_ge(norm_done, n * NCH + c + 1)
                            sp.dma_start(columns(xn, n, c), X[:, c % 2]).then_inc(xn_st[c % 2], 16)
                        for c in chunks(s, -2):
                            sp.wait_ge(v_mm, n * NCH + c - 1)
                            sp.sem_inc(passed, 1)
                            sp.wait_ge(xn_st[c % 2], n * (8 * NCH) + 16 * (c // 2))
                            load_x(n, c)
                        for c in chunks(s, 0):
                            sp.wait_ge(v_ready, n * NCH + c + 1)
                            for r in range(2):
                                y = HALO + RC * c + r
                                sp.dma_start(
                                    v_pad[n, y:y + 2 * NT - 1:2, HALO:HALO + W, :].rearrange("t w c -> w t c"),
                                    VS[W * r:W * (r + 1), c % 2]).then_inc(v_st[c % 2], 16)
                    if j is not None:
                        for c in chunks(s, -1):
                            load_tk(j, c)
                        for c in chunks(s, 1):
                            sp.wait_ge(om_ready, j * NCH + c + 1)
                            sp.dma_start(om_raw[j, NT * c:NT * (c + 1)].rearrange("t p o -> p t o"), OMS[:]) \
                                .then_inc(om_st, 16)
                        for c in chunks(s, 2):
                            sp.wait_ge(ks_ready, j * NCH + c + 1)
                            sp.dma_start(taps_t[j, :, :, N * c:N * (c + 1)].rearrange("h p w -> p h w"), KS[:]) \
                                .then_inc(ks_st, 16)

            images(sp, pair)
            for s in range(2):
                sp.wait_ge(v_st[s], 16 * B * NCH)
            sp.wait_ge(om_st, 16 * B * NCH)
            sp.wait_ge(ks_st, 16 * B * NCH)

        @block.scalar
        def _(act):
            act.wait_ge(zeroed, 6)
            fills = routed_x.shape[0] * C // (B * P * ZB)
            assert fills * B * P * ZB == routed_x.shape[0] * C
            xz = routed_x.rearrange("(b f q) c -> b f (q c)", b=B, f=fills).rearrange(
                "b f (p z) -> b f p z", p=P)
            vflat = v_pad.rearrange("n y w c -> n (y w c)")
            side = WP * C
            top = HALO * side + HALO * C
            below = (VR - HALO - H) * side + HALO * C

            def fill(dst, src):
                act.dma_start(dst, src).then_inc(fill_st, 16)

            def pair(n, j):
                def square(c):
                    act.wait_ge(sub_done, n * NCH + c + 1)
                    act.wait_ge(var_done, n * NCH + c)
                    nc.scalar.activation(SQ[:], X[:, c % 2], ACT.Square).then_inc(sq_done, 1)

                def std(c):
                    act.wait_ge(var_done, n * NCH + c + 1)
                    act.wait_ge(rstd_done, n * NCH + c)
                    nc.scalar.activation(STD[:], psV, ACT.Sqrt, bias=eps[:]).then_inc(std_done, 1)

                if n is not None:
                    for at, size in ((0, top), (VR * side - below, below)):
                        fill(vflat[n, at:at + size].rearrange("(p z) -> p z", p=P), zero[:, :size // P])
                    sides = vflat[n, 3 * side - HALO * C:3 * side - HALO * C + (H - 1) * side].rearrange(
                        "(y z) -> y z", z=side)[:, :2 * HALO * C]
                    fill(sides, zero[:H - 1, :2 * HALO * C])
                    for f in range(fills):
                        fill(xz[n, f], zero[:])
                    square(0)
                    std(0)
                for s in range(NCH + 2):
                    if j is not None:
                        for c in chunks(s, 2):
                            act.wait_ge(tr_mm, j * NCH + c)
                            nc.scalar.activation(K[:].rearrange("p t u -> p (t u)"), zero[:, :TG * TAPP], ACT.Copy) \
                                .then_inc(k_clr, 1)
                    if n is not None:
                        for c in chunks(s, -1):
                            square(c)
                        for c in chunks(s, 0):
                            act.wait_ge(v_mm, n * NCH + c + 1)
                            act.wait_ge(v_st[c % 2], n * (16 * NCH) + 32 * (c // 2))
                            nc.scalar.activation(VS[:, c % 2], psVal[:], ACT.Copy).then_inc(v_raw, 1)
                        for c in chunks(s, -1):
                            std(c)
                    if j is not None:
                        for c in chunks(s, 0):
                            act.wait_ge(tk_turned, j * NCH + c + 1)
                            act.wait_ge(dw_step, j * (18 * NCH))
                            for h in range(KC):
                                last = nc.scalar.activation(XL[:, h, 1 + RC * c:1 + RC * (c + 1), 1:1 + W],
                                                            psX[:, h].rearrange("p (y w) -> p y w", w=W), ACT.Copy)
                            last.then_inc(xl_done, 1)
                        for c in chunks(s, 1):
                            act.wait_ge(om_mm, j * NCH + c + 1)
                            act.wait_ge(om_st, j * (16 * NCH) + 16 * c)
                            act.wait_ge(mtx_done, j * NCH + c)
                            nc.scalar.activation(OMS[:].rearrange("p (b t) o -> p b (t o)", b=2), psO[:, :, :2 * OM],
                                                 ACT.Copy).then_inc(om_evac, 1)
                            act.wait_ge(om_ready, j * NCH + c + 1)
                            act.wait_ge(rm_done, j * (3 * NCH) + 3 * c)
                            off = OMS[:].rearrange("p t (g o) -> p (t g) o", g=G)[:, :, :2 * PT]
                            nc.scalar.activation(TENT[:, 1], off, ACT.Abs).then_inc(tent_step, 1)
                            nc.scalar.activation(TENT[:, 0], off, ACT.Relu, scale=-1.0)
                            nc.scalar.activation(TENT[:, 2], off, ACT.Relu)
                            act.wait_ge(tent_step, j * NCH + c + 1)
                            nc.scalar.activation(TENT[:, 1], TENT[:, 1], ACT.Identity, scale=-1.0, bias=1.0) \
                                .then_inc(tent_done, 1)
                        for c in chunks(s, 2):
                            act.wait_ge(tr_mm, j * NCH + c + 1)
                            act.wait_ge(ks_st, j * (16 * NCH) + 16 * c)
                            nc.scalar.activation(KS[:], psK[:], ACT.Copy).then_inc(ks_ready, 1)

            images(act, pair)
            act.wait_ge(fill_st, 16 * B * (3 + fills))

        @block.gpsimd
        def _(pool):
            nc.gpsimd.memset(zero[:], 0.0).then_inc(zeroed, 1)
            nc.gpsimd.memset(XL[:], 0.0).then_inc(zeroed, 1)
            nc.gpsimd.memset(room[:], 1.0).then_inc(zeroed, 1)
            nc.gpsimd.memset(eps[:], 1e-6).then_inc(zeroed, 1)
            nc.gpsimd.memset(ones[:], 1.0).then_inc(zeroed, 1)
            nc.gpsimd.memset(K[:], 0.0).then_inc(zeroed, 1)
            pool.wait_ge(const_in, 16 * 8)
            pool.wait_ge(zeroed, 6)

            def pair(n, j):
                def diagonal(c):
                    pool.wait_ge(rstd_done, n * NCH + c + 1)
                    pool.wait_ge(spread_mm, n * NCH + c)
                    nc.gpsimd.tensor_tensor(RDIAG[:], ident[:].unsqueeze(1).broadcast_to([P, NT, P]),
                                            RSTD[:].unsqueeze(2).broadcast_to([P, NT, P]), ALU.mult) \
                        .then_inc(diag_done, 1)

                if n is not None:
                    diagonal(0)
                for s in range(NCH + 2):
                    if n is not None:
                        for c in chunks(s, 0):
                            pool.wait_ge(v_raw, n * NCH + c + 1)
                            v = VS[:, c % 2]
                            nc.gpsimd.tensor_tensor(v, v, vpb_bc[:].unsqueeze(1).broadcast_to([P, NT, C]), ALU.add) \
                                .then_inc(v_ready, 1)
                        for c in chunks(s, -1):
                            diagonal(c)
                    if j is not None:
                        for c in chunks(s, 2):
                            pool.wait_ge(mtx_done, j * NCH + c + 1)
                            pool.wait_ge(k_add, j * (9 * NCH) + 9 * c)
                            for i in range(3):
                                mtx = MTX[:, :, i, :].unsqueeze(2).broadcast_to([P, TG, 3, PT])
                                ty = TENT[:, :, :, 1::2].rearrange("p j t q -> p t j q")
                                nc.gpsimd.tensor_tensor(RM[:, i], mtx, ty, ALU.mult).then_inc(rm_done, 1)
                        for c in chunks(s, 1):
                            pool.wait_ge(om_evac, j * NCH + c + 1)
                            nc.gpsimd.tensor_tensor(OMS[:], OMS[:], omb_bc[:].unsqueeze(1).broadcast_to([P, NT, OM]),
                                                    ALU.add).then_inc(om_ready, 1)

            images(pool, pair)

        @block.tensor
        def _(pe):
            pe.wait_ge(const_in, 16 * 8)
            pe.wait_ge(zeroed, 6)

            def pair(n, j):
                def mean(c):
                    pe.wait_ge(x_in[c % 2], n * (8 * NCH) + 16 * (c // 2) + 16)
                    pe.wait_ge(sub_done, n * NCH + c)
                    for h in range(KC):
                        last = nc.tensor.matmul(psM[:], mean_w[:], X[:, c % 2, h], start=(h == 0), stop=(h == KC - 1))
                    last.then_inc(mean_done, 1)

                def var(c):
                    pe.wait_ge(sq_done, n * NCH + c + 1)
                    pe.wait_ge(std_done, n * NCH + c)
                    if j is not None:
                        pe.wait_ge(om_evac, j * NCH + max(c - 2, 0))
                    for t in range(NT):
                        for h in range(KC):
                            last = nc.tensor.matmul(psV[:, t:t + 1], SQ[:, h, P * t:P * (t + 1)], mean_w[:, 0:1],
                                                    start=(h == 0), stop=(h == KC - 1))
                    last.then_inc(var_done, 1)

                def spread(c):
                    pe.wait_ge(diag_done, n * NCH + c + 1)
                    pe.wait_ge(norm_done, n * NCH + c)
                    nc.tensor.matmul(psR[:], ones[:], RDIAG[:].rearrange("p t q -> p (t q)"), start=True, stop=True) \
                        .then_inc(spread_mm, 1)

                if n is not None:
                    mean(0)
                    mean(1)
                    var(0)
                    spread(0)
                for s in range(NCH + 2):
                    if n is not None:
                        for c in chunks(s, 0):
                            pe.wait_ge(norm_done, n * NCH + c + 1)
                            pe.wait_ge(v_raw, n * NCH + c)
                            if j is not None:
                                pe.wait_ge(xl_done, j * NCH + c)
                            for t in range(NT):
                                for h in range(KC):
                                    last = nc.tensor.matmul(psVal[:, t], X[:, c % 2, h, P * t:P * (t + 1)], vp_sb[:, h],
                                                            start=(h == 0), stop=(h == KC - 1))
                            last.then_inc(v_mm, 1)
                        for c in chunks(s, -2):
                            mean(c)
                        for c in chunks(s, -1):
                            var(c)
                    if j is not None:
                        for c in chunks(s, 0):
                            pe.wait_ge(tk_in[c % 2], j * (8 * NCH) + 16 * (c // 2) + 16)
                            pe.wait_ge(xl_done, j * NCH + c)
                            pe.wait_ge(v_raw, n * NCH + c + 1 if n is not None else B * NCH)
                            for h in range(KC):
                                for t in range(NT):
                                    last = nc.tensor.transpose(psX[:, h, P * t:P * (t + 1)],
                                                               TK[:, c % 2, t, P * h:P * (h + 1)], ident[:])
                            last.then_inc(tk_turned, 1)
                        for c in chunks(s, 1):
                            pe.wait_ge(dw_step, j * (18 * NCH) + 18 * (c + 1))
                            pe.wait_ge(om_evac, j * NCH + c)
                            pe.wait_ge(std_done, n * NCH + min(c + 3, NCH) if n is not None else B * NCH)
                            for t in range(NT):
                                for h in range(KC):
                                    last = nc.tensor.matmul(psO[:, t // 2, OM * (t % 2):OM * (t % 2 + 1)],
                                                            F[:, h, P * t:P * (t + 1)], om_sb[:, h],
                                                            start=(h == 0), stop=(h == KC - 1))
                            last.then_inc(om_mm, 1)
                    if n is not None:
                        for c in chunks(s, -1):
                            spread(c)
                    if j is not None:
                        for c in chunks(s, 2):
                            pe.wait_ge(k_add, j * (9 * NCH) + 9 * (c + 1))
                            pe.wait_ge(ks_ready, j * NCH + c)
                            for t in range(NT):
                                for h in range(2):
                                    last = nc.tensor.transpose(
                                        psK[:, h, P * t:P * (t + 1)],
                                        K[:, G * t + 4 * h:G * t + 4 * h + 4].rearrange("p g u -> p (g u)"), ident[:])
                            last.then_inc(tr_mm, 1)

            images(pe, pair)

        @block.vector
        def _(dve):
            dve.wait_ge(const_in, 16 * 8)
            dve.wait_ge(zeroed, 6)

            def pair(n, j):
                def sub(c):
                    dve.wait_ge(x_in[c % 2], n * (8 * NCH) + 16 * (c // 2) + 16)
                    dve.wait_ge(mean_done, n * NCH + c + 1)
                    xs = X[:, c % 2]
                    nc.vector.tensor_tensor(xs, xs, psM[:].unsqueeze(1).broadcast_to([P, KC, N]), ALU.subtract) \
                        .then_inc(sub_done, 1)

                def rstd(c):
                    dve.wait_ge(std_done, n * NCH + c + 1)
                    dve.wait_ge(diag_done, n * NCH + c)
                    nc.vector.reciprocal(RSTD[:], STD[:]).then_inc(rstd_done, 1)

                if n is not None:
                    sub(0)
                    rstd(0)
                for s in range(NCH + 2):
                    if n is not None:
                        for c in chunks(s, -1):
                            sub(c)
                        for c in chunks(s, 0):
                            dve.wait_ge(spread_mm, n * NCH + c + 1)
                            xs = X[:, c % 2]
                            nc.vector.tensor_tensor(xs, xs, psR[:].unsqueeze(1).broadcast_to([P, KC, N]), ALU.mult) \
                                .then_inc(norm_done, 1)
                    if j is not None:
                        for c in chunks(s, 2):
                            dve.wait_ge(tent_done, j * NCH + c + 1)
                            dve.wait_ge(rm_done, j * (3 * NCH) + 3 * c)
                            mask = OMS[:].rearrange("p t (g o) -> p (t g) o", g=G)[:, :, 2 * PT:3 * PT] \
                                .unsqueeze(2).broadcast_to([P, TG, 3, PT])
                            tx = TENT[:, :, :, 0::2].rearrange("p i t q -> p t i q")
                            nc.vector.tensor_tensor(MTX[:], mask, tx, ALU.mult)
                            nc.vector.tensor_reduce(room[:, 1:2], TENT[:, 1], AX.XY, ALU.min).then_inc(mtx_done, 1)
                            dve.wait_ge(mtx_done, j * NCH + c + 1)
                            nc.vector.tensor_tensor(room[:, 0:1], room[:, 0:1], room[:, 1:2], ALU.min) \
                                .then_inc(red_done, 1)
                        for c in chunks(s, 1):
                            dve.wait_ge(xl_done, j * NCH + min(c + 2, NCH))
                            dve.wait_ge(om_mm, j * NCH + c)
                            for t in range(9):
                                for h in range(KC):
                                    src = XL[:, h, RC * c + t // 3:RC * c + t // 3 + RC, t % 3:t % 3 + W]
                                    acc = F[:, h].rearrange("p (y w) -> p y w", w=W)
                                    if t == 0:
                                        ins = nc.vector.tensor_scalar(acc, src, dw_sb[:, h, t:t + 1],
                                                                      dwb_sb[:, h:h + 1], ALU.mult, ALU.add)
                                    else:
                                        dve.wait_ge(dw_step, j * (18 * NCH) + 18 * c + 2 * t + h - 1)
                                        ins = nc.vector.scalar_tensor_tensor(acc, src, dw_sb[:, h, t:t + 1], acc,
                                                                             ALU.mult, ALU.add)
                                    ins.then_inc(dw_step, 1)
                    if n is not None:
                        for c in chunks(s, -1):
                            rstd(c)
                    if j is not None:
                        for c in chunks(s, 2):
                            dve.wait_ge(k_clr, j * NCH + c + 1)
                            for i in range(3):
                                dve.wait_ge(rm_done, j * (3 * NCH) + 3 * c + i + 1)
                                for k in range(3):
                                    if i or k:
                                        dve.wait_ge(k_add, j * (9 * NCH) + 9 * c + 3 * i + k)
                                    at = 5 * k + i
                                    kk = K[:, :, at:at + 15].rearrange("p t (v u) -> p t u v", u=5)[:, :, 0:3]
                                    nc.vector.tensor_tensor(
                                        kk, kk, RM[:, i, :, k].rearrange("p t (a b) -> p t a b", a=3),
                                        ALU.add).then_inc(k_add, 1)

            images(dve, pair)

def deform(nc, x, op_w, op_b, select_d, v_pad, taps_t, x1):
    B, C, HW = x.shape
    W = 64
    H = HW // W
    KC = C // P
    N = 512
    NCH = HW // N
    NBX = W // BW
    NBY = -(-H // BH)
    NB = NBX * NBY
    CG = C // G
    GH = G // KC
    APOS = 4
    AB = NPOS // APOS
    LAST = H - BH * (NBY - 1)
    SELW = select_d.shape[1]
    with ExitStack() as ctx:
        def sb(name, shape):
            return ctx.enter_context(nc.sbuf_tensor(name, shape, F32))

        def ps(name, shape):
            return ctx.enter_context(nc.psum_tensor(name, shape, F32))

        def sem(name):
            return ctx.enter_context(nc.semaphore(name))

        V = sb("V", [Q, KC, NB, P])
        KT = sb("KT", [P, KC, H, W])
        A = sb("A", [Q, 2, NB, NPOS])
        D = sb("D", [P, KC, H, W])
        XR = sb("XR", [P, 2, KC, N])
        op_sb = sb("op_sb", [P, KC, C])
        opb_sb = sb("opb_sb", [P, KC])
        SEL = sb("SEL", [P, SELW])
        psA = ps("psA", [P, 4, 512])
        psD = ps("psD", [P, 2, 512])
        psP = ps("psP", [P, KC, N])

        w_in, passed = sem("w_in"), sem("p2_passed")
        v_in = [sem(f"v_in{i}") for i in range(KC)]
        kt_in = [sem(f"kt_in{i}") for i in range(KC)]
        a_mm, d_mm, p_mm = sem("a_mm"), sem("d_mm"), sem("p_mm")
        a_out = [sem("a_out_act"), sem("a_out_dve")]
        d_out = [sem("d_out_act"), sem("d_out_dve")]
        res_done = sem("res_done")
        xr_in = [sem(f"xr_in{i}") for i in range(2)]
        x1_st = [sem(f"x1_st{i}") for i in range(2)]
        block = ctx.enter_context(nc.Block())

        APG = AB * G
        DPG = NBY * G

        @block.sync
        def _(sp):
            sp.dma_start(SEL[:], select_d).then_inc(w_in, 16)
            sp.dma_start(op_sb[:], op_w.rearrange("(h p) o -> p h o", p=P)).then_inc(w_in, 16)
            sp.dma_start(opb_sb[:], op_b).then_inc(w_in, 16)

            def load_taps(n, h):
                sp.dma_start(KT[:, h].rearrange("p y w -> p (y w)"), taps_t[n, h]).then_inc(kt_in[h], 16)

            def load_values(n, h):
                for bx in range(NBX):
                    for r in range(RH):
                        src = v_pad[n, r:r + BH * (NBY - 1) + 1:BH, BW * bx:BW * bx + RW, P * h:P * (h + 1)]
                        sp.dma_start(V[RW * r:RW * (r + 1), h, bx::NBX], src.rearrange("a w c -> w a c")) \
                            .then_inc(v_in[h], 16)

            for h in range(KC):
                load_taps(0, h)
                load_values(0, h)
            if B > 1:
                with sp.Fori(1, B) as n:
                    for h in range(KC):
                        sp.wait_ge(a_mm, (n - 1) * APG + APG // 2 * (h + 1))
                        load_taps(n, h)
                        sp.wait_ge(d_mm, (n - 1) * DPG + DPG // 2 * (h + 1))
                        load_values(n, h)

        @block.gpsimd
        def _(pool):
            with pool.Fori(0, B) as n:
                def load(c):
                    pool.wait_ge(x1_st[c % 2], n * (8 * NCH) + 16 * (c // 2))
                    pool.sem_inc(passed, 1)
                    pool.dma_start(XR[:, c % 2], x[n, :, N * c:N * (c + 1)].rearrange("(h p) w -> p h w", p=P)) \
                        .then_inc(xr_in[c % 2], 16)

                load(0)
                for c in range(NCH):
                    if c + 1 < NCH:
                        load(c + 1)
                    pool.wait_ge(res_done, n * (KC * NCH) + KC * (c + 1))
                    pool.sem_inc(passed, 1)
                    pool.dma_start(x1[n, :, N * c:N * (c + 1)].rearrange("(h p) w -> p h w", p=P), XR[:, c % 2]) \
                        .then_inc(x1_st[c % 2], 16)
            for s in range(2):
                pool.wait_ge(x1_st[s], 8 * NCH * B)

        def copy_matrices(eng, who, n, g, b):
            s = g * AB + b
            eng.wait_ge(a_mm, n * APG + s + 1)
            eng.wait_ge(d_mm, n * DPG + NBY * max(g - 1, 0))
            py = b * APOS // BW
            nb = NB if py < LAST else NB - NBX
            at = b * APOS
            dst = A[:, g % 2, :nb, at:at + APOS].rearrange("q k a -> q a k")
            src = psA[:Q, b % 4, :APOS * nb].rearrange("q (a k) -> q a k", k=nb)
            if who:
                nc.vector.tensor_copy(dst, src).then_inc(a_out[1], 1)
            else:
                nc.scalar.activation(dst, src, ACT.Copy).then_inc(a_out[0], 1)

        def copy_outputs(eng, who, n, g, by):
            eng.wait_ge(d_mm, n * DPG + g * NBY + by + 1)
            if g == 0:
                eng.wait_ge(p_mm, n * (KC * NCH))
            rows = BH if by < NBY - 1 else LAST
            q0 = CG * (g % GH)
            dst = D[q0:q0 + CG, g // GH, BH * by:BH * by + rows].rearrange("q y (b x) -> q y b x", b=NBX)
            src = psD[q0:q0 + CG, (g * NBY + by) % 2, :NPOS * NBX].rearrange(
                "q (b y x) -> q y b x", b=NBX, y=BH)[:, :rows]
            if who:
                nc.vector.tensor_copy(dst, src).then_inc(d_out[1], 1)
            else:
                nc.scalar.activation(dst, src, ACT.Copy).then_inc(d_out[0], 1)

        def copies(eng, who, n):
            for b in range(AB):
                if b % 2 == who:
                    copy_matrices(eng, who, n, 0, b)
            for g in range(G):
                for k in range(AB):
                    if k < NBY and (g * NBY + k) % 2 == who:
                        copy_outputs(eng, who, n, g, k)
                    if g + 1 < G and k % 2 == who:
                        copy_matrices(eng, who, n, g + 1, k)

        @block.scalar
        def _(act):
            with act.Fori(0, B) as n:
                copies(act, 0, n)

        @block.vector
        def _(dve):
            dve.wait_ge(w_in, 48)
            with dve.Fori(0, B) as n:
                copies(dve, 1, n)
                for c in range(NCH):
                    dve.wait_ge(xr_in[c % 2], n * (8 * NCH) + 16 * (c // 2) + 16)
                    for m in range(KC):
                        dve.wait_ge(p_mm, n * (KC * NCH) + KC * c + m + 1)
                        nc.vector.scalar_tensor_tensor(XR[:, c % 2, m], psP[:, m], opb_sb[:, m:m + 1], XR[:, c % 2, m],
                                                       ALU.add, ALU.add).then_inc(res_done, 1)

        @block.tensor
        def _(pe):
            pe.wait_ge(w_in, 48)

            def matrices(n, g, b):
                s = g * AB + b
                if s < 4:
                    pe.wait_ge(a_out[b % 2], n * (APG // 2))
                else:
                    pe.wait_ge(a_out[b % 2], n * (APG // 2) + s // 2 - 1)
                if b == 0 and g % GH == 0:
                    pe.wait_ge(kt_in[g // GH], n * 16 + 16)
                k0 = TAPP * (g % GH)
                for a in range(APOS):
                    py, px = divmod(b * APOS + a, BW)
                    nb = NB if py < LAST else NB - NBX
                    at = (BH - 1) * RW + BW - 1 - (py * RW + px)
                    last = nc.tensor.matmul(psA[:Q, b % 4, a * nb:(a + 1) * nb], SEL[k0:k0 + TAPS, at:at + Q],
                                            KT[k0:k0 + TAPS, g // GH, py::BH, px::BW], start=True, stop=True)
                last.then_inc(a_mm, 1)

            def outputs(n, g, by):
                r = g * NBY + by
                if by == 0:
                    for w in range(2):
                        pe.wait_ge(a_out[w], n * (APG // 2) + AB // 2 * (g + 1))
                if g % GH == 0 and by == 0:
                    pe.wait_ge(v_in[g // GH], n * (16 * RH * NBX) + 16 * RH * NBX)
                if r < 2:
                    pe.wait_ge(d_out[r % 2], n * (DPG // 2))
                else:
                    pe.wait_ge(d_out[r % 2], n * (DPG // 2) + r // 2)
                c0 = CG * (g % GH)
                size = NPOS if by < NBY - 1 else LAST * BW
                for bx in range(NBX):
                    k = by * NBX + bx
                    last = nc.tensor.matmul(psD[c0:c0 + CG, r % 2, NPOS * bx:NPOS * bx + size],
                                            V[:, g // GH, k, c0:c0 + CG], A[:, g % 2, k, :size],
                                            start=True, stop=True)
                last.then_inc(d_mm, 1)

            with pe.Fori(0, B) as n:
                for b in range(AB):
                    matrices(n, 0, b)
                for g in range(G):
                    for k in range(AB):
                        if k < NBY:
                            outputs(n, g, k)
                        if g + 1 < G:
                            matrices(n, g + 1, k)
                for w in range(2):
                    pe.wait_ge(d_out[w], n * (DPG // 2) + DPG // 2)
                for c in range(NCH):
                    for m in range(KC):
                        pe.wait_ge(res_done, n * (KC * NCH) + max(KC * c + m - 1, 0))
                        for h in range(KC):
                            last = nc.tensor.matmul(
                                psP[:, m], op_sb[:, h, P * m:P * (m + 1)],
                                D[:, h, N // W * c:N // W * (c + 1)].rearrange("p y w -> p (y w)"),
                                start=(h == 0), stop=(h == KC - 1))
                        last.then_inc(p_mm, 1)

def resample(nc, x, op_w, op_b, ident_d, pix, geo, v_pad, om_raw, sampled, x1, flag):
    B, C, HW = x.shape
    W = 64
    KC = C // P
    TI = HW // P
    WP = v_pad.shape[2]
    CG = C // G
    NK = 4 * PT
    GO = 3 * PT
    TOP = float(W + 2)
    values = v_pad.rearrange("n y w (g c) -> (n y w g) c", g=G)
    om_t = om_raw.rearrange("n t p o -> (n t) p o")
    with ExitStack() as ctx:
        def sb(name, shape, dt=F32):
            return ctx.enter_context(nc.sbuf_tensor("f_" + name, shape, dt))

        def sem(name):
            return ctx.enter_context(nc.semaphore("f_" + name))

        ident = sb("ident", [P, P])
        opw = sb("opw", [P, KC, C])
        opb = sb("opb", [P, KC])
        PIX = sb("PIX", [P, 2, PT])
        OMG = sb("OMG", [P, GO])
        GEO = sb("GEO", [P, 2])
        XY = sb("XY", [P, 2, PT])
        II = sb("II", [P, 2, PT], I32)
        FL = sb("FL", [P, 2, PT])
        OV = sb("OV", [P, 2, PT])
        FR = sb("FR", [P, 2, 2, PT])
        ROW = sb("ROW", [P, PT])
        IDX = sb("IDX", [P, 4, PT], U32)
        WC = sb("WC", [P, 4, PT])
        GV = sb("GV", [P, NK, CG])
        ACC = sb("ACC", [P, CG])
        ST = sb("ST", [P, C])
        SC = sb("SC", [P, KC, P])
        XR = sb("XR", [P, KC, P])
        psT = ctx.enter_context(nc.psum_tensor("f_psT", [P, KC, P], F32))
        psP = ctx.enter_context(nc.psum_tensor("f_psP", [P, KC, P], F32))
        w_in, om_in, geo_in, idx_done, got, gathered, acc_done, acc_st, step, passed = (
            sem(n) for n in ("w_in", "om_in", "geo_in", "idx_done", "got", "gathered", "acc_done", "acc_st", "step", "passed"))
        t_in, turned, copied, mm, res, x1_st = (sem(n) for n in ("t_in", "turned", "copied", "mm", "res", "x1_st"))
        DS = 13
        block = ctx.enter_context(nc.Block())

        @block.sync
        def _(sp):
            for dst, src in ((ident[:], ident_d), (opw[:], op_w.rearrange("(h p) o -> p h o", p=P)),
                             (opb[:], op_b), (PIX[:], pix)):
                sp.dma_start(dst, src).then_inc(w_in, 16)
            sp.wait_ge(w_in, 64)
            fast = sp.value_load(flag, min_val=0, max_val=1)
            with sp.If(fast < 1):
                with sp.Fori(0, B * TI) as t:
                    with sp.Fori(0, G) as g:
                        k = t * G + g
                        sp.wait_ge(acc_done, k)
                        sp.dma_start(OMG[:], om_t[t, :, bass.ds(g * GO, GO)]).then_inc(om_in, 16)
                        sp.dma_start(GEO[:], geo[k].partition_broadcast(P)).then_inc(geo_in, 16)
                        sp.wait_ge(acc_done, k + 1)
                        sp.dma_start(sampled[t, :, bass.ds(g * CG, CG)], ACC[:]).then_inc(acc_st, 16)
                sp.wait_ge(acc_st, 16 * B * TI * G)
                with sp.Fori(0, B) as n:
                    with sp.Fori(0, TI) as t:
                        k = n * TI + t
                        sp.wait_ge(x1_st, k * 16)
                        sp.dma_start(ST[:], sampled[k]).then_inc(t_in, 16)
                        sp.dma_start(XR[:], x[n, :, bass.ds(t * P, P)].rearrange("(h p) w -> p h w", p=P)) \
                            .then_inc(t_in, 16)
                        sp.wait_ge(res, k * KC + KC)
                        sp.dma_start(x1[n, :, bass.ds(t * P, P)].rearrange("(h p) w -> p h w", p=P), XR[:]) \
                            .then_inc(x1_st, 16)
                sp.wait_ge(x1_st, 16 * B * TI)

        @block.gpsimd
        def _(pool):
            fast = pool.value_load(flag, min_val=0, max_val=1)
            with pool.If(fast < 1):
                with pool.Fori(0, B * TI) as t:
                    with pool.Fori(0, G) as g:
                        k = t * G + g
                        pool.wait_ge(idx_done, k + 1)
                        pool.sem_inc(passed, 1)
                        for j in range(NK):
                            pool.indirect_dma_start(
                                out=GV[:, j], out_offset=None, in_=values,
                                in_offset=bass.IndirectOffsetOnAxis(ap=IDX[:, j // PT, j % PT:j % PT + 1], axis=0)) \
                                .then_inc(got, 16)
                        pool.wait_ge(got, 16 * NK)
                        pool.sem_inc(gathered, 1)
                        pool.inc_swdge_sem([got], [16 * NK], mode="sub")

        @block.vector
        def _(dve):
            V = nc.vector
            dve.wait_ge(w_in, 64)
            fast = dve.value_load(flag, min_val=0, max_val=1)
            with dve.If(fast < 1):
                with dve.Fori(0, B * TI) as t:
                    with dve.Fori(0, G) as g:
                        k = t * G + g
                        done = [0]

                        def run(ins):
                            done[0] += 1
                            ins.then_inc(step, 1)
                            dve.wait_ge(step, k * DS + done[0])

                        dve.wait_ge(om_in, k * 16 + 16)
                        dve.wait_ge(geo_in, k * 16 + 16)
                        run(V.tensor_tensor(XY[:], OMG[:, :2 * PT].rearrange("p (q s) -> p s q", s=2), PIX[:], ALU.add))
                        run(V.tensor_scalar(XY[:, 1], XY[:, 1], GEO[:, 0:1], None, ALU.add))
                        run(V.tensor_scalar(XY[:], XY[:], 0.0, TOP, ALU.max, ALU.min))
                        run(V.tensor_copy(II[:], XY[:]))
                        run(V.tensor_copy(FL[:], II[:]))
                        run(V.tensor_tensor(OV[:], FL[:], XY[:], ALU.is_gt))
                        run(V.tensor_tensor(FL[:], FL[:], OV[:], ALU.subtract))
                        run(V.tensor_tensor(FR[:, 1], XY[:], FL[:], ALU.subtract))
                        run(V.tensor_scalar(FR[:, 0], FR[:, 1], -1.0, 1.0, ALU.mult, ALU.add))
                        run(V.scalar_tensor_tensor(ROW[:], FL[:, 1], float(WP), FL[:, 0], ALU.mult, ALU.add))
                        run(V.tensor_scalar(ROW[:], ROW[:], float(G), GEO[:, 1:2], ALU.mult, ALU.add))
                        for j in range(4):
                            V.tensor_scalar(IDX[:, j], ROW[:], float((j // 2 * WP + j % 2) * G), None, ALU.add)
                            ins = V.tensor_tensor(WC[:, j], FR[:, j // 2, 1], FR[:, j % 2, 0], ALU.mult)
                        run(ins)
                        V.tensor_tensor(WC[:], WC[:], OMG[:, 2 * PT:].unsqueeze(1).broadcast_to([P, 4, PT]), ALU.mult) \
                            .then_inc(idx_done, 1)
                        dve.wait_ge(idx_done, k + 1)
                        dve.wait_ge(gathered, k + 1)
                        run(V.tensor_tensor(GV[:], GV[:], WC[:].rearrange("p j q -> p (j q)").unsqueeze(2)
                                            .broadcast_to([P, NK, CG]), ALU.mult))
                        dve.wait_ge(acc_st, k * 16)
                        V.tensor_reduce(ACC[:], GV[:].rearrange("p k c -> p c k"), AX.X, ALU.add).then_inc(acc_done, 1)
                        assert done[0] == DS
                with dve.Fori(0, B * TI) as k:
                    dve.wait_ge(t_in, k * 32 + 32)
                    dve.wait_ge(mm, k + 1)
                    for m in range(KC):
                        V.scalar_tensor_tensor(XR[:, m], psP[:, m], opb[:, m:m + 1], XR[:, m], ALU.add, ALU.add) \
                            .then_inc(res, 1)

        @block.tensor
        def _(pe):
            pe.wait_ge(w_in, 64)
            fast = pe.value_load(flag, min_val=0, max_val=1)
            with pe.If(fast < 1):
                with pe.Fori(0, B * TI) as k:
                    pe.wait_ge(t_in, k * 32 + 32)
                    for h in range(KC):
                        last = nc.tensor.transpose(psT[:, h], ST[:, P * h:P * (h + 1)], ident[:])
                    last.then_inc(turned, 1)
                    pe.wait_ge(copied, k + 1)
                    for m in range(KC):
                        for h in range(KC):
                            last = nc.tensor.matmul(psP[:, m], opw[:, h, P * m:P * (m + 1)], SC[:, h],
                                                    start=(h == 0), stop=(h == KC - 1))
                    last.then_inc(mm, 1)

        @block.scalar
        def _(act):
            fast = act.value_load(flag, min_val=0, max_val=1)
            with act.If(fast < 1):
                with act.Fori(0, B * TI) as k:
                    act.wait_ge(turned, k + 1)
                    nc.scalar.activation(SC[:], psT[:], ACT.Copy).then_inc(copied, 1)

def route(nc, x1, gate_w, gate_b, cst, xe, CAP, NJ, tables, yrow, wgt):
    B, C, HW = x1.shape
    E = gate_b.shape[0]
    KC = C // P
    N = 512
    NT = N // P
    NCH = HW // N
    NK = B * NCH
    NTOK = NK * NT
    KMAX = CAP // TM
    with ExitStack() as ctx:
        def sb(name, shape, dt=F32):
            return ctx.enter_context(nc.sbuf_tensor(name, shape, dt))

        def ps(name, shape):
            return ctx.enter_context(nc.psum_tensor(name, shape, F32))

        def sem(name):
            return ctx.enter_context(nc.semaphore(name))

        ident = sb("p3_ident", [P, P])
        tri = sb("tri", [P, P])
        ones = sb("p3_ones", [P, P])
        gw = sb("gw", [P, KC, E])
        gb = sb("gb", [P, E])
        rank = sb("rank", [P, E])
        ebase = sb("ebase", [P, E])
        own = sb("own", [P, NTOK])
        steps = sb("steps", [P, KMAX])
        jota = sb("jota", [P, NJ])
        eps = sb("p3_eps", [P, 1])
        XC = sb("XC", [P, 2, KC, N])
        ST = sb("ST", [P, NT, 6])
        MV = sb("MV", [P, NT, 2])
        STD = sb("p3_STD", [P, NT])
        RS = sb("RS", [P, NT])
        NB = sb("NB", [P, NT])
        XT = sb("XT", [P, 2, NT, C])
        LT = sb("LT", [P, NT, E])
        MX = sb("MX", [P, NT])
        EQ = sb("EQ", [P, NT, E])
        FI = sb("FI", [P, NT])
        OH = sb("OH", [P, NT + 1, E])
        PO = sb("PO", [P, NT, E])
        PB = sb("PB", [P, NT, E])
        POS = sb("POS", [P, NT])
        ROW = sb("ROW", [P, NT])
        KEEP = sb("KEEP", [P, NT])
        IDX = sb("IDX", [P, 2, NT], U32)
        cnt = sb("cnt", [P, E])
        LALL = sb("LALL", [P, NTOK, E])
        OHALL = sb("OHALL", [P, NTOK, E])
        PALL = sb("PALL", [P, NTOK])
        small = sb("small", [P, 8, E])
        CMP = sb("CMP", [P, E, KMAX])
        JC = sb("JC", [P, NJ, E])
        JT = sb("JT", [P, 4, NJ])
        W1 = sb("W1", [P, NTOK])
        psT = ps("psT", [P, 2, 2, C])
        psG = ps("psG", [P, NT, E])
        psC = ps("psC", [P, NT + 1, E])

        c_in, zeroed = sem("c_in"), sem("p3_zeroed")
        x_in = [sem(f"p3_x_in{i}") for i in range(2)]
        t_mm, g_mm, c_mm = sem("t_mm"), sem("g_mm"), sem("c_mm")
        st_done, mv_done, std_done, rs_done, nb_done = (sem(n) for n in ("st_done", "mv_done", "p3_std", "rs_done", "nb_done"))
        xt_done, idx_done, pos_step, oh_done = sem("xt_done"), sem("idx_done"), sem("pos_step"), sem("oh_done")
        sc_st = [sem(f"sc_st{i}") for i in range(2)]
        passed = sem("p3_passed")
        gw_mm, gw_done = sem("gw_mm"), sem("gw_done")
        fin, fin_act = sem("fin"), sem("fin_act")
        block = ctx.enter_context(nc.Block())
        consts = [(ident, cst["ident"]), (tri, cst["tri"]), (own, cst["own"])]
        rows = [(gb, gate_b), (rank, cst["rank"]), (ebase, cst["ebase"]), (steps, cst["steps"]), (jota, cst["jota"])]
        NC_IN = 16 * (len(consts) + len(rows) + 1)
        DCH = 13

        @block.sync
        def _(sp):
            for dst, src in consts:
                sp.dma_start(dst[:], src).then_inc(c_in, 16)
            for dst, src in rows:
                sp.dma_start(dst[:], src.partition_broadcast(P)).then_inc(c_in, 16)
            sp.dma_start(gw[:], gate_w.rearrange("(h p) e -> p h e", p=P)).then_inc(c_in, 16)
            with sp.Fori(0, B) as n:
                for c in range(NCH):
                    sp.wait_ge(g_mm, n * NCH + max(c - 1, 0))
                    sp.dma_start(XC[:, c % 2], x1[n, :, N * c:N * (c + 1)].rearrange("(h p) w -> p h w", p=P)) \
                        .then_inc(x_in[c % 2], 16)

        @block.tensor
        def _(pe):
            pe.wait_ge(c_in, NC_IN)
            pe.wait_ge(zeroed, 4)
            for h in range(KC):
                last = nc.tensor.matmul(psC[:, 0], ones[:], gw[:, h], start=(h == 0), stop=(h == KC - 1))
            last.then_inc(gw_mm, 1)
            pe.wait_ge(gw_done, KC)
            with pe.Fori(0, B) as n:
                def turn(c):
                    pe.wait_ge(x_in[c % 2], n * (8 * NCH) + 16 * (c // 2) + 16)
                    pe.wait_ge(xt_done, n * (NT * NCH) + NT * c)
                    for t in range(NT):
                        for h in range(KC):
                            last = nc.tensor.transpose(psT[:, t // 2, t % 2, P * h:P * (h + 1)],
                                                       XC[:, c % 2, h, P * t:P * (t + 1)], ident[:])
                    last.then_inc(t_mm, 1)
                    pe.wait_ge(pos_step, n * (DCH * NCH) + DCH * c)
                    for t in range(NT):
                        for h in range(KC):
                            last = nc.tensor.matmul(psG[:, t], XC[:, c % 2, h, P * t:P * (t + 1)], gw[:, h],
                                                    start=(h == 0), stop=(h == KC - 1))
                    last.then_inc(g_mm, 1)

                for c in range(NCH):
                    turn(c)
                    pe.wait_ge(oh_done, n * NCH + c + 1)
                    nc.tensor.matmul(psC[:], tri[:], OH[:], start=True, stop=True)
                    for t in range(NT):
                        last = nc.tensor.matmul(psC[:, t + 1:], ones[:],
                                                OH[:, t:t + 1].broadcast_to([P, NT - t, E]),
                                                start=False, stop=True, skip_group_check=True)
                    last.then_inc(c_mm, 1)

        @block.scalar
        def _(act):
            act.wait_ge(zeroed, 4)
            with act.Fori(0, B) as n:
                for c in range(NCH):
                    act.wait_ge(mv_done, n * (NT * NCH) + NT * (c + 1))
                    nc.scalar.activation(STD[:], MV[:, :, 1], ACT.Sqrt, bias=eps[:]).then_inc(std_done, 1)
                    act.wait_ge(nb_done, n * NCH + c + 1)
                    act.wait_ge(sc_st[c % 2], n * (16 * NT * NCH // 2) + 16 * NT * (c // 2))
                    for t in range(NT):
                        nc.scalar.activation(XT[:, c % 2, t], psT[:, t // 2, t % 2], ACT.Identity,
                                             bias=NB[:, t:t + 1], scale=RS[:, t:t + 1]).then_inc(xt_done, 1)
            act.wait_ge(fin, 2)
            nc.scalar.activation(LALL[:], LALL[:], ACT.Exp).then_inc(fin_act, 1)

        @block.gpsimd
        def _(pool):
            nc.gpsimd.memset(ones[:], 1.0).then_inc(zeroed, 1)
            nc.gpsimd.memset(eps[:], 1e-5).then_inc(zeroed, 1)
            nc.gpsimd.memset(OH[:], 0.0).then_inc(zeroed, 1)
            nc.gpsimd.memset(cnt[:], 0.0).then_inc(zeroed, 1)
            with pool.Fori(0, B) as n:
                for c in range(NCH):
                    pool.wait_ge(xt_done, n * (NT * NCH) + NT * (c + 1))
                    pool.wait_ge(idx_done, n * NCH + c + 1)
                    pool.sem_inc(passed, 1)
                    for t in range(NT):
                        pool.indirect_dma_start(
                            out=xe, out_offset=bass.IndirectOffsetOnAxis(ap=IDX[:, c % 2, t:t + 1], axis=0),
                            in_=XT[:, c % 2, t], in_offset=None).then_inc(sc_st[c % 2], 16)
            for s in range(2):
                pool.wait_ge(sc_st[s], 16 * NT * NK // 2)

        @block.vector
        def _(dve):
            dve.wait_ge(c_in, NC_IN)
            dve.wait_ge(zeroed, 4)

            def over(ap, k):
                return ap.unsqueeze(1).broadcast_to([P, k, E])

            def per(ap, k):
                return ap.unsqueeze(2).broadcast_to([P, k, E])

            V = nc.vector
            dve.wait_ge(gw_mm, 1)
            for h in range(KC):
                V.scalar_tensor_tensor(gw[:, h], psC[:, 0], -1.0 / C, gw[:, h], ALU.mult, ALU.add).then_inc(gw_done, 1)
            with dve.Fori(0, B) as n:
                for c in range(NCH):
                    base = n * (DCH * NCH) + DCH * c
                    done = [0]

                    def step(ins):
                        done[0] += 1
                        ins.then_inc(pos_step, 1)
                        dve.wait_ge(pos_step, base + done[0])

                    dve.wait_ge(t_mm, n * NCH + c + 1)
                    for t in range(NT):
                        V.bn_stats(ST[:, t], psT[:, t // 2, t % 2]).then_inc(st_done, 1)
                    dve.wait_ge(st_done, n * (NT * NCH) + NT * (c + 1))
                    dve.sem_inc(passed, 1)
                    for t in range(NT):
                        V.bn_aggr(MV[:, t], ST[:, t]).then_inc(mv_done, 1)
                    dve.wait_ge(std_done, n * NCH + c + 1)
                    dve.wait_ge(xt_done, n * (NT * NCH) + NT * c)
                    V.reciprocal(RS[:], STD[:]).then_inc(rs_done, 1)
                    dve.wait_ge(rs_done, n * NCH + c + 1)
                    V.scalar_tensor_tensor(NB[:], MV[:, :, 0], -1.0, RS[:], ALU.mult, ALU.mult).then_inc(nb_done, 1)
                    dve.wait_ge(g_mm, n * NCH + c + 1)
                    tiles = bass.ds(n * (NT * NCH) + NT * c, NT)
                    step(V.tensor_tensor(LT[:], psG[:], per(RS[:], NT), ALU.mult))
                    step(V.tensor_tensor(LT[:], LT[:], over(gb[:], NT), ALU.add))
                    V.tensor_copy(LALL[:, tiles], LT[:])
                    step(V.tensor_reduce(MX[:], LT[:], AX.X, ALU.max))
                    step(V.tensor_tensor(EQ[:], LT[:], per(MX[:], NT), ALU.is_equal))
                    step(V.tensor_tensor(EQ[:], EQ[:], over(rank[:], NT), ALU.mult))
                    step(V.tensor_reduce(FI[:], EQ[:], AX.X, ALU.max))
                    V.tensor_tensor(OH[:, :NT], EQ[:], per(FI[:], NT), ALU.is_equal).then_inc(oh_done, 1)
                    dve.wait_ge(oh_done, n * NCH + c + 1)
                    V.tensor_copy(OHALL[:, tiles], OH[:, :NT])
                    step(V.tensor_tensor(PB[:], OH[:, :NT], over(ebase[:], NT), ALU.mult))
                    V.tensor_reduce(ROW[:], PB[:], AX.X, ALU.add)
                    dve.wait_ge(c_mm, n * NCH + c + 1)
                    step(V.tensor_tensor(PO[:], psC[:, :NT], over(cnt[:], NT), ALU.add))
                    step(V.tensor_tensor(PO[:], PO[:], OH[:, :NT], ALU.mult))
                    V.tensor_tensor(cnt[:], cnt[:], psC[:, NT], ALU.add)
                    step(V.tensor_reduce(POS[:], PO[:], AX.X, ALU.add))
                    V.tensor_copy(PALL[:, tiles], POS[:])
                    V.tensor_scalar(KEEP[:], POS[:], float(CAP), None, ALU.is_lt)
                    step(V.tensor_tensor(ROW[:], ROW[:], own[:, tiles], ALU.subtract))
                    step(V.tensor_tensor(ROW[:], ROW[:], POS[:], ALU.add))
                    step(V.tensor_tensor(ROW[:], ROW[:], KEEP[:], ALU.mult))
                    assert done[0] == DCH
                    dve.wait_ge(sc_st[c % 2], n * (16 * NT * NCH // 2) + 16 * NT * (c // 2))
                    V.tensor_tensor(IDX[:, c % 2], ROW[:], own[:, tiles], ALU.add).then_inc(idx_done, 1)

            dve.wait_ge(idx_done, NK)
            done = [0]

            def last(ins):
                done[0] += 1
                ins.then_inc(fin, 1)
                dve.wait_ge(fin, done[0])

            last(V.tensor_reduce(W1[:], LALL[:], AX.X, ALU.max))
            last(V.tensor_tensor(LALL[:], LALL[:], per(W1[:], NTOK), ALU.subtract))
            kept, ntile, first, end = small[:, 0], small[:, 1], small[:, 2], small[:, 3]
            last(V.tensor_scalar(kept, cnt[:], float(CAP), None, ALU.min))
            last(V.tensor_tensor(CMP[:], kept.unsqueeze(2).broadcast_to([P, E, KMAX]),
                                 steps[:].unsqueeze(1).broadcast_to([P, E, KMAX]), ALU.is_gt))
            last(V.tensor_reduce(ntile, CMP[:], AX.X, ALU.add))
            last(V.memset(first, 0.0))
            for e in range(1, E):
                last(V.tensor_tensor(first[:, e:e + 1], first[:, e - 1:e], ntile[:, e - 1:e], ALU.add))
            last(V.tensor_tensor(end, first, ntile, ALU.add))
            last(V.tensor_tensor(JC[:], jota[:].unsqueeze(2).broadcast_to([P, NJ, E]), over(end, NJ), ALU.is_ge))
            last(V.tensor_reduce(JT[:, 0], JC[:], AX.X, ALU.add))
            last(V.tensor_tensor(JC[:], JC[:], over(ntile, NJ), ALU.mult))
            last(V.tensor_reduce(JT[:, 1], JC[:], AX.X, ALU.add))
            last(V.tensor_tensor(JT[:, 1], jota[:], JT[:, 1], ALU.subtract))
            last(V.tensor_scalar(JT[:, 0], JT[:, 0], float(E - 1), None, ALU.min))
            last(V.tensor_scalar(JT[:, 1], JT[:, 1], float(KMAX - 1), float(TM), ALU.min, ALU.mult))
            last(V.scalar_tensor_tensor(JT[:, 2], JT[:, 0], float(CAP), JT[:, 1], ALU.mult, ALU.add))
            last(V.tensor_copy(tables[:, 0], JT[0:1, 0]))
            last(V.tensor_copy(tables[:, 1], JT[0:1, 2]))
            last(V.tensor_tensor(OHALL[:], OHALL[:], over(first, NTOK), ALU.mult))
            last(V.tensor_reduce(own[:], OHALL[:], AX.X, ALU.add))
            last(V.scalar_tensor_tensor(own[:], own[:], float(TM), PALL[:], ALU.mult, ALU.add))
            last(V.tensor_scalar(PALL[:], PALL[:], float(CAP), None, ALU.is_lt))
            last(V.tensor_tensor(yrow[:], own[:], PALL[:], ALU.mult))
            dve.wait_ge(fin_act, 1)
            last(V.tensor_reduce(W1[:], LALL[:], AX.X, ALU.add))
            last(V.reciprocal(W1[:], W1[:]))
            last(V.tensor_tensor(wgt[:], W1[:], PALL[:], ALU.mult))

def experts(nc, xe, w1, b1, w2, b2, ident_d, ye, CAP, NJ, tables, room):
    E, C, FF = w1.shape
    KC = C // P
    FC = FF // P
    NT = TM // P
    assert NJ % 2 == 0
    with ExitStack() as ctx:
        def sb(name, shape, dt=F32):
            return ctx.enter_context(nc.sbuf_tensor(name, shape, dt))

        def ps(name, shape):
            return ctx.enter_context(nc.psum_tensor(name, shape, F32))

        def sem(name):
            return ctx.enter_context(nc.semaphore(name))

        ident = sb("p4_ident", [P, P])
        W1 = sb("w1_sb", [P, 2, KC, FF])
        W2 = sb("w2_sb", [P, 2, FC, C])
        B1 = sb("b1_sb", [P, 2, FC])
        B2 = sb("b2_sb", [P, 2, C])
        XR = sb("p4_XR", [P, 2, NT, C])
        XT = sb("p4_XT", [P, 2, KC, TM])
        HM = sb("HM", [P, FC, TM])
        Y = sb("Y", [P, 2, NT, C])
        ABS = sb("ABS", [P, NT, C])
        ASUM = sb("ASUM", [P, 1])
        psT = ps("p4_psT", [P, KC, TM])
        psH = ps("psH", [P, 4, TM])
        psY = ps("psY", [P, NT, C])

        id_in, zeroed = sem("id_in"), sem("p4_zeroed")
        w_in = [sem(f"p4_w_in{i}") for i in range(2)]
        x_in = [sem(f"p4_x_in{i}") for i in range(2)]
        y_st = [sem(f"y_st{i}") for i in range(2)]
        t_mm, t_out, h_mm, h_out, y_mm, y_out, abs_out, sum_done = (
            sem(n) for n in ("p4_t_mm", "t_out", "h_mm", "h_out", "y_mm", "y_out", "abs_out", "sum_done"))
        block = ctx.enter_context(nc.Block())

        @block.sync
        def _(sp):
            sp.dma_start(ident[:], ident_d).then_inc(id_in, 16)
            with sp.Fori(0, NJ // 2) as i:
                for s in range(2):
                    expert = sp.value_load(tables[0:1, 0, bass.ds(2 * i + s, 1)], min_val=0, max_val=E - 1)
                    row = sp.value_load(tables[0:1, 1, bass.ds(2 * i + s, 1)], min_val=0, max_val=E * CAP - TM)
                    sp.wait_ge(t_mm, 2 * i + max(s - 1, 0))
                    sp.dma_start(XR[:, s], xe[bass.ds(row, TM), :].rearrange("(t p) c -> p t c", p=P)) \
                        .then_inc(x_in[s], 16)
                    sp.wait_ge(y_mm, 2 * i + max(s - 1, 0))
                    sp.wait_ge(y_out, 2 * i + max(s - 1, 0))
                    sp.dma_start(W1[:, s], w1[bass.ds(expert, 1)].rearrange("e (h p) f -> p (e h) f", p=P)) \
                        .then_inc(w_in[s], 16)
                    sp.dma_start(B1[:, s], b1[bass.ds(expert, 1)].rearrange("e p m -> p (e m)")).then_inc(w_in[s], 16)
                    sp.dma_start(W2[:, s], w2[bass.ds(expert, 1)].rearrange("e (m p) c -> p (e m) c", p=P)) \
                        .then_inc(w_in[s], 16)
                    sp.dma_start(B2[:, s], b2[bass.ds(expert, 1)].rearrange("e c -> (e c)").partition_broadcast(P)) \
                        .then_inc(w_in[s], 16)

        @block.gpsimd
        def _(pool):
            nc.gpsimd.memset(room[:, 0:1], 0.0).then_inc(zeroed, 1)
            with pool.Fori(0, NJ // 2) as i:
                for s in range(2):
                    pool.wait_ge(y_out, 2 * i + s + 1)
                    pool.dma_start(ye[bass.ds((2 * i + s) * TM, TM), :].rearrange("(t p) c -> p t c", p=P), Y[:, s]) \
                        .then_inc(y_st[s], 16)
            for s in range(2):
                pool.wait_ge(y_st[s], 8 * NJ)

        @block.tensor
        def _(pe):
            def turn(j, s, slot_tile):
                pe.wait_ge(x_in[s], slot_tile * 16 + 16)
                pe.wait_ge(t_out, j)
                for t in range(NT):
                    for h in range(KC):
                        last = nc.tensor.transpose(psT[:, h, P * t:P * (t + 1)],
                                                   XR[:, s, t, P * h:P * (h + 1)], ident[:])
                last.then_inc(t_mm, 1)

            def hidden(j, s, i):
                pe.wait_ge(t_out, j + 1)
                pe.wait_ge(w_in[s], i * 64 + 64)
                for m in range(FC):
                    if m >= 4:
                        pe.wait_ge(h_out, j * FC + m - 3)
                    else:
                        pe.wait_ge(h_out, j * FC)
                    for h in range(KC):
                        last = nc.tensor.matmul(psH[:, m % 4], W1[:, s, h, P * m:P * (m + 1)], XT[:, s, h],
                                                start=(h == 0), stop=(h == KC - 1))
                    last.then_inc(h_mm, 1)

            def output(j, s):
                pe.wait_ge(h_out, j * FC + FC)
                pe.wait_ge(y_out, j)
                for t in range(NT):
                    for m in range(FC):
                        last = nc.tensor.matmul(psY[:, t], HM[:, m, P * t:P * (t + 1)], W2[:, s, m],
                                                start=(m == 0), stop=(m == FC - 1))
                last.then_inc(y_mm, 1)

            pe.wait_ge(id_in, 16)
            turn(0, 0, 0)
            if NJ > 2:
                with pe.Fori(0, NJ // 2 - 1) as i:
                    hidden(2 * i, 0, i)
                    turn(2 * i + 1, 1, i)
                    output(2 * i, 0)
                    hidden(2 * i + 1, 1, i)
                    turn(2 * i + 2, 0, i + 1)
                    output(2 * i + 1, 1)
            i = NJ // 2 - 1
            hidden(2 * i, 0, i)
            turn(2 * i + 1, 1, i)
            output(2 * i, 0)
            hidden(2 * i + 1, 1, i)
            output(2 * i + 1, 1)

        @block.scalar
        def _(act):
            with act.Fori(0, NJ // 2) as i:
                for s in range(2):
                    j = 2 * i + s
                    act.wait_ge(w_in[s], i * 64 + 64)
                    act.wait_ge(y_mm, j)
                    for m in range(FC):
                        act.wait_ge(h_mm, j * FC + m + 1)
                        nc.scalar.activation(HM[:, m], psH[:, m % 4], ACT.Relu, bias=B1[:, s, m:m + 1]) \
                            .then_inc(h_out, 1)
                    act.wait_ge(y_out, j + 1)
                    act.wait_ge(sum_done, j)
                    nc.scalar.activation(ABS[:], Y[:, s], ACT.Abs, accum_out=ASUM[:]).then_inc(abs_out, 1)

        @block.vector
        def _(dve):
            dve.wait_ge(zeroed, 1)

            def turned(j, s):
                dve.wait_ge(t_mm, j + 1)
                nc.vector.tensor_copy(XT[:, s], psT[:]).then_inc(t_out, 1)

            def finish(j, s, i):
                dve.wait_ge(y_mm, j + 1)
                dve.wait_ge(y_st[s], i * 16)
                dve.wait_ge(abs_out, j)
                nc.vector.tensor_tensor(Y[:, s], psY[:], B2[:, s].unsqueeze(1).broadcast_to([P, NT, C]), ALU.add) \
                    .then_inc(y_out, 1)
                dve.wait_ge(abs_out, j + 1)
                nc.vector.tensor_tensor(room[:, 0:1], room[:, 0:1], ASUM[:], ALU.add).then_inc(sum_done, 1)

            turned(0, 0)
            if NJ > 2:
                with dve.Fori(0, NJ // 2 - 1) as i:
                    turned(2 * i + 1, 1)
                    finish(2 * i, 0, i)
                    turned(2 * i + 2, 0)
                    finish(2 * i + 1, 1, i)
            i = NJ // 2 - 1
            turned(2 * i + 1, 1)
            finish(2 * i, 0, i)
            finish(2 * i + 1, 1, i)


def all_partitions(nc, ident_d, values, flag, op, limit, compare, tag):
    with ExitStack() as ctx:
        ident = ctx.enter_context(nc.sbuf_tensor(f"{tag}_ident", [P, P], F32))
        red = ctx.enter_context(nc.sbuf_tensor(f"{tag}_red", [1, 2], F32))
        row = ctx.enter_context(nc.psum_tensor(f"{tag}_row", [P, P], F32))
        id_in, turned, step = (ctx.enter_context(nc.semaphore(f"{tag}_{n}")) for n in ("in", "turned", "step"))
        block = ctx.enter_context(nc.Block())

        @block.sync
        def _(sp):
            sp.dma_start(ident[:], ident_d).then_inc(id_in, 16)

        @block.tensor
        def _(pe):
            pe.wait_ge(id_in, 16)
            nc.tensor.transpose(row[0:1], values, ident[:]).then_inc(turned, 1)

        @block.vector
        def _(dve):
            dve.wait_ge(turned, 1)
            nc.vector.tensor_reduce(red[:, 0:1], row[0:1], AX.X, op).then_inc(step, 1)
            dve.wait_ge(step, 1)
            nc.vector.tensor_scalar(red[:, 1:2], red[:, 0:1], limit, None, compare).then_inc(step, 1)
            dve.wait_ge(step, 2)
            nc.vector.tensor_copy(flag, red[:, 1:2]).then_inc(step, 1)
            dve.wait_ge(step, 3)


def combine(nc, x1, ye, ident_d, out, yrow, wgt, flag, HUGE=3.4028234663852886e38):
    B, C, HW = x1.shape
    KC = C // P
    N = 512
    NT = N // P
    NCH = HW // N
    with ExitStack() as ctx:
        def sb(name, shape, dt=F32):
            return ctx.enter_context(nc.sbuf_tensor(name, shape, dt))

        def ps(name, shape):
            return ctx.enter_context(nc.psum_tensor(name, shape, F32))

        def sem(name):
            return ctx.enter_context(nc.semaphore(name))

        ident = sb("p5_ident", [P, P])
        YG = sb("YG", [P, 4, NT, C])
        XC = sb("p5_XC", [P, 4, KC, N])
        PART = sb("PART", [P, 2, NT, C])
        TEST = sb("TEST", [P, NT, C])
        IDX = sb("p5_IDX", [P, 4, NT], U32)
        WS = sb("WS", [P, 4, NT])
        psT = ps("p5_psT", [P, 2, KC, N])

        id_in, passed = sem("p5_id_in"), sem("p5_passed")
        g_in = [sem(f"g_in{i}") for i in range(4)]
        x_in = [sem(f"p5_x_in{i}") for i in range(4)]
        o_st = [sem(f"o_st{i}") for i in range(4)]
        pick, scaled, clean, t_mm, added, fix = (sem(n) for n in ("pick", "scaled", "clean", "p5_t_mm", "added", "fix"))
        block = ctx.enter_context(nc.Block())
        assert NCH % 4 == 0
        QS = NCH // 4

        @block.sync
        def _(sp):
            sp.dma_start(ident[:], ident_d).then_inc(id_in, 16)
            with sp.Fori(0, B) as n:
                for c in range(NCH):
                    sp.wait_ge(o_st[c % 4], n * (16 * QS) + 16 * (c // 4))
                    sp.dma_start(XC[:, c % 4], x1[n, :, N * c:N * (c + 1)].rearrange("(h p) w -> p h w", p=P)) \
                        .then_inc(x_in[c % 4], 16)

        @block.gpsimd
        def _(pool):
            with pool.Fori(0, B) as n:
                for c in range(NCH):
                    pool.wait_ge(pick, n * NCH + c + 1)
                    pool.wait_ge(t_mm, n * NCH + max(c - 3, 0))
                    pool.sem_inc(passed, 1)
                    for t in range(NT):
                        pool.indirect_dma_start(
                            out=YG[:, c % 4, t], out_offset=None, in_=ye,
                            in_offset=bass.IndirectOffsetOnAxis(ap=IDX[:, c % 4, t:t + 1], axis=0)) \
                            .then_inc(g_in[c % 4], 16)

        def store(act, n, c):
            act.wait_ge(added, n * NCH + c + 1)
            act.dma_start(out[n, :, N * c:N * (c + 1)].rearrange("(h p) w -> p h w", p=P), XC[:, c % 4]) \
                .then_inc(o_st[c % 4], 16)

        @block.scalar
        def _(act):
            with act.Fori(0, B) as n:
                for c in range(NCH):
                    act.wait_ge(g_in[c % 4], n * (16 * NT * QS) + 16 * NT * (c // 4 + 1))
                    for t in range(NT):
                        last = nc.scalar.activation(YG[:, c % 4, t], YG[:, c % 4, t], ACT.Copy,
                                                    scale=WS[:, c % 4, t:t + 1])
                    last.then_inc(scaled, 1)
                    if c >= 1:
                        store(act, n, c - 1)
                store(act, n, NCH - 1)
            for s in range(4):
                act.wait_ge(o_st[s], 16 * QS * B)

        @block.tensor
        def _(pe):
            pe.wait_ge(id_in, 16)
            with pe.Fori(0, B) as n:
                for c in range(NCH):
                    pe.wait_ge(clean, n * NCH + c + 1)
                    pe.wait_ge(added, n * NCH + max(c - 1, 0))
                    for h in range(KC):
                        for t in range(NT):
                            last = nc.tensor.transpose(psT[:, c % 2, h, P * t:P * (t + 1)],
                                                       YG[:, c % 4, t, P * h:P * (h + 1)], ident[:])
                    last.then_inc(t_mm, 1)

        @block.vector
        def _(dve):
            V = nc.vector
            finite = dve.value_load(flag, min_val=0, max_val=1)

            def choose(n, c):
                dve.wait_ge(scaled, n * NCH + max(c - 3, 0))
                tiles = bass.ds(n * (NT * NCH) + NT * c, NT)
                V.tensor_copy(WS[:, c % 4], wgt[:, tiles])
                V.tensor_copy(IDX[:, c % 4], yrow[:, tiles]).then_inc(pick, 1)

            with dve.Fori(0, B) as n:
                for c in range(3):
                    choose(n, c)
                for c in range(NCH):
                    if c + 3 < NCH:
                        choose(n, c + 3)
                    dve.wait_ge(scaled, n * NCH + c + 1)
                    dve.sem_inc(passed, 1)
                    with dve.If(finite < 1):
                        y = YG[:, c % 4]
                        done = [0]

                        def step(ins):
                            done[0] += 1
                            ins.then_inc(fix, 1)
                            dve.wait_ge(fix, n * (10 * NCH) + 10 * c + done[0])

                        for part, keep, cap, beyond, within in ((PART[:, 0], ALU.max, 1.0, ALU.is_gt, ALU.is_le),
                                                                (PART[:, 1], ALU.min, -1.0, ALU.is_lt, ALU.is_ge)):
                            clip = ALU.min if cap > 0 else ALU.max
                            step(V.tensor_scalar(part, y, 0.0, cap * HUGE, keep, clip))
                            step(V.tensor_scalar(TEST[:], y, 0.0, cap * HUGE, keep, within))
                            step(V.tensor_tensor(part, part, TEST[:], ALU.mult))
                            step(V.tensor_scalar(TEST[:], y, 0.0, cap * HUGE, keep, beyond))
                            step(V.scalar_tensor_tensor(part, TEST[:], cap * 1e4, part, ALU.mult, ALU.add))
                        V.tensor_tensor(y, PART[:, 0], PART[:, 1], ALU.add)
                    dve.drain().then_inc(clean, 1)
                    dve.wait_ge(x_in[c % 4], n * (16 * QS) + 16 * (c // 4) + 16)
                    dve.wait_ge(t_mm, n * NCH + c + 1)
                    V.tensor_tensor(XC[:, c % 4], XC[:, c % 4], psT[:, c % 2], ALU.add).then_inc(added, 1)


def metaformer_layer(nc, x, dw_w, dw_b, om_w, om_b, vp_w, vp_b, op_w, op_b, gate_w, gate_b, w1, b1, w2, b2,
                     cst, out):
    B, C, HW = x.shape
    W = 64
    H = HW // W
    T = B * HW
    E = w1.shape[0]
    CAP = -(-5 * T // (4 * E))
    NJ = T // TM + E
    OM = om_w.shape[1]
    rows = BH * -(-H // BH) + 2 * HALO
    assert CAP % TM == 0 and T % TM == 0

    def dram(name, shape):
        return nc.dram_tensor(name, shape, F32, kind="Internal").ap()

    v_pad = dram("v_pad", (B, rows, W + 2 * HALO, C))
    xn = dram("xn", (B, C, HW))
    om_raw = dram("om_raw", (B, HW // P, P, OM))
    taps_t = dram("taps_t", (B, C // P, P, HW))
    sampled = dram("sampled", (T // P, P, C))
    x1 = dram("x1", (B, C, HW))
    xe = dram("xe", (E * CAP + T, C))
    ye = dram("ye", (NJ * TM, C))
    with ExitStack() as ctx:
        def sb(name, shape, dt=F32):
            return ctx.enter_context(nc.sbuf_tensor(name, shape, dt))

        room = sb("room", [P, 2])
        near = sb("near", [1, 1], I32)
        finite = sb("finite", [1, 1], I32)
        tables = sb("tables", [1, 2, NJ], I32)
        yrow = sb("yrow", [P, T // P], U32)
        wgt = sb("wgt", [P, T // P])
        conv_features(nc, x, dw_w, dw_b, om_w, om_b, vp_w, vp_b, cst["ident"], cst["mean"],
                      xn, v_pad, om_raw, taps_t, xe[0:E * CAP], room)
        all_partitions(nc, cst["ident"], room[:, 0:1], near[:], ALU.min, 0.0, ALU.is_gt, "near")
        deform(nc, x, op_w, op_b, cst["select"], v_pad, taps_t, x1)
        resample(nc, x, op_w, op_b, cst["ident"], cst["pix"], cst["geo"], v_pad, om_raw, sampled, x1, near[:])
        route(nc, x1, gate_w, gate_b, cst, xe, CAP, NJ, tables, yrow, wgt)
        experts(nc, xe, w1, b1, w2, b2, cst["ident"], ye, CAP, NJ, tables, room)
        all_partitions(nc, cst["ident"], room[:, 0:1], finite[:], ALU.add, 3.4028234663852886e38, ALU.is_le, "fin")
        combine(nc, x1, ye, cst["ident"], out, yrow, wgt, finite[:])


def constants(np, B, H, W, C, E):
    T = B * H * W
    cap = -(-5 * T // (4 * E))
    p, q = np.arange(P), np.arange(PT)
    last = (BH - 1) * RW + BW - 1
    select = np.zeros((P, last + Q))
    for g in range(P // TAPP):
        for tap in range(TAPS):
            select[TAPP * g + tap, last + tap // 5 * RW + tap % 5] = 1
    pix = np.zeros((P, 2, PT))
    pix[:, 0] = (p % W)[:, None] + HALO - 1 + q // 3
    pix[:, 1] = (p // W)[:, None] + HALO - 1 + q % 3
    tile, g = np.arange(T // P)[:, None], np.arange(G)[None]
    rows = BH * -(-H // BH) + 2 * HALO
    per = H * W // P
    geo = np.stack([P // W * (tile % per) + 0 * g, tile // per * rows * (W + 2 * HALO) * G + g], -1)
    made = {
        "ident": np.eye(P), "mean": np.full((P, P), 1 / C), "select": select, "pix": pix,
        "geo": geo.reshape(-1, 2), "tri": np.triu(np.ones((P, P)), 1), "own": E * cap + np.arange(T // P)[None] * P + p[:, None],
        "rank": E - np.arange(E), "ebase": np.arange(E) * cap, "steps": np.arange(cap // TM) * TM,
        "jota": np.arange(T // TM + E),
    }
    return {k: v.astype(np.float32) for k, v in made.items()}


def kernel(**inputs):
    import numpy as _np
    import concourse.bacc as _bacc
    from concourse.bass_utils import run_bass_kernel_spmd as _run

    nc = _bacc.Bacc("TRN2", target_bir_lowering=False, num_devices=1)
    a = {k: _np.asarray(v) for k, v in inputs.items()}
    B, C, H, W = a["x"].shape
    E, _, FF = a["L0_ffn_w1"].shape
    given = {
        "x": a["x"].reshape(B, C, H * W),
        "dw_w": a["L0_conv_dw_w"].reshape(C, 9), "dw_b": a["L0_conv_dw_b"].reshape(C // P, P).T,
        "om_w": a["L0_conv_om_w"].T, "om_b": a["L0_conv_om_b"],
        "vp_w": a["L0_conv_vp_w"].T, "vp_b": a["L0_conv_vp_b"],
        "op_w": a["L0_conv_op_w"].T, "op_b": a["L0_conv_op_b"].reshape(C // P, P).T,
        "gate_w": a["L0_ffn_gate_w"], "gate_b": a["L0_ffn_gate_b"],
        "w1": a["L0_ffn_w1"], "b1": a["L0_ffn_b1"].reshape(E, FF // P, P).transpose(0, 2, 1),
        "w2": a["L0_ffn_w2"], "b2": a["L0_ffn_b2"],
    }
    tables = constants(_np, B, H, W, C, E)
    arrays = {f"in_{k}": _np.ascontiguousarray(v) for k, v in {**given, **tables}.items()}
    aps = {k: nc.dram_tensor(k, v.shape, F32, kind="ExternalInput").ap() for k, v in arrays.items()}
    out = nc.dram_tensor("out_0", (B, C, H * W), F32, kind="ExternalOutput").ap()
    metaformer_layer(nc, *[aps[f"in_{k}"] for k in given], {k: aps[f"in_{k}"] for k in tables}, out)
    r = _run(nc, [arrays], core_ids=[0])
    return r.results[0]["out_0"].reshape(B, C, H, W)
```

```python
from contextlib import ExitStack

import concourse.bass as bass
from concourse import mybir

ALU = mybir.AluOpType
ACT = mybir.ActivationFunctionType
AX = mybir.AxisListType
F32 = mybir.dt.float32
I32 = mybir.dt.int32
U32 = mybir.dt.uint32

P = 128
TM = 512
G, PT = 8, 9
HALO = 2
BH, BW = 6, 8
RH, RW = BH + 2 * HALO, BW + 2 * HALO
Q = RH * RW
NPOS = BH * BW
TAPS = 25
TAPP = 32


def conv_features(nc, x, dw_w, dw_b, om_w, om_b, vp_w, vp_b, ident_d, mean_d,
                  xn, v_pad, om_raw, taps_t, routed_x, room):
    B, C, HW = x.shape
    W = 64
    H = HW // W
    KC = C // P
    RC = 512 // W
    N = RC * W
    NCH = HW // N
    NT = N // P
    OM = om_w.shape[1]
    TG = NT * G
    WP = W + 2 * HALO
    VR = v_pad.shape[1]
    ZB = 2048
    with ExitStack() as ctx:
        def sb(name, shape):
            return ctx.enter_context(nc.sbuf_tensor(name, shape, F32))

        def ps(name, shape):
            return ctx.enter_context(nc.psum_tensor(name, shape, F32))

        def sem(name):
            return ctx.enter_context(nc.semaphore(name))

        ident = sb("p1_ident", [P, P])
        mean_w = sb("mean_w", [P, P])
        dw_sb = sb("dw_sb", [P, KC, 9])
        dwb_sb = sb("dwb_sb", [P, KC])
        om_sb = sb("om_sb", [P, KC, OM])
        vp_sb = sb("vp_sb", [P, KC, C])
        omb_bc = sb("omb_bc", [P, OM])
        vpb_bc = sb("vpb_bc", [P, C])
        X = sb("X", [P, 2, KC, N])
        SQ = sb("SQ", [P, KC, N])
        eps = sb("eps", [P, 1])
        ones = sb("ones", [P, P])
        STD = sb("STD", [P, NT])
        RSTD = sb("RSTD", [P, NT])
        RDIAG = sb("RDIAG", [P, NT, P])
        XL = sb("XL", [P, KC, H + 2, W + 2])
        TK = sb("TK", [P, 2, NT, C])
        F = sb("F", [P, KC, N])
        OMS = sb("OMS", [P, NT, OM])
        VS = sb("VS", [P, 2, NT, C])
        TENT = sb("TENT", [P, 3, TG, 2 * PT])
        MTX = sb("MTX", [P, TG, 3, PT])
        RM = sb("RM", [P, 3, TG, 3, PT])
        K = sb("K", [P, TG, TAPP])
        KS = sb("KS", [P, 2, N])
        zero = sb("zero", [P, ZB])
        psM = ps("psM", [P, N])
        psR = ps("psR", [P, N])
        psVal = ps("psVal", [P, NT, C])
        psX = psVal[:].rearrange("p t c -> p (t c)").rearrange("p (h w) -> p h w", h=KC)
        psO = ps("psO", [P, 2, 512])
        psV = psR[:, :NT]
        psK = ps("psK", [P, 2, N])

        const_in = sem("const_in")
        zeroed = sem("zeroed")
        passed = sem("p1_passed")
        x_in = [sem(f"x_in{i}") for i in range(2)]
        mean_done, sub_done, sq_done, var_done = sem("mean_done"), sem("sub_done"), sem("sq_done"), sem("var_done")
        diag_done, spread_mm = sem("diag_done"), sem("spread_mm")
        xn_st = [sem(f"xn_st{i}") for i in range(2)]
        tk_in = [sem(f"tk_in{i}") for i in range(2)]
        tk_turned = sem("tk_turned")
        xl_done, std_done = sem("xl_done"), sem("std_done")
        rstd_done, norm_done, dw_step, om_mm = sem("rstd_done"), sem("norm_done"), sem("dw_step"), sem("om_mm")
        v_mm, v_raw, v_ready = sem("v_mm"), sem("v_raw"), sem("v_ready")
        v_st = [sem(f"v_st{i}") for i in range(2)]
        om_evac, om_ready, om_st, tent_done = sem("om_evac"), sem("om_ready"), sem("om_st"), sem("tent_done")
        tent_step = sem("tent_step")
        mtx_done, rm_done, k_clr, k_add, tr_mm = sem("mtx_done"), sem("rm_done"), sem("k_clr"), sem("k_add"), sem("tr_mm")
        ks_ready, ks_st, red_done, fill_st = sem("ks_ready"), sem("ks_st"), sem("red_done"), sem("fill_st")
        block = ctx.enter_context(nc.Block())

        LOAD, NORM, VALUE, TURN, OFFSETS, WEIGHTS = -2, -1, 0, NCH + 1, NCH + 3, NCH + 4
        AHEAD = 2

        def stage(i, s, lag):
            d, c = divmod(s - lag, NCH)
            if isinstance(i, int) and not 0 <= i + d < B:
                return []
            return [(i + d, c, (i + d) * NCH + c)]

        def stream(eng, step):
            for s in range(LOAD, NCH):
                step(0, s)
            for i in range(1, min(AHEAD, B)):
                for s in range(NCH):
                    step(i, s)
            if B - 1 > AHEAD:
                with eng.Fori(AHEAD, B - 1) as i:
                    for s in range(NCH):
                        step(i, s)
            for i in range(max(min(AHEAD, B), B - 1), B + AHEAD):
                for s in range(NCH):
                    step(i, s)

        @block.sync
        def _(sp):
            loads = [(ident[:], ident_d), (mean_w[:], mean_d),
                     (dw_sb[:], dw_w.rearrange("(h p) t -> p h t", p=P)), (dwb_sb[:], dw_b),
                     (om_sb[:], om_w.rearrange("(h p) o -> p h o", p=P)),
                     (vp_sb[:], vp_w.rearrange("(h p) o -> p h o", p=P)),
                     (omb_bc[:], om_b.partition_broadcast(P)), (vpb_bc[:], vp_b.partition_broadcast(P))]
            for dst, src in loads:
                sp.dma_start(dst, src).then_inc(const_in, 16)
            xn_rows = xn.rearrange("n c w -> n (c w)").rearrange("n (l c) -> n l c", c=C)

            def columns(ap, n, c):
                return ap[n, :, N * c:N * (c + 1)].rearrange("(h p) w -> p h w", p=P)

            def step(i, s):
                for n, c, q in stage(i, s, VALUE):
                    sp.wait_ge(norm_done, q + 1)
                    sp.dma_start(columns(xn, n, c), X[:, c % 2]).then_inc(xn_st[c % 2], 16)
                for n, c, q in stage(i, s, LOAD):
                    if not isinstance(q, int) or q >= 2:
                        sp.wait_ge(v_mm, q - 1)
                        sp.sem_inc(passed, 1)
                        sp.wait_ge(xn_st[c % 2], n * (8 * NCH) + 16 * (c // 2))
                    sp.dma_start(X[:, c % 2], columns(x, n, c)).then_inc(x_in[c % 2], 16)
                for n, c, q in stage(i, s, NCH):
                    if c == 0:
                        for k in range(2):
                            sp.wait_ge(xn_st[k], n * (8 * NCH) + 8 * NCH)
                            sp.sem_inc(passed, 1)
                    if not isinstance(q, int) or q >= 2:
                        sp.wait_ge(tk_turned, q - 1)
                    sp.dma_start(TK[:, c % 2], xn_rows[n, N * c:N * (c + 1)].rearrange("(t p) c -> p t c", p=P)) \
                        .then_inc(tk_in[c % 2], 16)
                for n, c, q in stage(i, s, VALUE):
                    sp.wait_ge(v_ready, q + 1)
                    for r in range(2):
                        y = HALO + RC * c + r
                        sp.dma_start(
                            v_pad[n, y:y + 2 * NT - 1:2, HALO:HALO + W, :].rearrange("t w c -> w t c"),
                            VS[W * r:W * (r + 1), c % 2]).then_inc(v_st[c % 2], 16)
                for n, c, q in stage(i, s, OFFSETS):
                    sp.wait_ge(om_ready, q + 1)
                    sp.dma_start(om_raw[n, NT * c:NT * (c + 1)].rearrange("t p o -> p t o"), OMS[:]) \
                        .then_inc(om_st, 16)
                for n, c, q in stage(i, s, WEIGHTS):
                    sp.wait_ge(ks_ready, q + 1)
                    sp.dma_start(taps_t[n, :, :, N * c:N * (c + 1)].rearrange("h p w -> p h w"), KS[:]) \
                        .then_inc(ks_st, 16)

            stream(sp, step)
            for k in range(2):
                sp.wait_ge(v_st[k], 16 * B * NCH)
            sp.wait_ge(om_st, 16 * B * NCH)
            sp.wait_ge(ks_st, 16 * B * NCH)

        @block.scalar
        def _(act):
            act.wait_ge(zeroed, 6)
            fills = routed_x.shape[0] * C // (B * P * ZB)
            assert fills * B * P * ZB == routed_x.shape[0] * C and 3 + fills <= NCH
            xz = routed_x.rearrange("(b f q) c -> b f (q c)", b=B, f=fills).rearrange(
                "b f (p z) -> b f p z", p=P)
            vflat = v_pad.rearrange("n y w c -> n (y w c)")
            side = WP * C
            top = HALO * side + HALO * C
            below = (VR - HALO - H) * side + HALO * C

            def fill(n, c):
                if c < 2:
                    at, size = ((0, top), (VR * side - below, below))[c]
                    act.dma_start(vflat[n, at:at + size].rearrange("(p z) -> p z", p=P), zero[:, :size // P]) \
                        .then_inc(fill_st, 16)
                elif c == 2:
                    sides = vflat[n, 3 * side - HALO * C:3 * side - HALO * C + (H - 1) * side].rearrange(
                        "(y z) -> y z", z=side)[:, :2 * HALO * C]
                    act.dma_start(sides, zero[:H - 1, :2 * HALO * C]).then_inc(fill_st, 16)
                elif c < 3 + fills:
                    act.dma_start(xz[n, c - 3], zero[:]).then_inc(fill_st, 16)

            def step(i, s):
                for n, c, q in stage(i, s, WEIGHTS):
                    act.wait_ge(tr_mm, q)
                    nc.scalar.activation(K[:].rearrange("p t u -> p (t u)"), zero[:, :TG * TAPP], ACT.Copy) \
                        .then_inc(k_clr, 1)
                for n, c, q in stage(i, s, NORM):
                    act.wait_ge(sub_done, q + 1)
                    act.wait_ge(var_done, q)
                    nc.scalar.activation(SQ[:], X[:, c % 2], ACT.Square).then_inc(sq_done, 1)
                for n, c, q in stage(i, s, VALUE):
                    act.wait_ge(v_mm, q + 1)
                    act.wait_ge(v_st[c % 2], n * (16 * NCH) + 32 * (c // 2))
                    nc.scalar.activation(VS[:, c % 2], psVal[:], ACT.Copy).then_inc(v_raw, 1)
                for n, c, q in stage(i, s, NORM):
                    act.wait_ge(var_done, q + 1)
                    act.wait_ge(rstd_done, q)
                    nc.scalar.activation(STD[:], psV, ACT.Sqrt, bias=eps[:]).then_inc(std_done, 1)
                for n, c, q in stage(i, s, TURN):
                    act.wait_ge(tk_turned, q + 1)
                    if not isinstance(n, int) or n > 0:
                        act.wait_ge(dw_step, (n - 1) * (18 * NCH) + 18 * min(c + 2, NCH))
                    for h in range(KC):
                        last = nc.scalar.activation(XL[:, h, 1 + RC * c:1 + RC * (c + 1), 1:1 + W],
                                                    psX[:, h].rearrange("p (y w) -> p y w", w=W), ACT.Copy)
                    last.then_inc(xl_done, 1)
                for n, c, q in stage(i, s, VALUE):
                    fill(n, c)
                for n, c, q in stage(i, s, OFFSETS):
                    act.wait_ge(om_mm, q + 1)
                    act.wait_ge(om_st, q * 16)
                    act.wait_ge(mtx_done, q)
                    nc.scalar.activation(OMS[:].rearrange("p (b t) o -> p b (t o)", b=2), psO[:, :, :2 * OM],
                                         ACT.Copy).then_inc(om_evac, 1)
                for n, c, q in stage(i, s, WEIGHTS):
                    act.wait_ge(tr_mm, q + 1)
                    act.wait_ge(ks_st, q * 16)
                    nc.scalar.activation(KS[:], psK[:], ACT.Copy).then_inc(ks_ready, 1)
                for n, c, q in stage(i, s, OFFSETS):
                    act.wait_ge(om_ready, q + 1)
                    act.wait_ge(rm_done, q * 3)
                    off = OMS[:].rearrange("p t (g o) -> p (t g) o", g=G)[:, :, :2 * PT]
                    nc.scalar.activation(TENT[:, 1], off, ACT.Abs).then_inc(tent_step, 1)
                    nc.scalar.activation(TENT[:, 0], off, ACT.Relu, scale=-1.0)
                    nc.scalar.activation(TENT[:, 2], off, ACT.Relu)
                    act.wait_ge(tent_step, q + 1)
                    nc.scalar.activation(TENT[:, 1], TENT[:, 1], ACT.Identity, scale=-1.0, bias=1.0) \
                        .then_inc(tent_done, 1)

            stream(act, step)
            act.wait_ge(fill_st, 16 * B * (3 + fills))

        @block.gpsimd
        def _(pool):
            nc.gpsimd.memset(zero[:], 0.0).then_inc(zeroed, 1)
            nc.gpsimd.memset(XL[:], 0.0).then_inc(zeroed, 1)
            nc.gpsimd.memset(room[:], 1.0).then_inc(zeroed, 1)
            nc.gpsimd.memset(eps[:], 1e-6).then_inc(zeroed, 1)
            nc.gpsimd.memset(ones[:], 1.0).then_inc(zeroed, 1)
            nc.gpsimd.memset(K[:], 0.0).then_inc(zeroed, 1)
            pool.wait_ge(const_in, 16 * 8)
            pool.wait_ge(zeroed, 6)

            def step(i, s):
                def products(k):
                    mtx = MTX[:, :, k, :].unsqueeze(2).broadcast_to([P, TG, 3, PT])
                    ty = TENT[:, :, :, 1::2].rearrange("p j t q -> p t j q")
                    nc.gpsimd.tensor_tensor(RM[:, k], mtx, ty, ALU.mult).then_inc(rm_done, 1)

                for n, c, q in stage(i, s, VALUE):
                    pool.wait_ge(v_raw, q + 1)
                    v = VS[:, c % 2]
                    nc.gpsimd.tensor_tensor(v, v, vpb_bc[:].unsqueeze(1).broadcast_to([P, NT, C]), ALU.add) \
                        .then_inc(v_ready, 1)
                for n, c, q in stage(i, s, WEIGHTS):
                    pool.wait_ge(mtx_done, q + 1)
                    pool.wait_ge(k_add, q * 9)
                    products(0)
                for n, c, q in stage(i, s, NORM):
                    pool.wait_ge(rstd_done, q + 1)
                    pool.wait_ge(spread_mm, q)
                    nc.gpsimd.tensor_tensor(RDIAG[:], ident[:].unsqueeze(1).broadcast_to([P, NT, P]),
                                            RSTD[:].unsqueeze(2).broadcast_to([P, NT, P]), ALU.mult) \
                        .then_inc(diag_done, 1)
                for n, c, q in stage(i, s, WEIGHTS):
                    products(1)
                    products(2)
                for n, c, q in stage(i, s, OFFSETS):
                    pool.wait_ge(om_evac, q + 1)
                    nc.gpsimd.tensor_tensor(OMS[:], OMS[:], omb_bc[:].unsqueeze(1).broadcast_to([P, NT, OM]),
                                            ALU.add).then_inc(om_ready, 1)

            stream(pool, step)

        @block.tensor
        def _(pe):
            pe.wait_ge(const_in, 16 * 8)
            pe.wait_ge(zeroed, 6)

            def step(i, s):
                for n, c, q in stage(i, s, VALUE):
                    pe.wait_ge(norm_done, q + 1)
                    pe.wait_ge(v_raw, q)
                    for _, _, r in stage(i, s - 1, TURN):
                        pe.wait_ge(xl_done, r + 1)
                    for t in range(NT):
                        for h in range(KC):
                            last = nc.tensor.matmul(psVal[:, t], X[:, c % 2, h, P * t:P * (t + 1)], vp_sb[:, h],
                                                    start=(h == 0), stop=(h == KC - 1))
                    last.then_inc(v_mm, 1)
                for n, c, q in stage(i, s, NORM):
                    pe.wait_ge(sq_done, q + 1)
                    pe.wait_ge(norm_done, q)
                    for t in range(NT):
                        for h in range(KC):
                            last = nc.tensor.matmul(psV[:, t:t + 1], SQ[:, h, P * t:P * (t + 1)], mean_w[:, 0:1],
                                                    start=(h == 0), stop=(h == KC - 1))
                    last.then_inc(var_done, 1)
                for n, c, q in stage(i, s, TURN):
                    pe.wait_ge(tk_in[c % 2], n * (8 * NCH) + 16 * (c // 2) + 16)
                    pe.wait_ge(xl_done, q)
                    for _, _, r in stage(i, s, VALUE):
                        pe.wait_ge(v_raw, r + 1)
                    for h in range(KC):
                        for t in range(NT):
                            last = nc.tensor.transpose(psX[:, h, P * t:P * (t + 1)],
                                                       TK[:, c % 2, t, P * h:P * (h + 1)], ident[:])
                    last.then_inc(tk_turned, 1)
                for n, c, q in stage(i, s, NORM):
                    pe.wait_ge(diag_done, q + 1)
                    nc.tensor.matmul(psR[:], ones[:], RDIAG[:].rearrange("p t q -> p (t q)"), start=True, stop=True) \
                        .then_inc(spread_mm, 1)
                for n, c, q in stage(i, s, LOAD):
                    pe.wait_ge(x_in[c % 2], n * (8 * NCH) + 16 * (c // 2) + 16)
                    pe.wait_ge(sub_done, q)
                    for h in range(KC):
                        last = nc.tensor.matmul(psM[:], mean_w[:], X[:, c % 2, h], start=(h == 0), stop=(h == KC - 1))
                    last.then_inc(mean_done, 1)
                for n, c, q in stage(i, s, OFFSETS):
                    pe.wait_ge(dw_step, q * 18 + 18)
                    pe.wait_ge(om_evac, q)
                    for t in range(NT):
                        for h in range(KC):
                            last = nc.tensor.matmul(psO[:, t // 2, OM * (t % 2):OM * (t % 2 + 1)],
                                                    F[:, h, P * t:P * (t + 1)], om_sb[:, h],
                                                    start=(h == 0), stop=(h == KC - 1))
                    last.then_inc(om_mm, 1)
                for n, c, q in stage(i, s, WEIGHTS):
                    pe.wait_ge(k_add, q * 9 + 9)
                    pe.wait_ge(ks_ready, q)
                    for t in range(NT):
                        for h in range(2):
                            last = nc.tensor.transpose(
                                psK[:, h, P * t:P * (t + 1)],
                                K[:, G * t + 4 * h:G * t + 4 * h + 4].rearrange("p g u -> p (g u)"), ident[:])
                    last.then_inc(tr_mm, 1)

            stream(pe, step)

        @block.vector
        def _(dve):
            dve.wait_ge(const_in, 16 * 8)
            dve.wait_ge(zeroed, 6)

            def step(i, s):
                def convolve(c, q, taps):
                    for t in taps:
                        for h in range(KC):
                            src = XL[:, h, RC * c + t // 3:RC * c + t // 3 + RC, t % 3:t % 3 + W]
                            acc = F[:, h].rearrange("p (y w) -> p y w", w=W)
                            if t == 0:
                                ins = nc.vector.tensor_scalar(acc, src, dw_sb[:, h, t:t + 1],
                                                              dwb_sb[:, h:h + 1], ALU.mult, ALU.add)
                            else:
                                dve.wait_ge(dw_step, q * 18 + 2 * t + h - 1)
                                ins = nc.vector.scalar_tensor_tensor(acc, src, dw_sb[:, h, t:t + 1], acc,
                                                                     ALU.mult, ALU.add)
                            ins.then_inc(dw_step, 1)

                for n, c, q in stage(i, s, NORM):
                    dve.wait_ge(x_in[c % 2], n * (8 * NCH) + 16 * (c // 2) + 16)
                    dve.wait_ge(mean_done, q + 1)
                    xs = X[:, c % 2]
                    nc.vector.tensor_tensor(xs, xs, psM[:].unsqueeze(1).broadcast_to([P, KC, N]), ALU.subtract) \
                        .then_inc(sub_done, 1)
                for n, c, q in stage(i, s, OFFSETS):
                    dve.wait_ge(xl_done, n * NCH + min(c + 2, NCH))
                    dve.wait_ge(om_mm, q)
                    convolve(c, q, range(0, 5))
                for n, c, q in stage(i, s, WEIGHTS):
                    dve.wait_ge(tent_done, q + 1)
                    dve.wait_ge(rm_done, q * 3)
                    mask = OMS[:].rearrange("p t (g o) -> p (t g) o", g=G)[:, :, 2 * PT:3 * PT] \
                        .unsqueeze(2).broadcast_to([P, TG, 3, PT])
                    tx = TENT[:, :, :, 0::2].rearrange("p i t q -> p t i q")
                    nc.vector.tensor_tensor(MTX[:], mask, tx, ALU.mult)
                    nc.vector.tensor_reduce(room[:, 1:2], TENT[:, 1], AX.XY, ALU.min).then_inc(mtx_done, 1)
                    dve.wait_ge(mtx_done, q + 1)
                    nc.vector.tensor_tensor(room[:, 0:1], room[:, 0:1], room[:, 1:2], ALU.min).then_inc(red_done, 1)
                for n, c, q in stage(i, s, NORM):
                    dve.wait_ge(std_done, q + 1)
                    dve.wait_ge(diag_done, q)
                    nc.vector.reciprocal(RSTD[:], STD[:]).then_inc(rstd_done, 1)
                for n, c, q in stage(i, s, OFFSETS):
                    convolve(c, q, range(5, 9))
                for n, c, q in stage(i, s, NORM):
                    dve.wait_ge(spread_mm, q + 1)
                    xs = X[:, c % 2]
                    nc.vector.tensor_tensor(xs, xs, psR[:].unsqueeze(1).broadcast_to([P, KC, N]), ALU.mult) \
                        .then_inc(norm_done, 1)
                for n, c, q in stage(i, s, WEIGHTS):
                    dve.wait_ge(k_clr, q + 1)
                    for i_ in range(3):
                        dve.wait_ge(rm_done, q * 3 + i_ + 1)
                        for k in range(3):
                            if i_ or k:
                                dve.wait_ge(k_add, q * 9 + 3 * i_ + k)
                            at = 5 * k + i_
                            kk = K[:, :, at:at + 15].rearrange("p t (v u) -> p t u v", u=5)[:, :, 0:3]
                            nc.vector.tensor_tensor(
                                kk, kk, RM[:, i_, :, k].rearrange("p t (a b) -> p t a b", a=3),
                                ALU.add).then_inc(k_add, 1)

            stream(dve, step)

def deform(nc, x, op_w, op_b, select_d, v_pad, taps_t, x1):
    B, C, HW = x.shape
    W = 64
    H = HW // W
    KC = C // P
    N = 512
    NCH = HW // N
    NBX = W // BW
    NBY = -(-H // BH)
    NB = NBX * NBY
    CG = C // G
    GH = G // KC
    APOS = 4
    AB = NPOS // APOS
    LAST = H - BH * (NBY - 1)
    SELW = select_d.shape[1]
    with ExitStack() as ctx:
        def sb(name, shape):
            return ctx.enter_context(nc.sbuf_tensor(name, shape, F32))

        def ps(name, shape):
            return ctx.enter_context(nc.psum_tensor(name, shape, F32))

        def sem(name):
            return ctx.enter_context(nc.semaphore(name))

        V = sb("V", [Q, KC, NB, P])
        KT = sb("KT", [P, KC, H, W])
        A = sb("A", [Q, 2, NB, NPOS])
        D = sb("D", [P, KC, H, W])
        XR = sb("XR", [P, 2, KC, N])
        op_sb = sb("op_sb", [P, KC, C])
        opb_sb = sb("opb_sb", [P, KC])
        SEL = sb("SEL", [P, SELW])
        psA = ps("psA", [P, 4, 512])
        psD = ps("psD", [P, 2, 512])
        psP = ps("psP", [P, KC, N])

        w_in, passed = sem("w_in"), sem("p2_passed")
        v_in = [sem(f"v_in{i}") for i in range(KC)]
        kt_in = [sem(f"kt_in{i}") for i in range(KC)]
        a_mm, d_mm, p_mm = sem("a_mm"), sem("d_mm"), sem("p_mm")
        a_out = [sem("a_out_act"), sem("a_out_dve")]
        d_out = [sem("d_out_act"), sem("d_out_dve")]
        res_done = sem("res_done")
        xr_in = [sem(f"xr_in{i}") for i in range(2)]
        x1_st = [sem(f"x1_st{i}") for i in range(2)]
        block = ctx.enter_context(nc.Block())

        APG = AB * G
        DPG = NBY * G

        @block.sync
        def _(sp):
            sp.dma_start(SEL[:], select_d).then_inc(w_in, 16)
            sp.dma_start(op_sb[:], op_w.rearrange("(h p) o -> p h o", p=P)).then_inc(w_in, 16)
            sp.dma_start(opb_sb[:], op_b).then_inc(w_in, 16)

            def load_taps(n, h):
                sp.dma_start(KT[:, h].rearrange("p y w -> p (y w)"), taps_t[n, h]).then_inc(kt_in[h], 16)

            def load_values(n, h):
                for bx in range(NBX):
                    for r in range(RH):
                        src = v_pad[n, r:r + BH * (NBY - 1) + 1:BH, BW * bx:BW * bx + RW, P * h:P * (h + 1)]
                        sp.dma_start(V[RW * r:RW * (r + 1), h, bx::NBX], src.rearrange("a w c -> w a c")) \
                            .then_inc(v_in[h], 16)

            for h in range(KC):
                load_taps(0, h)
                load_values(0, h)
            if B > 1:
                with sp.Fori(1, B) as n:
                    for h in range(KC):
                        sp.wait_ge(a_mm, (n - 1) * APG + APG // 2 * (h + 1))
                        load_taps(n, h)
                        sp.wait_ge(d_mm, (n - 1) * DPG + DPG // 2 * (h + 1))
                        load_values(n, h)

        @block.gpsimd
        def _(pool):
            with pool.Fori(0, B) as n:
                def load(c):
                    pool.wait_ge(x1_st[c % 2], n * (8 * NCH) + 16 * (c // 2))
                    pool.sem_inc(passed, 1)
                    pool.dma_start(XR[:, c % 2], x[n, :, N * c:N * (c + 1)].rearrange("(h p) w -> p h w", p=P)) \
                        .then_inc(xr_in[c % 2], 16)

                load(0)
                for c in range(NCH):
                    if c + 1 < NCH:
                        load(c + 1)
                    pool.wait_ge(res_done, n * (KC * NCH) + KC * (c + 1))
                    pool.sem_inc(passed, 1)
                    pool.dma_start(x1[n, :, N * c:N * (c + 1)].rearrange("(h p) w -> p h w", p=P), XR[:, c % 2]) \
                        .then_inc(x1_st[c % 2], 16)
            for s in range(2):
                pool.wait_ge(x1_st[s], 8 * NCH * B)

        def copy_matrices(eng, who, n, g, b):
            s = g * AB + b
            eng.wait_ge(a_mm, n * APG + s + 1)
            eng.wait_ge(d_mm, n * DPG + NBY * max(g - 1, 0))
            py = b * APOS // BW
            nb = NB if py < LAST else NB - NBX
            at = b * APOS
            dst = A[:, g % 2, :nb, at:at + APOS].rearrange("q k a -> q a k")
            src = psA[:Q, b % 4, :APOS * nb].rearrange("q (a k) -> q a k", k=nb)
            if who:
                nc.vector.tensor_copy(dst, src).then_inc(a_out[1], 1)
            else:
                nc.scalar.activation(dst, src, ACT.Copy).then_inc(a_out[0], 1)

        def copy_outputs(eng, who, n, g, by):
            eng.wait_ge(d_mm, n * DPG + g * NBY + by + 1)
            if g == 0:
                eng.wait_ge(p_mm, n * (KC * NCH))
            rows = BH if by < NBY - 1 else LAST
            q0 = CG * (g % GH)
            dst = D[q0:q0 + CG, g // GH, BH * by:BH * by + rows].rearrange("q y (b x) -> q y b x", b=NBX)
            src = psD[q0:q0 + CG, (g * NBY + by) % 2, :NPOS * NBX].rearrange(
                "q (b y x) -> q y b x", b=NBX, y=BH)[:, :rows]
            if who:
                nc.vector.tensor_copy(dst, src).then_inc(d_out[1], 1)
            else:
                nc.scalar.activation(dst, src, ACT.Copy).then_inc(d_out[0], 1)

        def copies(eng, who, n):
            for b in range(AB):
                if b % 2 == who:
                    copy_matrices(eng, who, n, 0, b)
            for g in range(G):
                for k in range(AB):
                    if k < NBY and (g * NBY + k) % 2 == who:
                        copy_outputs(eng, who, n, g, k)
                    if g + 1 < G and k % 2 == who:
                        copy_matrices(eng, who, n, g + 1, k)

        @block.scalar
        def _(act):
            with act.Fori(0, B) as n:
                copies(act, 0, n)

        @block.vector
        def _(dve):
            dve.wait_ge(w_in, 48)
            with dve.Fori(0, B) as n:
                copies(dve, 1, n)
                for c in range(NCH):
                    dve.wait_ge(xr_in[c % 2], n * (8 * NCH) + 16 * (c // 2) + 16)
                    for m in range(KC):
                        dve.wait_ge(p_mm, n * (KC * NCH) + KC * c + m + 1)
                        nc.vector.scalar_tensor_tensor(XR[:, c % 2, m], psP[:, m], opb_sb[:, m:m + 1], XR[:, c % 2, m],
                                                       ALU.add, ALU.add).then_inc(res_done, 1)

        @block.tensor
        def _(pe):
            pe.wait_ge(w_in, 48)

            def matrices(n, g, b):
                s = g * AB + b
                if s < 4:
                    pe.wait_ge(a_out[b % 2], n * (APG // 2))
                else:
                    pe.wait_ge(a_out[b % 2], n * (APG // 2) + s // 2 - 1)
                if b == 0 and g % GH == 0:
                    pe.wait_ge(kt_in[g // GH], n * 16 + 16)
                k0 = TAPP * (g % GH)
                for a in range(APOS):
                    py, px = divmod(b * APOS + a, BW)
                    nb = NB if py < LAST else NB - NBX
                    at = (BH - 1) * RW + BW - 1 - (py * RW + px)
                    last = nc.tensor.matmul(psA[:Q, b % 4, a * nb:(a + 1) * nb], SEL[k0:k0 + TAPS, at:at + Q],
                                            KT[k0:k0 + TAPS, g // GH, py::BH, px::BW], start=True, stop=True)
                last.then_inc(a_mm, 1)

            def outputs(n, g, by):
                r = g * NBY + by
                if by == 0:
                    for w in range(2):
                        pe.wait_ge(a_out[w], n * (APG // 2) + AB // 2 * (g + 1))
                if g % GH == 0 and by == 0:
                    pe.wait_ge(v_in[g // GH], n * (16 * RH * NBX) + 16 * RH * NBX)
                if r < 2:
                    pe.wait_ge(d_out[r % 2], n * (DPG // 2))
                else:
                    pe.wait_ge(d_out[r % 2], n * (DPG // 2) + r // 2)
                c0 = CG * (g % GH)
                size = NPOS if by < NBY - 1 else LAST * BW
                for bx in range(NBX):
                    k = by * NBX + bx
                    last = nc.tensor.matmul(psD[c0:c0 + CG, r % 2, NPOS * bx:NPOS * bx + size],
                                            V[:, g // GH, k, c0:c0 + CG], A[:, g % 2, k, :size],
                                            start=True, stop=True)
                last.then_inc(d_mm, 1)

            with pe.Fori(0, B) as n:
                for b in range(AB):
                    matrices(n, 0, b)
                for g in range(G):
                    for k in range(AB):
                        if k < NBY:
                            outputs(n, g, k)
                        if g + 1 < G:
                            matrices(n, g + 1, k)
                for w in range(2):
                    pe.wait_ge(d_out[w], n * (DPG // 2) + DPG // 2)
                for c in range(NCH):
                    for m in range(KC):
                        pe.wait_ge(res_done, n * (KC * NCH) + max(KC * c + m - 1, 0))
                        for h in range(KC):
                            last = nc.tensor.matmul(
                                psP[:, m], op_sb[:, h, P * m:P * (m + 1)],
                                D[:, h, N // W * c:N // W * (c + 1)].rearrange("p y w -> p (y w)"),
                                start=(h == 0), stop=(h == KC - 1))
                        last.then_inc(p_mm, 1)

def resample(nc, x, op_w, op_b, ident_d, pix, geo, v_pad, om_raw, sampled, x1, flag):
    B, C, HW = x.shape
    W = 64
    KC = C // P
    TI = HW // P
    WP = v_pad.shape[2]
    CG = C // G
    NK = 4 * PT
    GO = 3 * PT
    TOP = float(W + 2)
    values = v_pad.rearrange("n y w (g c) -> (n y w g) c", g=G)
    om_t = om_raw.rearrange("n t p o -> (n t) p o")
    with ExitStack() as ctx:
        def sb(name, shape, dt=F32):
            return ctx.enter_context(nc.sbuf_tensor("f_" + name, shape, dt))

        def sem(name):
            return ctx.enter_context(nc.semaphore("f_" + name))

        ident = sb("ident", [P, P])
        opw = sb("opw", [P, KC, C])
        opb = sb("opb", [P, KC])
        PIX = sb("PIX", [P, 2, PT])
        OMG = sb("OMG", [P, GO])
        GEO = sb("GEO", [P, 2])
        XY = sb("XY", [P, 2, PT])
        II = sb("II", [P, 2, PT], I32)
        FL = sb("FL", [P, 2, PT])
        OV = sb("OV", [P, 2, PT])
        FR = sb("FR", [P, 2, 2, PT])
        ROW = sb("ROW", [P, PT])
        IDX = sb("IDX", [P, 4, PT], U32)
        WC = sb("WC", [P, 4, PT])
        GV = sb("GV", [P, NK, CG])
        ACC = sb("ACC", [P, CG])
        ST = sb("ST", [P, C])
        SC = sb("SC", [P, KC, P])
        XR = sb("XR", [P, KC, P])
        psT = ctx.enter_context(nc.psum_tensor("f_psT", [P, KC, P], F32))
        psP = ctx.enter_context(nc.psum_tensor("f_psP", [P, KC, P], F32))
        w_in, om_in, geo_in, idx_done, got, gathered, acc_done, acc_st, step, passed = (
            sem(n) for n in ("w_in", "om_in", "geo_in", "idx_done", "got", "gathered", "acc_done", "acc_st", "step", "passed"))
        t_in, turned, copied, mm, res, x1_st = (sem(n) for n in ("t_in", "turned", "copied", "mm", "res", "x1_st"))
        DS = 13
        block = ctx.enter_context(nc.Block())

        @block.sync
        def _(sp):
            for dst, src in ((ident[:], ident_d), (opw[:], op_w.rearrange("(h p) o -> p h o", p=P)),
                             (opb[:], op_b), (PIX[:], pix)):
                sp.dma_start(dst, src).then_inc(w_in, 16)
            sp.wait_ge(w_in, 64)
            fast = sp.value_load(flag, min_val=0, max_val=1)
            with sp.If(fast < 1):
                with sp.Fori(0, B * TI) as t:
                    with sp.Fori(0, G) as g:
                        k = t * G + g
                        sp.wait_ge(acc_done, k)
                        sp.dma_start(OMG[:], om_t[t, :, bass.ds(g * GO, GO)]).then_inc(om_in, 16)
                        sp.dma_start(GEO[:], geo[k].partition_broadcast(P)).then_inc(geo_in, 16)
                        sp.wait_ge(acc_done, k + 1)
                        sp.dma_start(sampled[t, :, bass.ds(g * CG, CG)], ACC[:]).then_inc(acc_st, 16)
                sp.wait_ge(acc_st, 16 * B * TI * G)
                with sp.Fori(0, B) as n:
                    with sp.Fori(0, TI) as t:
                        k = n * TI + t
                        sp.wait_ge(x1_st, k * 16)
                        sp.dma_start(ST[:], sampled[k]).then_inc(t_in, 16)
                        sp.dma_start(XR[:], x[n, :, bass.ds(t * P, P)].rearrange("(h p) w -> p h w", p=P)) \
                            .then_inc(t_in, 16)
                        sp.wait_ge(res, k * KC + KC)
                        sp.dma_start(x1[n, :, bass.ds(t * P, P)].rearrange("(h p) w -> p h w", p=P), XR[:]) \
                            .then_inc(x1_st, 16)
                sp.wait_ge(x1_st, 16 * B * TI)

        @block.gpsimd
        def _(pool):
            fast = pool.value_load(flag, min_val=0, max_val=1)
            with pool.If(fast < 1):
                with pool.Fori(0, B * TI) as t:
                    with pool.Fori(0, G) as g:
                        k = t * G + g
                        pool.wait_ge(idx_done, k + 1)
                        pool.sem_inc(passed, 1)
                        for j in range(NK):
                            pool.indirect_dma_start(
                                out=GV[:, j], out_offset=None, in_=values,
                                in_offset=bass.IndirectOffsetOnAxis(ap=IDX[:, j // PT, j % PT:j % PT + 1], axis=0)) \
                                .then_inc(got, 16)
                        pool.wait_ge(got, 16 * NK)
                        pool.sem_inc(gathered, 1)
                        pool.inc_swdge_sem([got], [16 * NK], mode="sub")

        @block.vector
        def _(dve):
            V = nc.vector
            dve.wait_ge(w_in, 64)
            fast = dve.value_load(flag, min_val=0, max_val=1)
            with dve.If(fast < 1):
                with dve.Fori(0, B * TI) as t:
                    with dve.Fori(0, G) as g:
                        k = t * G + g
                        done = [0]

                        def run(ins):
                            done[0] += 1
                            ins.then_inc(step, 1)
                            dve.wait_ge(step, k * DS + done[0])

                        dve.wait_ge(om_in, k * 16 + 16)
                        dve.wait_ge(geo_in, k * 16 + 16)
                        run(V.tensor_tensor(XY[:], OMG[:, :2 * PT].rearrange("p (q s) -> p s q", s=2), PIX[:], ALU.add))
                        run(V.tensor_scalar(XY[:, 1], XY[:, 1], GEO[:, 0:1], None, ALU.add))
                        run(V.tensor_scalar(XY[:], XY[:], 0.0, TOP, ALU.max, ALU.min))
                        run(V.tensor_copy(II[:], XY[:]))
                        run(V.tensor_copy(FL[:], II[:]))
                        run(V.tensor_tensor(OV[:], FL[:], XY[:], ALU.is_gt))
                        run(V.tensor_tensor(FL[:], FL[:], OV[:], ALU.subtract))
                        run(V.tensor_tensor(FR[:, 1], XY[:], FL[:], ALU.subtract))
                        run(V.tensor_scalar(FR[:, 0], FR[:, 1], -1.0, 1.0, ALU.mult, ALU.add))
                        run(V.scalar_tensor_tensor(ROW[:], FL[:, 1], float(WP), FL[:, 0], ALU.mult, ALU.add))
                        run(V.tensor_scalar(ROW[:], ROW[:], float(G), GEO[:, 1:2], ALU.mult, ALU.add))
                        for j in range(4):
                            V.tensor_scalar(IDX[:, j], ROW[:], float((j // 2 * WP + j % 2) * G), None, ALU.add)
                            ins = V.tensor_tensor(WC[:, j], FR[:, j // 2, 1], FR[:, j % 2, 0], ALU.mult)
                        run(ins)
                        V.tensor_tensor(WC[:], WC[:], OMG[:, 2 * PT:].unsqueeze(1).broadcast_to([P, 4, PT]), ALU.mult) \
                            .then_inc(idx_done, 1)
                        dve.wait_ge(idx_done, k + 1)
                        dve.wait_ge(gathered, k + 1)
                        run(V.tensor_tensor(GV[:], GV[:], WC[:].rearrange("p j q -> p (j q)").unsqueeze(2)
                                            .broadcast_to([P, NK, CG]), ALU.mult))
                        dve.wait_ge(acc_st, k * 16)
                        V.tensor_reduce(ACC[:], GV[:].rearrange("p k c -> p c k"), AX.X, ALU.add).then_inc(acc_done, 1)
                        assert done[0] == DS
                with dve.Fori(0, B * TI) as k:
                    dve.wait_ge(t_in, k * 32 + 32)
                    dve.wait_ge(mm, k + 1)
                    for m in range(KC):
                        V.scalar_tensor_tensor(XR[:, m], psP[:, m], opb[:, m:m + 1], XR[:, m], ALU.add, ALU.add) \
                            .then_inc(res, 1)

        @block.tensor
        def _(pe):
            pe.wait_ge(w_in, 64)
            fast = pe.value_load(flag, min_val=0, max_val=1)
            with pe.If(fast < 1):
                with pe.Fori(0, B * TI) as k:
                    pe.wait_ge(t_in, k * 32 + 32)
                    for h in range(KC):
                        last = nc.tensor.transpose(psT[:, h], ST[:, P * h:P * (h + 1)], ident[:])
                    last.then_inc(turned, 1)
                    pe.wait_ge(copied, k + 1)
                    for m in range(KC):
                        for h in range(KC):
                            last = nc.tensor.matmul(psP[:, m], opw[:, h, P * m:P * (m + 1)], SC[:, h],
                                                    start=(h == 0), stop=(h == KC - 1))
                    last.then_inc(mm, 1)

        @block.scalar
        def _(act):
            fast = act.value_load(flag, min_val=0, max_val=1)
            with act.If(fast < 1):
                with act.Fori(0, B * TI) as k:
                    act.wait_ge(turned, k + 1)
                    nc.scalar.activation(SC[:], psT[:], ACT.Copy).then_inc(copied, 1)

def route(nc, x1, gate_w, gate_b, cst, xe, CAP, NJ, tables, yrow, wgt):
    B, C, HW = x1.shape
    E = gate_b.shape[0]
    KC = C // P
    N = 512
    NT = N // P
    NCH = HW // N
    NK = B * NCH
    NTOK = NK * NT
    KMAX = CAP // TM
    with ExitStack() as ctx:
        def sb(name, shape, dt=F32):
            return ctx.enter_context(nc.sbuf_tensor(name, shape, dt))

        def ps(name, shape):
            return ctx.enter_context(nc.psum_tensor(name, shape, F32))

        def sem(name):
            return ctx.enter_context(nc.semaphore(name))

        ident = sb("p3_ident", [P, P])
        tri = sb("tri", [P, P])
        ones = sb("p3_ones", [P, P])
        gw = sb("gw", [P, KC, E])
        gb = sb("gb", [P, E])
        rank = sb("rank", [P, E])
        ebase = sb("ebase", [P, E])
        own = sb("own", [P, NTOK])
        steps = sb("steps", [P, KMAX])
        jota = sb("jota", [P, NJ])
        eps = sb("p3_eps", [P, 1])
        XC = sb("XC", [P, 2, KC, N])
        ST = sb("ST", [P, NT, 6])
        MV = sb("MV", [P, NT, 2])
        STD = sb("p3_STD", [P, NT])
        RS = sb("RS", [P, NT])
        NB = sb("NB", [P, NT])
        XT = sb("XT", [P, 2, NT, C])
        LT = sb("LT", [P, NT, E])
        MX = sb("MX", [P, NT])
        EQ = sb("EQ", [P, NT, E])
        FI = sb("FI", [P, NT])
        OH = sb("OH", [P, NT + 1, E])
        PO = sb("PO", [P, NT, E])
        PB = sb("PB", [P, NT, E])
        POS = sb("POS", [P, NT])
        ROW = sb("ROW", [P, NT])
        KEEP = sb("KEEP", [P, NT])
        IDX = sb("IDX", [P, 2, NT], U32)
        cnt = sb("cnt", [P, E])
        LALL = sb("LALL", [P, NTOK, E])
        OHALL = sb("OHALL", [P, NTOK, E])
        PALL = sb("PALL", [P, NTOK])
        small = sb("small", [P, 8, E])
        CMP = sb("CMP", [P, E, KMAX])
        JC = sb("JC", [P, NJ, E])
        JT = sb("JT", [P, 4, NJ])
        W1 = sb("W1", [P, NTOK])
        psT = ps("psT", [P, 2, 2, C])
        psG = ps("psG", [P, NT, E])
        psC = ps("psC", [P, NT + 1, E])

        c_in, zeroed = sem("c_in"), sem("p3_zeroed")
        x_in = [sem(f"p3_x_in{i}") for i in range(2)]
        t_mm, g_mm, c_mm = sem("t_mm"), sem("g_mm"), sem("c_mm")
        st_done, mv_done, std_done, rs_done, nb_done = (sem(n) for n in ("st_done", "mv_done", "p3_std", "rs_done", "nb_done"))
        xt_done, idx_done, pos_step, oh_done = sem("xt_done"), sem("idx_done"), sem("pos_step"), sem("oh_done")
        sc_st = [sem(f"sc_st{i}") for i in range(2)]
        passed = sem("p3_passed")
        gw_mm, gw_done = sem("gw_mm"), sem("gw_done")
        fin, fin_act = sem("fin"), sem("fin_act")
        block = ctx.enter_context(nc.Block())
        consts = [(ident, cst["ident"]), (tri, cst["tri"]), (own, cst["own"])]
        rows = [(gb, gate_b), (rank, cst["rank"]), (ebase, cst["ebase"]), (steps, cst["steps"]), (jota, cst["jota"])]
        NC_IN = 16 * (len(consts) + len(rows) + 1)
        DCH = 13

        @block.sync
        def _(sp):
            for dst, src in consts:
                sp.dma_start(dst[:], src).then_inc(c_in, 16)
            for dst, src in rows:
                sp.dma_start(dst[:], src.partition_broadcast(P)).then_inc(c_in, 16)
            sp.dma_start(gw[:], gate_w.rearrange("(h p) e -> p h e", p=P)).then_inc(c_in, 16)
            with sp.Fori(0, B) as n:
                for c in range(NCH):
                    sp.wait_ge(g_mm, n * NCH + max(c - 1, 0))
                    sp.dma_start(XC[:, c % 2], x1[n, :, N * c:N * (c + 1)].rearrange("(h p) w -> p h w", p=P)) \
                        .then_inc(x_in[c % 2], 16)

        @block.tensor
        def _(pe):
            pe.wait_ge(c_in, NC_IN)
            pe.wait_ge(zeroed, 4)
            for h in range(KC):
                last = nc.tensor.matmul(psC[:, 0], ones[:], gw[:, h], start=(h == 0), stop=(h == KC - 1))
            last.then_inc(gw_mm, 1)
            pe.wait_ge(gw_done, KC)
            with pe.Fori(0, B) as n:
                def turn(c):
                    pe.wait_ge(x_in[c % 2], n * (8 * NCH) + 16 * (c // 2) + 16)
                    pe.wait_ge(xt_done, n * (NT * NCH) + NT * c)
                    for t in range(NT):
                        for h in range(KC):
                            last = nc.tensor.transpose(psT[:, t // 2, t % 2, P * h:P * (h + 1)],
                                                       XC[:, c % 2, h, P * t:P * (t + 1)], ident[:])
                    last.then_inc(t_mm, 1)
                    pe.wait_ge(pos_step, n * (DCH * NCH) + DCH * c)
                    for t in range(NT):
                        for h in range(KC):
                            last = nc.tensor.matmul(psG[:, t], XC[:, c % 2, h, P * t:P * (t + 1)], gw[:, h],
                                                    start=(h == 0), stop=(h == KC - 1))
                    last.then_inc(g_mm, 1)

                for c in range(NCH):
                    turn(c)
                    pe.wait_ge(oh_done, n * NCH + c + 1)
                    nc.tensor.matmul(psC[:], tri[:], OH[:], start=True, stop=True)
                    for t in range(NT):
                        last = nc.tensor.matmul(psC[:, t + 1:], ones[:],
                                                OH[:, t:t + 1].broadcast_to([P, NT - t, E]),
                                                start=False, stop=True, skip_group_check=True)
                    last.then_inc(c_mm, 1)

        @block.scalar
        def _(act):
            act.wait_ge(zeroed, 4)
            with act.Fori(0, B) as n:
                for c in range(NCH):
                    act.wait_ge(mv_done, n * (NT * NCH) + NT * (c + 1))
                    nc.scalar.activation(STD[:], MV[:, :, 1], ACT.Sqrt, bias=eps[:]).then_inc(std_done, 1)
                    act.wait_ge(nb_done, n * NCH + c + 1)
                    act.wait_ge(sc_st[c % 2], n * (16 * NT * NCH // 2) + 16 * NT * (c // 2))
                    for t in range(NT):
                        nc.scalar.activation(XT[:, c % 2, t], psT[:, t // 2, t % 2], ACT.Identity,
                                             bias=NB[:, t:t + 1], scale=RS[:, t:t + 1]).then_inc(xt_done, 1)
            act.wait_ge(fin, 2)
            nc.scalar.activation(LALL[:], LALL[:], ACT.Exp).then_inc(fin_act, 1)

        @block.gpsimd
        def _(pool):
            nc.gpsimd.memset(ones[:], 1.0).then_inc(zeroed, 1)
            nc.gpsimd.memset(eps[:], 1e-5).then_inc(zeroed, 1)
            nc.gpsimd.memset(OH[:], 0.0).then_inc(zeroed, 1)
            nc.gpsimd.memset(cnt[:], 0.0).then_inc(zeroed, 1)
            with pool.Fori(0, B) as n:
                for c in range(NCH):
                    pool.wait_ge(xt_done, n * (NT * NCH) + NT * (c + 1))
                    pool.wait_ge(idx_done, n * NCH + c + 1)
                    pool.sem_inc(passed, 1)
                    for t in range(NT):
                        pool.indirect_dma_start(
                            out=xe, out_offset=bass.IndirectOffsetOnAxis(ap=IDX[:, c % 2, t:t + 1], axis=0),
                            in_=XT[:, c % 2, t], in_offset=None).then_inc(sc_st[c % 2], 16)
            for s in range(2):
                pool.wait_ge(sc_st[s], 16 * NT * NK // 2)

        @block.vector
        def _(dve):
            dve.wait_ge(c_in, NC_IN)
            dve.wait_ge(zeroed, 4)

            def over(ap, k):
                return ap.unsqueeze(1).broadcast_to([P, k, E])

            def per(ap, k):
                return ap.unsqueeze(2).broadcast_to([P, k, E])

            V = nc.vector
            dve.wait_ge(gw_mm, 1)
            for h in range(KC):
                V.scalar_tensor_tensor(gw[:, h], psC[:, 0], -1.0 / C, gw[:, h], ALU.mult, ALU.add).then_inc(gw_done, 1)
            with dve.Fori(0, B) as n:
                for c in range(NCH):
                    base = n * (DCH * NCH) + DCH * c
                    done = [0]

                    def step(ins):
                        done[0] += 1
                        ins.then_inc(pos_step, 1)
                        dve.wait_ge(pos_step, base + done[0])

                    dve.wait_ge(t_mm, n * NCH + c + 1)
                    for t in range(NT):
                        V.bn_stats(ST[:, t], psT[:, t // 2, t % 2]).then_inc(st_done, 1)
                    dve.wait_ge(st_done, n * (NT * NCH) + NT * (c + 1))
                    dve.sem_inc(passed, 1)
                    for t in range(NT):
                        V.bn_aggr(MV[:, t], ST[:, t]).then_inc(mv_done, 1)
                    dve.wait_ge(std_done, n * NCH + c + 1)
                    dve.wait_ge(xt_done, n * (NT * NCH) + NT * c)
                    V.reciprocal(RS[:], STD[:]).then_inc(rs_done, 1)
                    dve.wait_ge(rs_done, n * NCH + c + 1)
                    V.scalar_tensor_tensor(NB[:], MV[:, :, 0], -1.0, RS[:], ALU.mult, ALU.mult).then_inc(nb_done, 1)
                    dve.wait_ge(g_mm, n * NCH + c + 1)
                    tiles = bass.ds(n * (NT * NCH) + NT * c, NT)
                    step(V.tensor_tensor(LT[:], psG[:], per(RS[:], NT), ALU.mult))
                    step(V.tensor_tensor(LT[:], LT[:], over(gb[:], NT), ALU.add))
                    V.tensor_copy(LALL[:, tiles], LT[:])
                    step(V.tensor_reduce(MX[:], LT[:], AX.X, ALU.max))
                    step(V.tensor_tensor(EQ[:], LT[:], per(MX[:], NT), ALU.is_equal))
                    step(V.tensor_tensor(EQ[:], EQ[:], over(rank[:], NT), ALU.mult))
                    step(V.tensor_reduce(FI[:], EQ[:], AX.X, ALU.max))
                    V.tensor_tensor(OH[:, :NT], EQ[:], per(FI[:], NT), ALU.is_equal).then_inc(oh_done, 1)
                    dve.wait_ge(oh_done, n * NCH + c + 1)
                    V.tensor_copy(OHALL[:, tiles], OH[:, :NT])
                    step(V.tensor_tensor(PB[:], OH[:, :NT], over(ebase[:], NT), ALU.mult))
                    V.tensor_reduce(ROW[:], PB[:], AX.X, ALU.add)
                    dve.wait_ge(c_mm, n * NCH + c + 1)
                    step(V.tensor_tensor(PO[:], psC[:, :NT], over(cnt[:], NT), ALU.add))
                    step(V.tensor_tensor(PO[:], PO[:], OH[:, :NT], ALU.mult))
                    V.tensor_tensor(cnt[:], cnt[:], psC[:, NT], ALU.add)
                    step(V.tensor_reduce(POS[:], PO[:], AX.X, ALU.add))
                    V.tensor_copy(PALL[:, tiles], POS[:])
                    V.tensor_scalar(KEEP[:], POS[:], float(CAP), None, ALU.is_lt)
                    step(V.tensor_tensor(ROW[:], ROW[:], own[:, tiles], ALU.subtract))
                    step(V.tensor_tensor(ROW[:], ROW[:], POS[:], ALU.add))
                    step(V.tensor_tensor(ROW[:], ROW[:], KEEP[:], ALU.mult))
                    assert done[0] == DCH
                    dve.wait_ge(sc_st[c % 2], n * (16 * NT * NCH // 2) + 16 * NT * (c // 2))
                    V.tensor_tensor(IDX[:, c % 2], ROW[:], own[:, tiles], ALU.add).then_inc(idx_done, 1)

            dve.wait_ge(idx_done, NK)
            done = [0]

            def last(ins):
                done[0] += 1
                ins.then_inc(fin, 1)
                dve.wait_ge(fin, done[0])

            last(V.tensor_reduce(W1[:], LALL[:], AX.X, ALU.max))
            last(V.tensor_tensor(LALL[:], LALL[:], per(W1[:], NTOK), ALU.subtract))
            kept, ntile, first, end = small[:, 0], small[:, 1], small[:, 2], small[:, 3]
            last(V.tensor_scalar(kept, cnt[:], float(CAP), None, ALU.min))
            last(V.tensor_tensor(CMP[:], kept.unsqueeze(2).broadcast_to([P, E, KMAX]),
                                 steps[:].unsqueeze(1).broadcast_to([P, E, KMAX]), ALU.is_gt))
            last(V.tensor_reduce(ntile, CMP[:], AX.X, ALU.add))
            last(V.memset(first, 0.0))
            for e in range(1, E):
                last(V.tensor_tensor(first[:, e:e + 1], first[:, e - 1:e], ntile[:, e - 1:e], ALU.add))
            last(V.tensor_tensor(end, first, ntile, ALU.add))
            last(V.tensor_tensor(JC[:], jota[:].unsqueeze(2).broadcast_to([P, NJ, E]), over(end, NJ), ALU.is_ge))
            last(V.tensor_reduce(JT[:, 0], JC[:], AX.X, ALU.add))
            last(V.tensor_tensor(JC[:], JC[:], over(ntile, NJ), ALU.mult))
            last(V.tensor_reduce(JT[:, 1], JC[:], AX.X, ALU.add))
            last(V.tensor_tensor(JT[:, 1], jota[:], JT[:, 1], ALU.subtract))
            last(V.tensor_scalar(JT[:, 0], JT[:, 0], float(E - 1), None, ALU.min))
            last(V.tensor_scalar(JT[:, 1], JT[:, 1], float(KMAX - 1), float(TM), ALU.min, ALU.mult))
            last(V.scalar_tensor_tensor(JT[:, 2], JT[:, 0], float(CAP), JT[:, 1], ALU.mult, ALU.add))
            last(V.tensor_copy(tables[:, 0], JT[0:1, 0]))
            last(V.tensor_copy(tables[:, 1], JT[0:1, 2]))
            last(V.tensor_tensor(OHALL[:], OHALL[:], over(first, NTOK), ALU.mult))
            last(V.tensor_reduce(own[:], OHALL[:], AX.X, ALU.add))
            last(V.scalar_tensor_tensor(own[:], own[:], float(TM), PALL[:], ALU.mult, ALU.add))
            last(V.tensor_scalar(PALL[:], PALL[:], float(CAP), None, ALU.is_lt))
            last(V.tensor_tensor(yrow[:], own[:], PALL[:], ALU.mult))
            dve.wait_ge(fin_act, 1)
            last(V.tensor_reduce(W1[:], LALL[:], AX.X, ALU.add))
            last(V.reciprocal(W1[:], W1[:]))
            last(V.tensor_tensor(wgt[:], W1[:], PALL[:], ALU.mult))

def experts(nc, xe, w1, b1, w2, b2, ident_d, ye, CAP, NJ, tables, room):
    E, C, FF = w1.shape
    KC = C // P
    FC = FF // P
    NT = TM // P
    assert NJ % 2 == 0
    with ExitStack() as ctx:
        def sb(name, shape, dt=F32):
            return ctx.enter_context(nc.sbuf_tensor(name, shape, dt))

        def ps(name, shape):
            return ctx.enter_context(nc.psum_tensor(name, shape, F32))

        def sem(name):
            return ctx.enter_context(nc.semaphore(name))

        ident = sb("p4_ident", [P, P])
        W1 = sb("w1_sb", [P, 2, KC, FF])
        W2 = sb("w2_sb", [P, 2, FC, C])
        B1 = sb("b1_sb", [P, 2, FC])
        B2 = sb("b2_sb", [P, 2, C])
        XR = sb("p4_XR", [P, 2, NT, C])
        XT = sb("p4_XT", [P, 2, KC, TM])
        HM = sb("HM", [P, FC, TM])
        Y = sb("Y", [P, 2, NT, C])
        ABS = sb("ABS", [P, NT, C])
        ASUM = sb("ASUM", [P, 1])
        psT = ps("p4_psT", [P, KC, TM])
        psH = ps("psH", [P, 4, TM])
        psY = ps("psY", [P, NT, C])

        id_in, zeroed = sem("id_in"), sem("p4_zeroed")
        w_in = [sem(f"p4_w_in{i}") for i in range(2)]
        x_in = [sem(f"p4_x_in{i}") for i in range(2)]
        y_st = [sem(f"y_st{i}") for i in range(2)]
        t_mm, t_out, h_mm, h_out, y_mm, y_out, abs_out, sum_done = (
            sem(n) for n in ("p4_t_mm", "t_out", "h_mm", "h_out", "y_mm", "y_out", "abs_out", "sum_done"))
        block = ctx.enter_context(nc.Block())

        @block.sync
        def _(sp):
            sp.dma_start(ident[:], ident_d).then_inc(id_in, 16)
            with sp.Fori(0, NJ // 2) as i:
                for s in range(2):
                    expert = sp.value_load(tables[0:1, 0, bass.ds(2 * i + s, 1)], min_val=0, max_val=E - 1)
                    row = sp.value_load(tables[0:1, 1, bass.ds(2 * i + s, 1)], min_val=0, max_val=E * CAP - TM)
                    sp.wait_ge(t_mm, 2 * i + max(s - 1, 0))
                    sp.dma_start(XR[:, s], xe[bass.ds(row, TM), :].rearrange("(t p) c -> p t c", p=P)) \
                        .then_inc(x_in[s], 16)
                    sp.wait_ge(y_mm, 2 * i + max(s - 1, 0))
                    sp.wait_ge(y_out, 2 * i + max(s - 1, 0))
                    sp.dma_start(W1[:, s], w1[bass.ds(expert, 1)].rearrange("e (h p) f -> p (e h) f", p=P)) \
                        .then_inc(w_in[s], 16)
                    sp.dma_start(B1[:, s], b1[bass.ds(expert, 1)].rearrange("e p m -> p (e m)")).then_inc(w_in[s], 16)
                    sp.dma_start(W2[:, s], w2[bass.ds(expert, 1)].rearrange("e (m p) c -> p (e m) c", p=P)) \
                        .then_inc(w_in[s], 16)
                    sp.dma_start(B2[:, s], b2[bass.ds(expert, 1)].rearrange("e c -> (e c)").partition_broadcast(P)) \
                        .then_inc(w_in[s], 16)

        @block.gpsimd
        def _(pool):
            nc.gpsimd.memset(room[:, 0:1], 0.0).then_inc(zeroed, 1)
            with pool.Fori(0, NJ // 2) as i:
                for s in range(2):
                    pool.wait_ge(y_out, 2 * i + s + 1)
                    pool.dma_start(ye[bass.ds((2 * i + s) * TM, TM), :].rearrange("(t p) c -> p t c", p=P), Y[:, s]) \
                        .then_inc(y_st[s], 16)
            for s in range(2):
                pool.wait_ge(y_st[s], 8 * NJ)

        @block.tensor
        def _(pe):
            def turn(j, s, slot_tile):
                pe.wait_ge(x_in[s], slot_tile * 16 + 16)
                pe.wait_ge(t_out, j)
                for t in range(NT):
                    for h in range(KC):
                        last = nc.tensor.transpose(psT[:, h, P * t:P * (t + 1)],
                                                   XR[:, s, t, P * h:P * (h + 1)], ident[:])
                last.then_inc(t_mm, 1)

            def hidden(j, s, i):
                pe.wait_ge(t_out, j + 1)
                pe.wait_ge(w_in[s], i * 64 + 64)
                for m in range(FC):
                    if m >= 4:
                        pe.wait_ge(h_out, j * FC + m - 3)
                    else:
                        pe.wait_ge(h_out, j * FC)
                    for h in range(KC):
                        last = nc.tensor.matmul(psH[:, m % 4], W1[:, s, h, P * m:P * (m + 1)], XT[:, s, h],
                                                start=(h == 0), stop=(h == KC - 1))
                    last.then_inc(h_mm, 1)

            def output(j, s):
                pe.wait_ge(h_out, j * FC + FC)
                pe.wait_ge(y_out, j)
                for t in range(NT):
                    for m in range(FC):
                        last = nc.tensor.matmul(psY[:, t], HM[:, m, P * t:P * (t + 1)], W2[:, s, m],
                                                start=(m == 0), stop=(m == FC - 1))
                last.then_inc(y_mm, 1)

            pe.wait_ge(id_in, 16)
            turn(0, 0, 0)
            if NJ > 2:
                with pe.Fori(0, NJ // 2 - 1) as i:
                    hidden(2 * i, 0, i)
                    turn(2 * i + 1, 1, i)
                    output(2 * i, 0)
                    hidden(2 * i + 1, 1, i)
                    turn(2 * i + 2, 0, i + 1)
                    output(2 * i + 1, 1)
            i = NJ // 2 - 1
            hidden(2 * i, 0, i)
            turn(2 * i + 1, 1, i)
            output(2 * i, 0)
            hidden(2 * i + 1, 1, i)
            output(2 * i + 1, 1)

        @block.scalar
        def _(act):
            with act.Fori(0, NJ // 2) as i:
                for s in range(2):
                    j = 2 * i + s
                    act.wait_ge(w_in[s], i * 64 + 64)
                    act.wait_ge(y_mm, j)
                    for m in range(FC):
                        act.wait_ge(h_mm, j * FC + m + 1)
                        nc.scalar.activation(HM[:, m], psH[:, m % 4], ACT.Relu, bias=B1[:, s, m:m + 1]) \
                            .then_inc(h_out, 1)
                    act.wait_ge(y_out, j + 1)
                    act.wait_ge(sum_done, j)
                    nc.scalar.activation(ABS[:], Y[:, s], ACT.Abs, accum_out=ASUM[:]).then_inc(abs_out, 1)

        @block.vector
        def _(dve):
            dve.wait_ge(zeroed, 1)

            def turned(j, s):
                dve.wait_ge(t_mm, j + 1)
                nc.vector.tensor_copy(XT[:, s], psT[:]).then_inc(t_out, 1)

            def finish(j, s, i):
                dve.wait_ge(y_mm, j + 1)
                dve.wait_ge(y_st[s], i * 16)
                dve.wait_ge(abs_out, j)
                nc.vector.tensor_tensor(Y[:, s], psY[:], B2[:, s].unsqueeze(1).broadcast_to([P, NT, C]), ALU.add) \
                    .then_inc(y_out, 1)
                dve.wait_ge(abs_out, j + 1)
                nc.vector.tensor_tensor(room[:, 0:1], room[:, 0:1], ASUM[:], ALU.add).then_inc(sum_done, 1)

            turned(0, 0)
            if NJ > 2:
                with dve.Fori(0, NJ // 2 - 1) as i:
                    turned(2 * i + 1, 1)
                    finish(2 * i, 0, i)
                    turned(2 * i + 2, 0)
                    finish(2 * i + 1, 1, i)
            i = NJ // 2 - 1
            turned(2 * i + 1, 1)
            finish(2 * i, 0, i)
            finish(2 * i + 1, 1, i)


def all_partitions(nc, ident_d, values, flag, op, limit, compare, tag):
    with ExitStack() as ctx:
        ident = ctx.enter_context(nc.sbuf_tensor(f"{tag}_ident", [P, P], F32))
        red = ctx.enter_context(nc.sbuf_tensor(f"{tag}_red", [1, 2], F32))
        row = ctx.enter_context(nc.psum_tensor(f"{tag}_row", [P, P], F32))
        id_in, turned, step = (ctx.enter_context(nc.semaphore(f"{tag}_{n}")) for n in ("in", "turned", "step"))
        block = ctx.enter_context(nc.Block())

        @block.sync
        def _(sp):
            sp.dma_start(ident[:], ident_d).then_inc(id_in, 16)

        @block.tensor
        def _(pe):
            pe.wait_ge(id_in, 16)
            nc.tensor.transpose(row[0:1], values, ident[:]).then_inc(turned, 1)

        @block.vector
        def _(dve):
            dve.wait_ge(turned, 1)
            nc.vector.tensor_reduce(red[:, 0:1], row[0:1], AX.X, op).then_inc(step, 1)
            dve.wait_ge(step, 1)
            nc.vector.tensor_scalar(red[:, 1:2], red[:, 0:1], limit, None, compare).then_inc(step, 1)
            dve.wait_ge(step, 2)
            nc.vector.tensor_copy(flag, red[:, 1:2]).then_inc(step, 1)
            dve.wait_ge(step, 3)


def combine(nc, x1, ye, ident_d, out, yrow, wgt, flag, HUGE=3.4028234663852886e38):
    B, C, HW = x1.shape
    KC = C // P
    N = 512
    NT = N // P
    NCH = HW // N
    with ExitStack() as ctx:
        def sb(name, shape, dt=F32):
            return ctx.enter_context(nc.sbuf_tensor(name, shape, dt))

        def ps(name, shape):
            return ctx.enter_context(nc.psum_tensor(name, shape, F32))

        def sem(name):
            return ctx.enter_context(nc.semaphore(name))

        ident = sb("p5_ident", [P, P])
        YG = sb("YG", [P, 4, NT, C])
        XC = sb("p5_XC", [P, 4, KC, N])
        PART = sb("PART", [P, 2, NT, C])
        TEST = sb("TEST", [P, NT, C])
        IDX = sb("p5_IDX", [P, 4, NT], U32)
        WS = sb("WS", [P, 4, NT])
        psT = ps("p5_psT", [P, 2, KC, N])

        id_in, passed = sem("p5_id_in"), sem("p5_passed")
        g_in = [sem(f"g_in{i}") for i in range(4)]
        x_in = [sem(f"p5_x_in{i}") for i in range(4)]
        o_st = [sem(f"o_st{i}") for i in range(4)]
        pick, scaled, clean, t_mm, added, fix = (sem(n) for n in ("pick", "scaled", "clean", "p5_t_mm", "added", "fix"))
        block = ctx.enter_context(nc.Block())
        assert NCH % 4 == 0
        QS = NCH // 4

        @block.sync
        def _(sp):
            sp.dma_start(ident[:], ident_d).then_inc(id_in, 16)
            with sp.Fori(0, B) as n:
                for c in range(NCH):
                    sp.wait_ge(o_st[c % 4], n * (16 * QS) + 16 * (c // 4))
                    sp.dma_start(XC[:, c % 4], x1[n, :, N * c:N * (c + 1)].rearrange("(h p) w -> p h w", p=P)) \
                        .then_inc(x_in[c % 4], 16)

        @block.gpsimd
        def _(pool):
            with pool.Fori(0, B) as n:
                for c in range(NCH):
                    pool.wait_ge(pick, n * NCH + c + 1)
                    pool.wait_ge(t_mm, n * NCH + max(c - 3, 0))
                    pool.sem_inc(passed, 1)
                    for t in range(NT):
                        pool.indirect_dma_start(
                            out=YG[:, c % 4, t], out_offset=None, in_=ye,
                            in_offset=bass.IndirectOffsetOnAxis(ap=IDX[:, c % 4, t:t + 1], axis=0)) \
                            .then_inc(g_in[c % 4], 16)

        def store(act, n, c):
            act.wait_ge(added, n * NCH + c + 1)
            act.dma_start(out[n, :, N * c:N * (c + 1)].rearrange("(h p) w -> p h w", p=P), XC[:, c % 4]) \
                .then_inc(o_st[c % 4], 16)

        @block.scalar
        def _(act):
            with act.Fori(0, B) as n:
                for c in range(NCH):
                    act.wait_ge(g_in[c % 4], n * (16 * NT * QS) + 16 * NT * (c // 4 + 1))
                    for t in range(NT):
                        last = nc.scalar.activation(YG[:, c % 4, t], YG[:, c % 4, t], ACT.Copy,
                                                    scale=WS[:, c % 4, t:t + 1])
                    last.then_inc(scaled, 1)
                    if c >= 1:
                        store(act, n, c - 1)
                store(act, n, NCH - 1)
            for s in range(4):
                act.wait_ge(o_st[s], 16 * QS * B)

        @block.tensor
        def _(pe):
            pe.wait_ge(id_in, 16)
            with pe.Fori(0, B) as n:
                for c in range(NCH):
                    pe.wait_ge(clean, n * NCH + c + 1)
                    pe.wait_ge(added, n * NCH + max(c - 1, 0))
                    for h in range(KC):
                        for t in range(NT):
                            last = nc.tensor.transpose(psT[:, c % 2, h, P * t:P * (t + 1)],
                                                       YG[:, c % 4, t, P * h:P * (h + 1)], ident[:])
                    last.then_inc(t_mm, 1)

        @block.vector
        def _(dve):
            V = nc.vector
            finite = dve.value_load(flag, min_val=0, max_val=1)

            def choose(n, c):
                dve.wait_ge(scaled, n * NCH + max(c - 3, 0))
                tiles = bass.ds(n * (NT * NCH) + NT * c, NT)
                V.tensor_copy(WS[:, c % 4], wgt[:, tiles])
                V.tensor_copy(IDX[:, c % 4], yrow[:, tiles]).then_inc(pick, 1)

            with dve.Fori(0, B) as n:
                for c in range(3):
                    choose(n, c)
                for c in range(NCH):
                    if c + 3 < NCH:
                        choose(n, c + 3)
                    dve.wait_ge(scaled, n * NCH + c + 1)
                    dve.sem_inc(passed, 1)
                    with dve.If(finite < 1):
                        y = YG[:, c % 4]
                        done = [0]

                        def step(ins):
                            done[0] += 1
                            ins.then_inc(fix, 1)
                            dve.wait_ge(fix, n * (10 * NCH) + 10 * c + done[0])

                        for part, keep, cap, beyond, within in ((PART[:, 0], ALU.max, 1.0, ALU.is_gt, ALU.is_le),
                                                                (PART[:, 1], ALU.min, -1.0, ALU.is_lt, ALU.is_ge)):
                            clip = ALU.min if cap > 0 else ALU.max
                            step(V.tensor_scalar(part, y, 0.0, cap * HUGE, keep, clip))
                            step(V.tensor_scalar(TEST[:], y, 0.0, cap * HUGE, keep, within))
                            step(V.tensor_tensor(part, part, TEST[:], ALU.mult))
                            step(V.tensor_scalar(TEST[:], y, 0.0, cap * HUGE, keep, beyond))
                            step(V.scalar_tensor_tensor(part, TEST[:], cap * 1e4, part, ALU.mult, ALU.add))
                        V.tensor_tensor(y, PART[:, 0], PART[:, 1], ALU.add)
                    dve.drain().then_inc(clean, 1)
                    dve.wait_ge(x_in[c % 4], n * (16 * QS) + 16 * (c // 4) + 16)
                    dve.wait_ge(t_mm, n * NCH + c + 1)
                    V.tensor_tensor(XC[:, c % 4], XC[:, c % 4], psT[:, c % 2], ALU.add).then_inc(added, 1)


def metaformer_layer(nc, x, dw_w, dw_b, om_w, om_b, vp_w, vp_b, op_w, op_b, gate_w, gate_b, w1, b1, w2, b2,
                     cst, out):
    B, C, HW = x.shape
    W = 64
    H = HW // W
    T = B * HW
    E = w1.shape[0]
    CAP = -(-5 * T // (4 * E))
    NJ = T // TM + E
    OM = om_w.shape[1]
    rows = BH * -(-H // BH) + 2 * HALO
    assert CAP % TM == 0 and T % TM == 0

    def dram(name, shape):
        return nc.dram_tensor(name, shape, F32, kind="Internal").ap()

    v_pad = dram("v_pad", (B, rows, W + 2 * HALO, C))
    xn = dram("xn", (B, C, HW))
    om_raw = dram("om_raw", (B, HW // P, P, OM))
    taps_t = dram("taps_t", (B, C // P, P, HW))
    sampled = dram("sampled", (T // P, P, C))
    x1 = dram("x1", (B, C, HW))
    xe = dram("xe", (E * CAP + T, C))
    ye = dram("ye", (NJ * TM, C))
    with ExitStack() as ctx:
        def sb(name, shape, dt=F32):
            return ctx.enter_context(nc.sbuf_tensor(name, shape, dt))

        room = sb("room", [P, 2])
        near = sb("near", [1, 1], I32)
        finite = sb("finite", [1, 1], I32)
        tables = sb("tables", [1, 2, NJ], I32)
        yrow = sb("yrow", [P, T // P], U32)
        wgt = sb("wgt", [P, T // P])
        conv_features(nc, x, dw_w, dw_b, om_w, om_b, vp_w, vp_b, cst["ident"], cst["mean"],
                      xn, v_pad, om_raw, taps_t, xe[0:E * CAP], room)
        all_partitions(nc, cst["ident"], room[:, 0:1], near[:], ALU.min, 0.0, ALU.is_gt, "near")
        deform(nc, x, op_w, op_b, cst["select"], v_pad, taps_t, x1)
        resample(nc, x, op_w, op_b, cst["ident"], cst["pix"], cst["geo"], v_pad, om_raw, sampled, x1, near[:])
        route(nc, x1, gate_w, gate_b, cst, xe, CAP, NJ, tables, yrow, wgt)
        experts(nc, xe, w1, b1, w2, b2, cst["ident"], ye, CAP, NJ, tables, room)
        all_partitions(nc, cst["ident"], room[:, 0:1], finite[:], ALU.add, 3.4028234663852886e38, ALU.is_le, "fin")
        combine(nc, x1, ye, cst["ident"], out, yrow, wgt, finite[:])


def constants(np, B, H, W, C, E):
    T = B * H * W
    cap = -(-5 * T // (4 * E))
    p, q = np.arange(P), np.arange(PT)
    last = (BH - 1) * RW + BW - 1
    select = np.zeros((P, last + Q))
    for g in range(P // TAPP):
        for tap in range(TAPS):
            select[TAPP * g + tap, last + tap // 5 * RW + tap % 5] = 1
    pix = np.zeros((P, 2, PT))
    pix[:, 0] = (p % W)[:, None] + HALO - 1 + q // 3
    pix[:, 1] = (p // W)[:, None] + HALO - 1 + q % 3
    tile, g = np.arange(T // P)[:, None], np.arange(G)[None]
    rows = BH * -(-H // BH) + 2 * HALO
    per = H * W // P
    geo = np.stack([P // W * (tile % per) + 0 * g, tile // per * rows * (W + 2 * HALO) * G + g], -1)
    made = {
        "ident": np.eye(P), "mean": np.full((P, P), 1 / C), "select": select, "pix": pix,
        "geo": geo.reshape(-1, 2), "tri": np.triu(np.ones((P, P)), 1), "own": E * cap + np.arange(T // P)[None] * P + p[:, None],
        "rank": E - np.arange(E), "ebase": np.arange(E) * cap, "steps": np.arange(cap // TM) * TM,
        "jota": np.arange(T // TM + E),
    }
    return {k: v.astype(np.float32) for k, v in made.items()}


def kernel(**inputs):
    import numpy as _np
    import concourse.bacc as _bacc
    from concourse.bass_utils import run_bass_kernel_spmd as _run

    nc = _bacc.Bacc("TRN2", target_bir_lowering=False, num_devices=1)
    a = {k: _np.asarray(v) for k, v in inputs.items()}
    B, C, H, W = a["x"].shape
    E, _, FF = a["L0_ffn_w1"].shape
    given = {
        "x": a["x"].reshape(B, C, H * W),
        "dw_w": a["L0_conv_dw_w"].reshape(C, 9), "dw_b": a["L0_conv_dw_b"].reshape(C // P, P).T,
        "om_w": a["L0_conv_om_w"].T, "om_b": a["L0_conv_om_b"],
        "vp_w": a["L0_conv_vp_w"].T, "vp_b": a["L0_conv_vp_b"],
        "op_w": a["L0_conv_op_w"].T, "op_b": a["L0_conv_op_b"].reshape(C // P, P).T,
        "gate_w": a["L0_ffn_gate_w"], "gate_b": a["L0_ffn_gate_b"],
        "w1": a["L0_ffn_w1"], "b1": a["L0_ffn_b1"].reshape(E, FF // P, P).transpose(0, 2, 1),
        "w2": a["L0_ffn_w2"], "b2": a["L0_ffn_b2"],
    }
    tables = constants(_np, B, H, W, C, E)
    arrays = {f"in_{k}": _np.ascontiguousarray(v) for k, v in {**given, **tables}.items()}
    aps = {k: nc.dram_tensor(k, v.shape, F32, kind="ExternalInput").ap() for k, v in arrays.items()}
    out = nc.dram_tensor("out_0", (B, C, H * W), F32, kind="ExternalOutput").ap()
    metaformer_layer(nc, *[aps[f"in_{k}"] for k in given], {k: aps[f"in_{k}"] for k in tables}, out)
    r = _run(nc, [arrays], core_ids=[0])
    return r.results[0]["out_0"].reshape(B, C, H, W)
```

```python
from contextlib import ExitStack

import concourse.bass as bass
from concourse import mybir

ALU = mybir.AluOpType
ACT = mybir.ActivationFunctionType
AX = mybir.AxisListType
F32 = mybir.dt.float32
BF16 = mybir.dt.bfloat16
F32R = mybir.dt.float32r
I32 = mybir.dt.int32
U32 = mybir.dt.uint32

P = 128
TM = 512
G, PT = 8, 9
HALO = 2
BH, BW = 6, 8
RH, RW = BH + 2 * HALO, BW + 2 * HALO
Q = RH * RW
NPOS = BH * BW
TAPS = 25
TAPP = 32
PARTS = 3


def conv_features(nc, x, dw_w, dw_b, om_w, om_b, vp_w, vp_b, ident_d, mean_d,
                  xn, v_pad, om_raw, taps_t, routed_x, room, passed):
    B, C, HW = x.shape
    W = 64
    H = HW // W
    KC = C // P
    RC = 512 // W
    N = RC * W
    NCH = HW // N
    NT = N // P
    OM = om_w.shape[1]
    TG = NT * G
    WP = W + 2 * HALO
    VR = v_pad.shape[1]
    ZB = 2048
    with ExitStack() as ctx:
        def sb(name, shape, dt=F32):
            return ctx.enter_context(nc.sbuf_tensor(name, shape, dt))

        def ps(name, shape):
            return ctx.enter_context(nc.psum_tensor(name, shape, F32))

        def sem(name):
            return ctx.enter_context(nc.semaphore(name))

        ident = sb("p1_ident", [P, P])
        mean_w = sb("mean_w", [P, P])
        dw_sb = sb("dw_sb", [P, KC, 9])
        dwb_sb = sb("dwb_sb", [P, KC])
        om_sb = sb("om_sb", [P, KC, OM])
        vp_sb = sb("vp_sb", [P, KC, C])
        omb_bc = sb("omb_bc", [P, OM])
        vpb_bc = sb("vpb_bc", [P, C])
        X = sb("X", [P, 2, KC, N])
        SQ = sb("SQ", [P, KC, N])
        eps = sb("eps", [P, 1])
        minus = sb("minus", [P, 1])
        OVER = sb("OVER", [P, TG, 2 * PT])
        ones = sb("ones", [P, P])
        STD = sb("STD", [P, NT])
        RSTD = sb("RSTD", [P, NT])
        RDIAG = sb("RDIAG", [P, NT, P])
        XL = sb("XL", [P, KC, H + 2, W + 2])
        TK = sb("TK", [P, 2, NT, C])
        F = sb("F", [P, 2, KC, N])
        OMS = sb("OMS", [P, NT, OM])
        VS = sb("VS", [P, 2, NT, C])
        TENT = sb("TENT", [P, 3, TG, 2 * PT])
        MTX = sb("MTX", [P, TG, 3, PT])
        RM = sb("RM", [P, 3, TG, 3, PT])
        K = sb("K", [P, TG, TAPP])
        KS = sb("KS", [P, KC, N])
        KB = sb("KB", [P, 2, PARTS, KC, N], BF16)
        zero = sb("zero", [P, ZB])
        psM = ps("psM", [P, N])
        psR = ps("psR", [P, N])
        psVal = ps("psVal", [P, NT, C])
        psX = psVal[:].rearrange("p t c -> p (t c)").rearrange("p (h w) -> p h w", h=KC)
        psO = ps("psO", [P, 2, 512])
        psV = psR[:, :NT]
        psK = ps("psK", [P, 2, N])

        const_in = sem("const_in")
        zeroed = sem("zeroed")
        x_in = [sem(f"x_in{i}") for i in range(2)]
        mean_done, sub_done, sq_done, var_done = sem("mean_done"), sem("sub_done"), sem("sq_done"), sem("var_done")
        diag_done, spread_mm = sem("diag_done"), sem("spread_mm")
        xn_st = [sem(f"xn_st{i}") for i in range(2)]
        tk_in = [sem(f"tk_in{i}") for i in range(2)]
        tk_turned = sem("tk_turned")
        xl_done, std_done = sem("xl_done"), sem("std_done")
        rstd_done, norm_done, dw_step, om_mm = sem("rstd_done"), sem("norm_done"), sem("dw_step"), sem("om_mm")
        v_mm, v_raw, v_ready = sem("v_mm"), sem("v_raw"), sem("v_ready")
        v_st = [sem(f"v_st{i}") for i in range(2)]
        om_evac, om_ready, om_st, tent_done = sem("om_evac"), sem("om_ready"), sem("om_st"), sem("tent_done")
        tent_step = sem("tent_step")
        mtx_done, rm_done, k_clr, k_add, tr_mm = sem("mtx_done"), sem("rm_done"), sem("k_clr"), sem("k_add"), sem("tr_mm")
        ks_raw, ks_high, rest, mid_done, ks_ready = (
            sem(n) for n in ("ks_raw", "ks_high", "rest", "mid_done", "ks_ready"))
        ks_st = [sem(f"ks_st{i}") for i in range(2)]
        fill_st = sem("fill_st")
        block = ctx.enter_context(nc.Block())

        LOAD, NORM, VALUE, TURN = -2, -1, 0, NCH + 1
        OFFSETS, WEIGHTS, SUMS, SPLIT = NCH + 3, NCH + 4, NCH + 5, NCH + 6
        AHEAD = 2

        def stage(i, s, lag):
            d, c = divmod(s - lag, NCH)
            if isinstance(i, int) and not 0 <= i + d < B:
                return []
            return [(i + d, c, (i + d) * NCH + c)]

        def stream(eng, step):
            for s in range(LOAD, NCH):
                step(0, s)
            for i in range(1, min(AHEAD, B)):
                for s in range(NCH):
                    step(i, s)
            if B - 1 > AHEAD:
                with eng.Fori(AHEAD, B - 1) as i:
                    for s in range(NCH):
                        step(i, s)
            for i in range(max(min(AHEAD, B), B - 1), B + AHEAD):
                for s in range(NCH):
                    step(i, s)

        @block.sync
        def _(sp):
            loads = [(ident[:], ident_d), (mean_w[:], mean_d),
                     (dw_sb[:], dw_w.rearrange("(h p) t -> p h t", p=P)), (dwb_sb[:], dw_b),
                     (om_sb[:], om_w.rearrange("(h p) o -> p h o", p=P)),
                     (vp_sb[:], vp_w.rearrange("(h p) o -> p h o", p=P)),
                     (omb_bc[:], om_b.partition_broadcast(P)), (vpb_bc[:], vp_b.partition_broadcast(P))]
            for dst, src in loads:
                sp.dma_start(dst, src).then_inc(const_in, 16)
            xn_rows = xn.rearrange("n c w -> n (c w)").rearrange("n (l c) -> n l c", c=C)

            def columns(ap, n, c):
                return ap[n, :, N * c:N * (c + 1)].rearrange("(h p) w -> p h w", p=P)

            def step(i, s):
                for n, c, q in stage(i, s, VALUE):
                    sp.wait_ge(norm_done, q + 1)
                    sp.dma_start(columns(xn, n, c), X[:, c % 2]).then_inc(xn_st[c % 2], 16)
                for n, c, q in stage(i, s, LOAD):
                    if not isinstance(q, int) or q >= 2:
                        sp.wait_ge(v_mm, q - 1)
                        sp.sem_inc(passed, 1)
                        sp.wait_ge(xn_st[c % 2], n * (8 * NCH) + 16 * (c // 2))
                    sp.dma_start(X[:, c % 2], columns(x, n, c)).then_inc(x_in[c % 2], 16)
                for n, c, q in stage(i, s, NCH):
                    if c == 0:
                        for k in range(2):
                            sp.wait_ge(xn_st[k], n * (8 * NCH) + 8 * NCH)
                            sp.sem_inc(passed, 1)
                    if not isinstance(q, int) or q >= 2:
                        sp.wait_ge(tk_turned, q - 1)
                    sp.dma_start(TK[:, c % 2], xn_rows[n, N * c:N * (c + 1)].rearrange("(t p) c -> p t c", p=P)) \
                        .then_inc(tk_in[c % 2], 16)
                for n, c, q in stage(i, s, VALUE):
                    sp.wait_ge(v_ready, q + 1)
                    for r in range(2):
                        y = HALO + RC * c + r
                        sp.dma_start(
                            v_pad[n, y:y + 2 * NT - 1:2, HALO:HALO + W, :].rearrange("t w c -> w t c"),
                            VS[W * r:W * (r + 1), c % 2]).then_inc(v_st[c % 2], 16)
                for n, c, q in stage(i, s, OFFSETS):
                    sp.wait_ge(om_ready, q + 1)
                    sp.dma_start(om_raw[n, NT * c:NT * (c + 1)].rearrange("t p o -> p t o"), OMS[:]) \
                        .then_inc(om_st, 16)
                for n, c, q in stage(i, s, SPLIT):
                    sp.wait_ge(ks_ready, q + 1)
                    sp.dma_start(taps_t[n, :, :, N * c:N * (c + 1)].rearrange("r p w -> p r w"),
                                 KB[:, c % 2].rearrange("p r h w -> p (r h) w")).then_inc(ks_st[c % 2], 16)

            stream(sp, step)
            for k in range(2):
                sp.wait_ge(v_st[k], 16 * B * NCH)
                sp.wait_ge(ks_st[k], 8 * B * NCH)
            sp.wait_ge(om_st, 16 * B * NCH)

        @block.scalar
        def _(act):
            act.wait_ge(zeroed, 7)
            fills = routed_x.shape[0] * C // (B * P * ZB)
            assert fills * B * P * ZB == routed_x.shape[0] * C and 3 + fills <= NCH
            xz = routed_x.rearrange("(b f q) c -> b f (q c)", b=B, f=fills).rearrange(
                "b f (p z) -> b f p z", p=P)
            vflat = v_pad.rearrange("n y w c -> n (y w c)")
            side = WP * C
            top = HALO * side + HALO * C
            below = (VR - HALO - H) * side + HALO * C

            def fill(n, c):
                if c < 2:
                    at, size = ((0, top), (VR * side - below, below))[c]
                    act.dma_start(vflat[n, at:at + size].rearrange("(p z) -> p z", p=P), zero[:, :size // P]) \
                        .then_inc(fill_st, 16)
                elif c == 2:
                    sides = vflat[n, 3 * side - HALO * C:3 * side - HALO * C + (H - 1) * side].rearrange(
                        "(y z) -> y z", z=side)[:, :2 * HALO * C]
                    act.dma_start(sides, zero[:H - 1, :2 * HALO * C]).then_inc(fill_st, 16)
                elif c < 3 + fills:
                    act.dma_start(xz[n, c - 3], zero[:]).then_inc(fill_st, 16)

            def step(i, s):
                for n, c, q in stage(i, s, NORM):
                    act.wait_ge(sub_done, q + 1)
                    act.wait_ge(var_done, q)
                    nc.scalar.activation(SQ[:], X[:, c % 2], ACT.Square).then_inc(sq_done, 1)
                for n, c, q in stage(i, s, WEIGHTS):
                    act.wait_ge(om_ready, q + 1)
                    act.wait_ge(rm_done, q * 3)
                    off = OMS[:].rearrange("p t (g o) -> p (t g) o", g=G)[:, :, :2 * PT]
                    nc.scalar.activation(TENT[:, 1], off, ACT.Abs).then_inc(tent_step, 1)
                    nc.scalar.activation(TENT[:, 0], off, ACT.Relu, scale=-1.0)
                    nc.scalar.activation(TENT[:, 2], off, ACT.Relu)
                    act.wait_ge(tent_step, q + 1)
                    nc.scalar.activation(OVER[:], TENT[:, 1], ACT.Relu, bias=minus[:], accum_out=room[:, 1:2])
                    nc.scalar.activation(TENT[:, 1], TENT[:, 1], ACT.Identity, scale=-1.0, bias=1.0) \
                        .then_inc(tent_done, 1)
                for n, c, q in stage(i, s, SPLIT):
                    act.wait_ge(ks_raw, q + 1)
                    act.wait_ge(ks_st[c % 2], n * (8 * NCH) + 16 * (c // 2))
                    nc.scalar.activation(KB[:, c % 2, 0], KS[:], ACT.Copy).then_inc(ks_high, 1)
                for n, c, q in stage(i, s, VALUE):
                    act.wait_ge(v_mm, q + 1)
                    act.wait_ge(v_st[c % 2], n * (16 * NCH) + 32 * (c // 2))
                    nc.scalar.activation(VS[:, c % 2], psVal[:], ACT.Copy).then_inc(v_raw, 1)
                for n, c, q in stage(i, s, NORM):
                    act.wait_ge(var_done, q + 1)
                    act.wait_ge(rstd_done, q)
                    nc.scalar.activation(STD[:], psV, ACT.Sqrt, bias=eps[:]).then_inc(std_done, 1)
                for n, c, q in stage(i, s, SPLIT):
                    act.wait_ge(rest, q + 1)
                    nc.scalar.activation(KB[:, c % 2, 1], KS[:], ACT.Copy).then_inc(mid_done, 1)
                for n, c, q in stage(i, s, TURN):
                    act.wait_ge(tk_turned, q + 1)
                    if not isinstance(n, int) or n > 0:
                        act.wait_ge(dw_step, (n - 1) * (18 * NCH) + 18 * min(c + 2, NCH))
                    for h in range(KC):
                        last = nc.scalar.activation(XL[:, h, 1 + RC * c:1 + RC * (c + 1), 1:1 + W],
                                                    psX[:, h].rearrange("p (y w) -> p y w", w=W), ACT.Copy)
                    last.then_inc(xl_done, 1)
                for n, c, q in stage(i, s, WEIGHTS):
                    act.wait_ge(tr_mm, q)
                    nc.scalar.activation(K[:].rearrange("p t u -> p (t u)"), zero[:, :TG * TAPP], ACT.Copy) \
                        .then_inc(k_clr, 1)
                for n, c, q in stage(i, s, VALUE):
                    fill(n, c)
                for n, c, q in stage(i, s, OFFSETS):
                    act.wait_ge(om_mm, q + 1)
                    act.wait_ge(om_st, q * 16)
                    act.wait_ge(mtx_done, q)
                    nc.scalar.activation(OMS[:].rearrange("p (b t) o -> p b (t o)", b=2), psO[:, :, :2 * OM],
                                         ACT.Copy).then_inc(om_evac, 1)
                for n, c, q in stage(i, s, SUMS):
                    act.wait_ge(tr_mm, q + 1)
                    act.wait_ge(ks_ready, q)
                    nc.scalar.activation(KS[:], psK[:], ACT.Copy).then_inc(ks_raw, 1)

            stream(act, step)
            act.wait_ge(fill_st, 16 * B * (3 + fills))

        @block.gpsimd
        def _(pool):
            nc.gpsimd.memset(zero[:], 0.0).then_inc(zeroed, 1)
            nc.gpsimd.memset(XL[:], 0.0).then_inc(zeroed, 1)
            nc.gpsimd.memset(room[:], 0.0).then_inc(zeroed, 1)
            nc.gpsimd.memset(minus[:], -1.0).then_inc(zeroed, 1)
            nc.gpsimd.memset(eps[:], 1e-6).then_inc(zeroed, 1)
            nc.gpsimd.memset(ones[:], 1.0).then_inc(zeroed, 1)
            nc.gpsimd.memset(K[:], 0.0).then_inc(zeroed, 1)
            pool.wait_ge(const_in, 16 * 8)
            pool.wait_ge(zeroed, 7)

            def step(i, s):
                def products(k):
                    mtx = MTX[:, :, k, :].unsqueeze(2).broadcast_to([P, TG, 3, PT])
                    ty = TENT[:, :, :, 1::2].rearrange("p j t q -> p t j q")
                    nc.gpsimd.tensor_tensor(RM[:, k], mtx, ty, ALU.mult).then_inc(rm_done, 1)

                for n, c, q in stage(i, s, SPLIT):
                    pool.wait_ge(ks_high, q + 1)
                    nc.gpsimd.tensor_tensor(KS[:], KS[:], KB[:, c % 2, 0], ALU.subtract).then_inc(rest, 1)
                for n, c, q in stage(i, s, NORM):
                    pool.wait_ge(rstd_done, q + 1)
                    pool.wait_ge(spread_mm, q)
                    nc.gpsimd.tensor_tensor(RDIAG[:], ident[:].unsqueeze(1).broadcast_to([P, NT, P]),
                                            RSTD[:].unsqueeze(2).broadcast_to([P, NT, P]), ALU.mult) \
                        .then_inc(diag_done, 1)
                for n, c, q in stage(i, s, VALUE):
                    pool.wait_ge(v_raw, q + 1)
                    v = VS[:, c % 2]
                    nc.gpsimd.tensor_tensor(v, v, vpb_bc[:].unsqueeze(1).broadcast_to([P, NT, C]), ALU.add) \
                        .then_inc(v_ready, 1)
                for n, c, q in stage(i, s, WEIGHTS):
                    pool.wait_ge(mtx_done, q + 1)
                    pool.wait_ge(k_add, q * 9)
                    products(0)
                for n, c, q in stage(i, s, WEIGHTS):
                    products(1)
                    products(2)
                for n, c, q in stage(i, s, SPLIT):
                    pool.wait_ge(mid_done, q + 1)
                    nc.gpsimd.tensor_tensor(KB[:, c % 2, 2], KS[:], KB[:, c % 2, 1], ALU.subtract).then_inc(ks_ready, 1)
                for n, c, q in stage(i, s, OFFSETS):
                    pool.wait_ge(om_evac, q + 1)
                    nc.gpsimd.tensor_tensor(OMS[:], OMS[:], omb_bc[:].unsqueeze(1).broadcast_to([P, NT, OM]),
                                            ALU.add).then_inc(om_ready, 1)

            stream(pool, step)

        @block.tensor
        def _(pe):
            pe.wait_ge(const_in, 16 * 8)
            pe.wait_ge(zeroed, 7)

            def step(i, s):
                for n, c, q in stage(i, s, VALUE):
                    pe.wait_ge(norm_done, q + 1)
                    pe.wait_ge(v_raw, q)
                    for _, _, r in stage(i, s - 1, TURN):
                        pe.wait_ge(xl_done, r + 1)
                    for t in range(NT):
                        for h in range(KC):
                            last = nc.tensor.matmul(psVal[:, t], X[:, c % 2, h, P * t:P * (t + 1)], vp_sb[:, h],
                                                    start=(h == 0), stop=(h == KC - 1))
                    last.then_inc(v_mm, 1)
                for n, c, q in stage(i, s, NORM):
                    pe.wait_ge(sq_done, q + 1)
                    pe.wait_ge(norm_done, q)
                    for t in range(NT):
                        for h in range(KC):
                            last = nc.tensor.matmul(psV[:, t:t + 1], SQ[:, h, P * t:P * (t + 1)], mean_w[:, 0:1],
                                                    start=(h == 0), stop=(h == KC - 1))
                    last.then_inc(var_done, 1)
                for n, c, q in stage(i, s, TURN):
                    pe.wait_ge(tk_in[c % 2], n * (8 * NCH) + 16 * (c // 2) + 16)
                    pe.wait_ge(xl_done, q)
                    for _, _, r in stage(i, s, VALUE):
                        pe.wait_ge(v_raw, r + 1)
                    for h in range(KC):
                        for t in range(NT):
                            last = nc.tensor.transpose(psX[:, h, P * t:P * (t + 1)],
                                                       TK[:, c % 2, t, P * h:P * (h + 1)], ident[:])
                    last.then_inc(tk_turned, 1)
                for n, c, q in stage(i, s, SUMS):
                    pe.wait_ge(k_add, q * 9 + 9)
                    pe.wait_ge(ks_raw, q)
                    for t in range(NT):
                        for h in range(2):
                            last = nc.tensor.transpose(
                                psK[:, h, P * t:P * (t + 1)],
                                K[:, G * t + 4 * h:G * t + 4 * h + 4].rearrange("p g u -> p (g u)"), ident[:])
                    last.then_inc(tr_mm, 1)
                for n, c, q in stage(i, s, NORM):
                    pe.wait_ge(diag_done, q + 1)
                    nc.tensor.matmul(psR[:], ones[:], RDIAG[:].rearrange("p t q -> p (t q)"), start=True, stop=True) \
                        .then_inc(spread_mm, 1)
                for n, c, q in stage(i, s, LOAD):
                    pe.wait_ge(x_in[c % 2], n * (8 * NCH) + 16 * (c // 2) + 16)
                    pe.wait_ge(sub_done, q)
                    for h in range(KC):
                        last = nc.tensor.matmul(psM[:], mean_w[:], X[:, c % 2, h], start=(h == 0), stop=(h == KC - 1))
                    last.then_inc(mean_done, 1)
                for n, c, q in stage(i, s, OFFSETS):
                    pe.wait_ge(dw_step, q * 18 + 18)
                    pe.wait_ge(om_evac, q)
                    for t in range(NT):
                        for h in range(KC):
                            last = nc.tensor.matmul(psO[:, t // 2, OM * (t % 2):OM * (t % 2 + 1)],
                                                    F[:, c % 2, h, P * t:P * (t + 1)], om_sb[:, h],
                                                    start=(h == 0), stop=(h == KC - 1))
                    last.then_inc(om_mm, 1)

            stream(pe, step)

        @block.vector
        def _(dve):
            dve.wait_ge(const_in, 16 * 8)
            dve.wait_ge(zeroed, 7)

            def step(i, s):
                def sums(q):
                    dve.wait_ge(k_clr, q + 1)
                    for j in range(3):
                        dve.wait_ge(rm_done, q * 3 + j + 1)
                        for k in range(3):
                            if j or k:
                                dve.wait_ge(k_add, q * 9 + 3 * j + k)
                            at = 5 * k + j
                            kk = K[:, :, at:at + 15].rearrange("p t (v u) -> p t u v", u=5)[:, :, 0:3]
                            nc.vector.tensor_tensor(
                                kk, kk, RM[:, j, :, k].rearrange("p t (a b) -> p t a b", a=3),
                                ALU.add).then_inc(k_add, 1)
                            yield

                def convolve(c, q, taps, between=iter(())):
                    for t in taps:
                        for h in range(KC):
                            src = XL[:, h, RC * c + t // 3:RC * c + t // 3 + RC, t % 3:t % 3 + W]
                            acc = F[:, c % 2, h].rearrange("p (y w) -> p y w", w=W)
                            if t == 0:
                                ins = nc.vector.tensor_scalar(acc, src, dw_sb[:, h, t:t + 1],
                                                              dwb_sb[:, h:h + 1], ALU.mult, ALU.add)
                            else:
                                dve.wait_ge(dw_step, q * 18 + 2 * t + h - 1)
                                ins = nc.vector.scalar_tensor_tensor(acc, src, dw_sb[:, h, t:t + 1], acc,
                                                                     ALU.mult, ALU.add)
                            ins.then_inc(dw_step, 1)
                            next(between, None)

                for n, c, q in stage(i, s, NORM):
                    dve.wait_ge(x_in[c % 2], n * (8 * NCH) + 16 * (c // 2) + 16)
                    dve.wait_ge(mean_done, q + 1)
                    xs = X[:, c % 2]
                    nc.vector.tensor_tensor(xs, xs, psM[:].unsqueeze(1).broadcast_to([P, KC, N]), ALU.subtract) \
                        .then_inc(sub_done, 1)
                adding = iter(())
                for n, c, q in stage(i, s, SUMS):
                    adding = sums(q)
                for n, c, q in stage(i, s, OFFSETS):
                    dve.wait_ge(xl_done, n * NCH + min(c + 2, NCH))
                    if not isinstance(q, int) or q >= 2:
                        dve.wait_ge(om_mm, q - 1)
                    convolve(c, q, range(0, 6), adding)
                for _ in adding:
                    pass
                for n, c, q in stage(i, s, NORM):
                    dve.wait_ge(std_done, q + 1)
                    dve.wait_ge(diag_done, q)
                    nc.vector.reciprocal(RSTD[:], STD[:]).then_inc(rstd_done, 1)
                for n, c, q in stage(i, s, WEIGHTS):
                    dve.wait_ge(tent_done, q + 1)
                    dve.wait_ge(rm_done, q * 3)
                    mask = OMS[:].rearrange("p t (g o) -> p (t g) o", g=G)[:, :, 2 * PT:3 * PT] \
                        .unsqueeze(2).broadcast_to([P, TG, 3, PT])
                    tx = TENT[:, :, :, 0::2].rearrange("p i t q -> p t i q")
                    nc.vector.tensor_tensor(room[:, 0:1], room[:, 0:1], room[:, 1:2], ALU.add)
                    nc.vector.tensor_tensor(MTX[:], mask, tx, ALU.mult).then_inc(mtx_done, 1)
                for n, c, q in stage(i, s, OFFSETS):
                    convolve(c, q, range(6, 9))
                for n, c, q in stage(i, s, NORM):
                    dve.wait_ge(spread_mm, q + 1)
                    xs = X[:, c % 2]
                    nc.vector.tensor_tensor(xs, xs, psR[:].unsqueeze(1).broadcast_to([P, KC, N]), ALU.mult) \
                        .then_inc(norm_done, 1)

            stream(dve, step)

def deform(nc, x, op_w, op_b, select_d, v_pad, taps_t, x1, passed):
    B, C, HW = x.shape
    W = 64
    H = HW // W
    KC = C // P
    N = 512
    NCH = HW // N
    NBX = W // BW
    NBY = -(-H // BH)
    NB = NBX * NBY
    CG = C // G
    GH = G // KC
    APOS = 4
    AB = NPOS // APOS
    LAST = H - BH * (NBY - 1)
    SELW = select_d.shape[1]
    TR = PARTS * TAPP
    XS = 4
    with ExitStack() as ctx:
        def sb(name, shape, dt=F32):
            return ctx.enter_context(nc.sbuf_tensor(name, shape, dt))

        def ps(name, shape):
            return ctx.enter_context(nc.psum_tensor(name, shape, F32))

        def sem(name):
            return ctx.enter_context(nc.semaphore(name))

        V = sb("V", [Q, KC, NB, P])
        KT = sb("KT", [TR, 2, H, W], BF16)
        A = sb("A", [Q, 2, NB, NPOS])
        D = sb("D", [P, KC, H, W])
        XR = sb("XR", [P, XS, KC, N])
        op_sb = sb("op_sb", [P, KC, C])
        opb_sb = sb("opb_sb", [P, KC])
        SELF = sb("SELF", [TR, SELW])
        SEL = sb("SEL", [TR, SELW], BF16)
        psA = ps("psA", [P, 4, 512])
        psD = ps("psD", [P, 2, 512])
        psP = ps("psP", [P, KC, N])

        w_in, sel_done = sem("w_in"), sem("sel_done")
        v_in = [sem(f"v_in{i}") for i in range(KC)]
        kt_in = [sem(f"kt_in{i}") for i in range(2)]
        a_mm, d_mm, p_mm = sem("a_mm"), sem("d_mm"), sem("p_mm")
        a_out = [sem("a_out_act"), sem("a_out_dve")]
        d_out = [sem("d_out_act"), sem("d_out_dve")]
        res_done = sem("res_done")
        xr_in = [sem(f"xr_in{i}") for i in range(XS)]
        x1_st = [sem(f"x1_st{i}") for i in range(XS)]
        block = ctx.enter_context(nc.Block())

        APG = AB * G
        DPG = NBY * G

        def images(eng, image):
            if B > 1:
                with eng.Fori(0, B - 1) as n:
                    image(n, False)
            image(B - 1, True)

        @block.sync
        def _(sp):
            sp.dma_start(SELF[:], select_d[0:TR]).then_inc(w_in, 16)
            sp.dma_start(op_sb[:], op_w.rearrange("(h p) o -> p h o", p=P)).then_inc(w_in, 16)
            sp.dma_start(opb_sb[:], op_b).then_inc(w_in, 16)
            def load_values(n, h):
                for bx in range(NBX):
                    for r in range(RH):
                        src = v_pad[n, r:r + BH * (NBY - 1) + 1:BH, BW * bx:BW * bx + RW, P * h:P * (h + 1)]
                        sp.dma_start(V[RW * r:RW * (r + 1), h, bx::NBX], src.rearrange("a w c -> w a c")) \
                            .then_inc(v_in[h], 16)

            load_values(0, 0)
            load_values(0, 1)

            def image(n, last):
                for h in range(KC):
                    if not last:
                        sp.wait_ge(d_mm, n * DPG + DPG // 2 * (h + 1))
                        sp.sem_inc(passed, 1)
                        load_values(n + 1, h)

            images(sp, image)

        @block.gpsimd
        def _(pool):
            with pool.Fori(0, B) as n:
                def load(c):
                    pool.wait_ge(x1_st[c % XS], n * (16 * NCH // XS) + 16 * (c // XS))
                    pool.sem_inc(passed, 1)
                    pool.dma_start(XR[:, c % XS], x[n, :, N * c:N * (c + 1)].rearrange("(h p) w -> p h w", p=P)) \
                        .then_inc(xr_in[c % XS], 16)

                for c in range(XS):
                    load(c)
                for c in range(NCH):
                    pool.wait_ge(res_done, n * (KC * NCH) + KC * (c + 1))
                    pool.sem_inc(passed, 1)
                    pool.dma_start(x1[n, :, N * c:N * (c + 1)].rearrange("(h p) w -> p h w", p=P), XR[:, c % XS]) \
                        .then_inc(x1_st[c % XS], 16)
                    if 0 <= c - 1 and c - 1 + XS < NCH:
                        load(c - 1 + XS)
            for s in range(XS):
                pool.wait_ge(x1_st[s], 16 * NCH // XS * B)

        def copy_matrices(eng, who, n, g, b):
            s = g * AB + b
            eng.wait_ge(a_mm, n * APG + s + 1)
            if not isinstance(n, int) or n * G + g >= 2:
                eng.wait_ge(d_mm, n * DPG + NBY * (g - 1))
            py = b * APOS // BW
            nb = NB if py < LAST else NB - NBX
            at = b * APOS
            dst = A[:, g % 2, :nb, at:at + APOS].rearrange("q k a -> q a k")
            src = psA[:Q, b % 4, :APOS * nb].rearrange("q (a k) -> q a k", k=nb)
            if who:
                nc.vector.tensor_copy(dst, src).then_inc(a_out[1], 1)
            else:
                nc.scalar.activation(dst, src, ACT.Copy).then_inc(a_out[0], 1)

        def copy_outputs(eng, who, n, g, by):
            eng.wait_ge(d_mm, n * DPG + g * NBY + by + 1)
            if g == 0:
                eng.wait_ge(p_mm, n * (KC * NCH))
            rows = BH if by < NBY - 1 else LAST
            q0 = CG * (g % GH)
            dst = D[q0:q0 + CG, g // GH, BH * by:BH * by + rows].rearrange("q y (b x) -> q y b x", b=NBX)
            src = psD[q0:q0 + CG, (g * NBY + by) % 2, :NPOS * NBX].rearrange(
                "q (b y x) -> q y b x", b=NBX, y=BH)[:, :rows]
            if who:
                nc.vector.tensor_copy(dst, src).then_inc(d_out[1], 1)
            else:
                nc.scalar.activation(dst, src, ACT.Copy).then_inc(d_out[0], 1)

        def copies(eng, who, n, last, load_taps=None):
            for g in range(G):
                for k in range(AB):
                    if k < NBY and (g * NBY + k) % 2 == who:
                        copy_outputs(eng, who, n, g, k)
                    if (g + 1 < G or not last) and k % 2 == who:
                        copy_matrices(eng, who, n + (g + 1) // G, (g + 1) % G, k)
                if load_taps and (g + 3 < G or not last):
                    eng.wait_ge(a_mm, n * APG + AB * (g + 2))
                    load_taps(n + (g + 3) // G, (g + 3) % G)

        @block.scalar
        def _(act):
            parts = taps_t.rearrange("n (r h) (g p) w -> n r h g p w", r=PARTS, g=GH)

            def load_taps(n, g):
                for r in range(PARTS):
                    act.dma_start(KT[TAPP * r:TAPP * (r + 1), g % 2].rearrange("p y w -> p (y w)"),
                                  parts[n, r, g // GH, g % GH]).then_inc(kt_in[g % 2], 16)

            load_taps(0, 0)
            load_taps(0, 1)
            for b in range(0, AB, 2):
                copy_matrices(act, 0, 0, 0, b)
            act.wait_ge(a_mm, AB)
            load_taps(0, 2)
            images(act, lambda n, last: copies(act, 0, n, last, load_taps))

        @block.vector
        def _(dve):
            dve.wait_ge(w_in, 48)
            nc.vector.tensor_copy(SEL[:], SELF[:]).then_inc(sel_done, 1)
            for b in range(1, AB, 2):
                copy_matrices(dve, 1, 0, 0, b)

            def image(n, last):
                copies(dve, 1, n, last)
                for c in range(NCH):
                    dve.wait_ge(xr_in[c % XS], n * (16 * NCH // XS) + 16 * (c // XS) + 16)
                    for m in range(KC):
                        dve.wait_ge(p_mm, n * (KC * NCH) + KC * c + m + 1)
                        xs = XR[:, c % XS, m]
                        nc.vector.scalar_tensor_tensor(xs, psP[:, m], opb_sb[:, m:m + 1], xs, ALU.add, ALU.add) \
                            .then_inc(res_done, 1)

            images(dve, image)

        @block.tensor
        def _(pe):
            pe.wait_ge(w_in, 48)
            pe.wait_ge(sel_done, 1)

            def matrices(n, g, b):
                s = g * AB + b
                if not isinstance(n, int) or s >= 4:
                    pe.wait_ge(a_out[b % 2], n * (APG // 2) + (s - 4) // 2 + 1)
                if b == 0:
                    pe.wait_ge(kt_in[g % 2], n * (8 * PARTS * G) + 16 * PARTS * (g // 2 + 1))
                for a in range(APOS):
                    py, px = divmod(b * APOS + a, BW)
                    nb = NB if py < LAST else NB - NBX
                    at = (BH - 1) * RW + BW - 1 - (py * RW + px)
                    last = nc.tensor.matmul(psA[:, b % 4, a * nb:(a + 1) * nb], SEL[:, at:at + P],
                                            KT[:, g % 2, py::BH, px::BW], start=True, stop=True)
                last.then_inc(a_mm, 1)

            def outputs(n, g, by):
                r = g * NBY + by
                if by == 0:
                    for w in range(2):
                        pe.wait_ge(a_out[w], n * (APG // 2) + AB // 2 * (g + 1))
                if g % GH == 0 and by == 0:
                    pe.wait_ge(v_in[g // GH], n * (16 * RH * NBX) + 16 * RH * NBX)
                if r < 2:
                    pe.wait_ge(d_out[r % 2], n * (DPG // 2))
                else:
                    pe.wait_ge(d_out[r % 2], n * (DPG // 2) + r // 2)
                c0 = CG * (g % GH)
                size = NPOS if by < NBY - 1 else LAST * BW
                for bx in range(NBX):
                    k = by * NBX + bx
                    last = nc.tensor.matmul(psD[c0:c0 + CG, r % 2, NPOS * bx:NPOS * bx + size],
                                            V[:, g // GH, k, c0:c0 + CG], A[:, g % 2, k, :size],
                                            start=True, stop=True)
                last.then_inc(d_mm, 1)

            for b in range(AB):
                matrices(0, 0, b)

            def image(n, last):
                for g in range(G):
                    for k in range(AB):
                        if k < NBY:
                            outputs(n, g, k)
                        if g + 1 < G or not last:
                            matrices(n + (g + 1) // G, (g + 1) % G, k)
                for w in range(2):
                    pe.wait_ge(d_out[w], n * (DPG // 2) + DPG // 2)
                for c in range(NCH):
                    for m in range(KC):
                        pe.wait_ge(res_done, n * (KC * NCH) + max(KC * c + m - 1, 0))
                        for h in range(KC):
                            prod = nc.tensor.matmul(
                                psP[:, m], op_sb[:, h, P * m:P * (m + 1)],
                                D[:, h, N // W * c:N // W * (c + 1)].rearrange("p y w -> p (y w)"),
                                start=(h == 0), stop=(h == KC - 1))
                        prod.then_inc(p_mm, 1)

            images(pe, image)

def resample(nc, x, op_w, op_b, ident_d, pix, geo, v_pad, om_raw, sampled, x1, flag):
    B, C, HW = x.shape
    W = 64
    KC = C // P
    TI = HW // P
    WP = v_pad.shape[2]
    CG = C // G
    NK = 4 * PT
    GO = 3 * PT
    TOP = float(W + 2)
    values = v_pad.rearrange("n y w (g c) -> (n y w g) c", g=G)
    om_t = om_raw.rearrange("n t p o -> (n t) p o")
    with ExitStack() as ctx:
        def sb(name, shape, dt=F32):
            return ctx.enter_context(nc.sbuf_tensor("f_" + name, shape, dt))

        def sem(name):
            return ctx.enter_context(nc.semaphore("f_" + name))

        ident = sb("ident", [P, P])
        opw = sb("opw", [P, KC, C])
        opb = sb("opb", [P, KC])
        PIX = sb("PIX", [P, 2, PT])
        OMG = sb("OMG", [P, GO])
        GEO = sb("GEO", [P, 2])
        XY = sb("XY", [P, 2, PT])
        II = sb("II", [P, 2, PT], I32)
        FL = sb("FL", [P, 2, PT])
        OV = sb("OV", [P, 2, PT])
        FR = sb("FR", [P, 2, 2, PT])
        ROW = sb("ROW", [P, PT])
        IDX = sb("IDX", [P, 4, PT], U32)
        WC = sb("WC", [P, 4, PT])
        GV = sb("GV", [P, NK, CG])
        ACC = sb("ACC", [P, CG])
        ST = sb("ST", [P, C])
        SC = sb("SC", [P, KC, P])
        XR = sb("XR", [P, KC, P])
        psT = ctx.enter_context(nc.psum_tensor("f_psT", [P, KC, P], F32))
        psP = ctx.enter_context(nc.psum_tensor("f_psP", [P, KC, P], F32))
        w_in, om_in, geo_in, idx_done, got, gathered, acc_done, acc_st, step, passed = (
            sem(n) for n in ("w_in", "om_in", "geo_in", "idx_done", "got", "gathered", "acc_done", "acc_st", "step", "passed"))
        t_in, turned, copied, mm, res, x1_st = (sem(n) for n in ("t_in", "turned", "copied", "mm", "res", "x1_st"))
        DS = 13
        block = ctx.enter_context(nc.Block())

        @block.sync
        def _(sp):
            for dst, src in ((ident[:], ident_d), (opw[:], op_w.rearrange("(h p) o -> p h o", p=P)),
                             (opb[:], op_b), (PIX[:], pix)):
                sp.dma_start(dst, src).then_inc(w_in, 16)
            sp.wait_ge(w_in, 64)
            fast = sp.value_load(flag, min_val=0, max_val=1)
            with sp.If(fast < 1):
                with sp.Fori(0, B * TI) as t:
                    with sp.Fori(0, G) as g:
                        k = t * G + g
                        sp.wait_ge(acc_done, k)
                        sp.dma_start(OMG[:], om_t[t, :, bass.ds(g * GO, GO)]).then_inc(om_in, 16)
                        sp.dma_start(GEO[:], geo[k].partition_broadcast(P)).then_inc(geo_in, 16)
                        sp.wait_ge(acc_done, k + 1)
                        sp.dma_start(sampled[t, :, bass.ds(g * CG, CG)], ACC[:]).then_inc(acc_st, 16)
                sp.wait_ge(acc_st, 16 * B * TI * G)
                with sp.Fori(0, B) as n:
                    with sp.Fori(0, TI) as t:
                        k = n * TI + t
                        sp.wait_ge(x1_st, k * 16)
                        sp.dma_start(ST[:], sampled[k]).then_inc(t_in, 16)
                        sp.dma_start(XR[:], x[n, :, bass.ds(t * P, P)].rearrange("(h p) w -> p h w", p=P)) \
                            .then_inc(t_in, 16)
                        sp.wait_ge(res, k * KC + KC)
                        sp.dma_start(x1[n, :, bass.ds(t * P, P)].rearrange("(h p) w -> p h w", p=P), XR[:]) \
                            .then_inc(x1_st, 16)
                sp.wait_ge(x1_st, 16 * B * TI)

        @block.gpsimd
        def _(pool):
            fast = pool.value_load(flag, min_val=0, max_val=1)
            with pool.If(fast < 1):
                with pool.Fori(0, B * TI) as t:
                    with pool.Fori(0, G) as g:
                        k = t * G + g
                        pool.wait_ge(idx_done, k + 1)
                        pool.sem_inc(passed, 1)
                        for j in range(NK):
                            pool.indirect_dma_start(
                                out=GV[:, j], out_offset=None, in_=values,
                                in_offset=bass.IndirectOffsetOnAxis(ap=IDX[:, j // PT, j % PT:j % PT + 1], axis=0)) \
                                .then_inc(got, 16)
                        pool.wait_ge(got, 16 * NK)
                        pool.sem_inc(gathered, 1)
                        pool.inc_swdge_sem([got], [16 * NK], mode="sub")

        @block.vector
        def _(dve):
            V = nc.vector
            dve.wait_ge(w_in, 64)
            fast = dve.value_load(flag, min_val=0, max_val=1)
            with dve.If(fast < 1):
                with dve.Fori(0, B * TI) as t:
                    with dve.Fori(0, G) as g:
                        k = t * G + g
                        done = [0]

                        def run(ins):
                            done[0] += 1
                            ins.then_inc(step, 1)
                            dve.wait_ge(step, k * DS + done[0])

                        dve.wait_ge(om_in, k * 16 + 16)
                        dve.wait_ge(geo_in, k * 16 + 16)
                        run(V.tensor_tensor(XY[:], OMG[:, :2 * PT].rearrange("p (q s) -> p s q", s=2), PIX[:], ALU.add))
                        run(V.tensor_scalar(XY[:, 1], XY[:, 1], GEO[:, 0:1], None, ALU.add))
                        run(V.tensor_scalar(XY[:], XY[:], 0.0, TOP, ALU.max, ALU.min))
                        run(V.tensor_copy(II[:], XY[:]))
                        run(V.tensor_copy(FL[:], II[:]))
                        run(V.tensor_tensor(OV[:], FL[:], XY[:], ALU.is_gt))
                        run(V.tensor_tensor(FL[:], FL[:], OV[:], ALU.subtract))
                        run(V.tensor_tensor(FR[:, 1], XY[:], FL[:], ALU.subtract))
                        run(V.tensor_scalar(FR[:, 0], FR[:, 1], -1.0, 1.0, ALU.mult, ALU.add))
                        run(V.scalar_tensor_tensor(ROW[:], FL[:, 1], float(WP), FL[:, 0], ALU.mult, ALU.add))
                        run(V.tensor_scalar(ROW[:], ROW[:], float(G), GEO[:, 1:2], ALU.mult, ALU.add))
                        for j in range(4):
                            V.tensor_scalar(IDX[:, j], ROW[:], float((j // 2 * WP + j % 2) * G), None, ALU.add)
                            ins = V.tensor_tensor(WC[:, j], FR[:, j // 2, 1], FR[:, j % 2, 0], ALU.mult)
                        run(ins)
                        V.tensor_tensor(WC[:], WC[:], OMG[:, 2 * PT:].unsqueeze(1).broadcast_to([P, 4, PT]), ALU.mult) \
                            .then_inc(idx_done, 1)
                        dve.wait_ge(idx_done, k + 1)
                        dve.wait_ge(gathered, k + 1)
                        run(V.tensor_tensor(GV[:], GV[:], WC[:].rearrange("p j q -> p (j q)").unsqueeze(2)
                                            .broadcast_to([P, NK, CG]), ALU.mult))
                        dve.wait_ge(acc_st, k * 16)
                        V.tensor_reduce(ACC[:], GV[:].rearrange("p k c -> p c k"), AX.X, ALU.add).then_inc(acc_done, 1)
                        assert done[0] == DS
                with dve.Fori(0, B * TI) as k:
                    dve.wait_ge(t_in, k * 32 + 32)
                    dve.wait_ge(mm, k + 1)
                    for m in range(KC):
                        V.scalar_tensor_tensor(XR[:, m], psP[:, m], opb[:, m:m + 1], XR[:, m], ALU.add, ALU.add) \
                            .then_inc(res, 1)

        @block.tensor
        def _(pe):
            pe.wait_ge(w_in, 64)
            fast = pe.value_load(flag, min_val=0, max_val=1)
            with pe.If(fast < 1):
                with pe.Fori(0, B * TI) as k:
                    pe.wait_ge(t_in, k * 32 + 32)
                    for h in range(KC):
                        last = nc.tensor.transpose(psT[:, h], ST[:, P * h:P * (h + 1)], ident[:])
                    last.then_inc(turned, 1)
                    pe.wait_ge(copied, k + 1)
                    for m in range(KC):
                        for h in range(KC):
                            last = nc.tensor.matmul(psP[:, m], opw[:, h, P * m:P * (m + 1)], SC[:, h],
                                                    start=(h == 0), stop=(h == KC - 1))
                    last.then_inc(mm, 1)

        @block.scalar
        def _(act):
            fast = act.value_load(flag, min_val=0, max_val=1)
            with act.If(fast < 1):
                with act.Fori(0, B * TI) as k:
                    act.wait_ge(turned, k + 1)
                    nc.scalar.activation(SC[:], psT[:], ACT.Copy).then_inc(copied, 1)

def route(nc, x1, gate_w, gate_b, cst, xe, CAP, NJ, tables, yrow, wgt, passed):
    B, C, HW = x1.shape
    E = gate_b.shape[0]
    KC = C // P
    N = 512
    NT = N // P
    NCH = HW // N
    NK = B * NCH
    NTOK = NK * NT
    KMAX = CAP // TM
    with ExitStack() as ctx:
        def sb(name, shape, dt=F32):
            return ctx.enter_context(nc.sbuf_tensor(name, shape, dt))

        def ps(name, shape):
            return ctx.enter_context(nc.psum_tensor(name, shape, F32))

        def sem(name):
            return ctx.enter_context(nc.semaphore(name))

        ident = sb("p3_ident", [P, P])
        trif = sb("trif", [P, P])
        tri = sb("tri", [P, P], BF16)
        ones = sb("p3_ones", [P, P])
        ones_b = sb("p3_ones_b", [P, P], BF16)
        gw = sb("gw", [P, KC, E])
        gb = sb("gb", [P, E])
        rank = sb("rank", [P, E])
        ebase = sb("ebase", [P, E])
        own = sb("own", [P, NTOK])
        steps = sb("steps", [P, KMAX])
        jota = sb("jota", [P, NJ])
        eps = sb("p3_eps", [P, 1])
        XC = sb("XC", [P, 2, KC, N])
        ST = sb("ST", [P, NT, 6])
        MV = sb("MV", [P, NT, 2])
        STD = sb("p3_STD", [P, NT])
        RS = sb("RS", [P, 2, NT])
        NB = sb("NB", [P, 2, NT])
        XT = sb("XT", [P, 2, NT, C])
        LT = sb("LT", [P, NT, E])
        MX = sb("MX", [P, NT])
        EQ = sb("EQ", [P, NT, E])
        FI = sb("FI", [P, NT])
        OH = sb("OH", [P, NT + 1, E], BF16)
        PO = sb("PO", [P, NT, E])
        PB = sb("PB", [P, NT, E])
        POS = sb("POS", [P, NT])
        ROW = sb("ROW", [P, NT])
        KEEP = sb("KEEP", [P, NT])
        IDX = sb("IDX", [P, 2, NT], U32)
        cnt = sb("cnt", [P, E])
        LALL = sb("LALL", [P, NTOK, E])
        OHALL = sb("OHALL", [P, NTOK, E])
        PALL = sb("PALL", [P, NTOK])
        small = sb("small", [P, 8, E])
        CMP = sb("CMP", [P, E, KMAX])
        JC = sb("JC", [P, NJ, E])
        JT = sb("JT", [P, 4, NJ])
        W1 = sb("W1", [P, NTOK])
        psT = ps("psT", [P, 2, 2, 2, C])
        psG = ps("psG", [P, 2, NT, 512 // NT])
        psC = ps("psC", [P, NT + 1, E])

        c_in, zeroed = sem("c_in"), sem("p3_zeroed")
        x_in = [sem(f"p3_x_in{i}") for i in range(2)]
        t_mm, g_mm, c_mm = sem("t_mm"), sem("g_mm"), sem("c_mm")
        st_done, mv_done, std_done, rs_done, nb_done = (sem(n) for n in ("st_done", "mv_done", "p3_std", "rs_done", "nb_done"))
        xt_done, idx_done, pos_step, oh_done = sem("xt_done"), sem("idx_done"), sem("pos_step"), sem("oh_done")
        sc_st = [sem(f"sc_st{i}") for i in range(2)]
        gw_mm, gw_done = sem("gw_mm"), sem("gw_done")
        fin, fin_act = sem("fin"), sem("fin_act")
        block = ctx.enter_context(nc.Block())
        consts = [(ident, cst["ident"]), (trif, cst["tri"]), (own, cst["own"])]
        rows = [(gb, gate_b), (rank, cst["rank"]), (ebase, cst["ebase"]), (steps, cst["steps"]), (jota, cst["jota"])]
        NC_IN = 16 * (len(consts) + len(rows) + 1)
        DCH = 13

        def chunks(eng, front, back):
            front(0, 0)
            if B > 1:
                with eng.Fori(0, B - 1) as n:
                    for c in range(NCH):
                        front(n + (c + 1) // NCH, (c + 1) % NCH)
                        back(n, c)
            for c in range(NCH):
                if c + 1 < NCH:
                    front(B - 1, c + 1)
                back(B - 1, c)

        @block.sync
        def _(sp):
            for dst, src in consts:
                sp.dma_start(dst[:], src).then_inc(c_in, 16)
            for dst, src in rows:
                sp.dma_start(dst[:], src.partition_broadcast(P)).then_inc(c_in, 16)
            sp.dma_start(gw[:], gate_w.rearrange("(h p) e -> p h e", p=P)).then_inc(c_in, 16)
            with sp.Fori(0, B) as n:
                for c in range(NCH):
                    sp.wait_ge(g_mm, n * NCH + max(c - 1, 0))
                    sp.dma_start(XC[:, c % 2], x1[n, :, N * c:N * (c + 1)].rearrange("(h p) w -> p h w", p=P)) \
                        .then_inc(x_in[c % 2], 16)

        @block.tensor
        def _(pe):
            pe.wait_ge(c_in, NC_IN)
            pe.wait_ge(zeroed, 5)
            for h in range(KC):
                last = nc.tensor.matmul(psC[:, 0], ones[:], gw[:, h], start=(h == 0), stop=(h == KC - 1))
            last.then_inc(gw_mm, 1)
            pe.wait_ge(gw_done, KC + 1)

            def turn(n, c):
                pe.wait_ge(x_in[c % 2], n * (8 * NCH) + 16 * (c // 2) + 16)
                pe.wait_ge(xt_done, n * (NT * NCH) + NT * max(c - 1, 0))
                for t in range(NT):
                    for h in range(KC):
                        last = nc.tensor.transpose(psT[:, c % 2, t // 2, t % 2, P * h:P * (h + 1)],
                                                   XC[:, c % 2, h, P * t:P * (t + 1)], ident[:])
                last.then_inc(t_mm, 1)
                pe.wait_ge(oh_done, n * NCH + max(c - 1, 0))
                for t in range(NT):
                    for h in range(KC):
                        last = nc.tensor.matmul(psG[:, c % 2, t, :E], XC[:, c % 2, h, P * t:P * (t + 1)], gw[:, h],
                                                start=(h == 0), stop=(h == KC - 1))
                last.then_inc(g_mm, 1)

            def count(n, c):
                pe.wait_ge(oh_done, n * NCH + c + 1)
                nc.tensor.matmul(psC[:], tri[:], OH[:], start=True, stop=True)
                for t in range(NT):
                    last = nc.tensor.matmul(psC[:, t + 1:], ones_b[:],
                                            OH[:, t:t + 1].broadcast_to([P, NT - t, E]),
                                            start=False, stop=True, skip_group_check=True)
                last.then_inc(c_mm, 1)

            chunks(pe, turn, count)

        @block.scalar
        def _(act):
            act.wait_ge(zeroed, 5)
            with act.Fori(0, B) as n:
                for c in range(NCH):
                    act.wait_ge(mv_done, n * (NT * NCH) + NT * (c + 1))
                    nc.scalar.activation(STD[:], MV[:, :, 1], ACT.Sqrt, bias=eps[:]).then_inc(std_done, 1)
                    act.wait_ge(nb_done, n * NCH + c + 1)
                    act.wait_ge(sc_st[c % 2], n * (16 * NT * NCH // 2) + 16 * NT * (c // 2))
                    for t in range(NT):
                        nc.scalar.activation(XT[:, c % 2, t], psT[:, c % 2, t // 2, t % 2], ACT.Identity,
                                             bias=NB[:, c % 2, t:t + 1], scale=RS[:, c % 2, t:t + 1]) \
                            .then_inc(xt_done, 1)
            act.wait_ge(fin, 2)
            nc.scalar.activation(LALL[:], LALL[:], ACT.Exp).then_inc(fin_act, 1)

        @block.gpsimd
        def _(pool):
            nc.gpsimd.memset(ones[:], 1.0).then_inc(zeroed, 1)
            nc.gpsimd.memset(ones_b[:], 1.0).then_inc(zeroed, 1)
            nc.gpsimd.memset(eps[:], 1e-5).then_inc(zeroed, 1)
            nc.gpsimd.memset(OH[:], 0.0).then_inc(zeroed, 1)
            nc.gpsimd.memset(cnt[:], 0.0).then_inc(zeroed, 1)
            with pool.Fori(0, B) as n:
                for c in range(NCH):
                    pool.wait_ge(xt_done, n * (NT * NCH) + NT * (c + 1))
                    pool.wait_ge(idx_done, n * NCH + c + 1)
                    pool.sem_inc(passed, 1)
                    for t in range(NT):
                        pool.indirect_dma_start(
                            out=xe, out_offset=bass.IndirectOffsetOnAxis(ap=IDX[:, c % 2, t:t + 1], axis=0),
                            in_=XT[:, c % 2, t], in_offset=None).then_inc(sc_st[c % 2], 16)
            for s in range(2):
                pool.wait_ge(sc_st[s], 16 * NT * NK // 2)

        @block.vector
        def _(dve):
            dve.wait_ge(c_in, NC_IN)
            dve.wait_ge(zeroed, 5)

            def over(ap, k):
                return ap.unsqueeze(1).broadcast_to([P, k, E])

            def per(ap, k):
                return ap.unsqueeze(2).broadcast_to([P, k, E])

            V = nc.vector
            V.tensor_copy(tri[:], trif[:]).then_inc(gw_done, 1)
            dve.wait_ge(gw_mm, 1)
            for h in range(KC):
                V.scalar_tensor_tensor(gw[:, h], psC[:, 0], -1.0 / C, gw[:, h], ALU.mult, ALU.add).then_inc(gw_done, 1)
            def statistics(n, c):
                dve.wait_ge(t_mm, n * NCH + c + 1)
                for t in range(NT):
                    V.bn_stats(ST[:, t], psT[:, c % 2, t // 2, t % 2]).then_inc(st_done, 1)
                    yield
                dve.wait_ge(st_done, n * (NT * NCH) + NT * (c + 1))
                dve.sem_inc(passed, 1)
                for t in range(NT):
                    V.bn_aggr(MV[:, t], ST[:, t]).then_inc(mv_done, 1)

            def scales(n, c):
                dve.wait_ge(std_done, n * NCH + c + 1)
                dve.wait_ge(xt_done, n * (NT * NCH) + NT * max(c - 1, 0))
                V.reciprocal(RS[:, c % 2], STD[:]).then_inc(rs_done, 1)
                dve.wait_ge(rs_done, n * NCH + c + 1)
                V.scalar_tensor_tensor(NB[:, c % 2], MV[:, :, 0], -1.0, RS[:, c % 2], ALU.mult, ALU.mult) \
                    .then_inc(nb_done, 1)

            def places(n, c, between, beside):
                base = n * (DCH * NCH) + DCH * c
                done = [0]

                def step(ins):
                    done[0] += 1
                    ins.then_inc(pos_step, 1)
                    if done[0] < 6:
                        next(between, None)
                    dve.wait_ge(pos_step, base + done[0])

                dve.wait_ge(rs_done, n * NCH + c + 1)
                dve.wait_ge(g_mm, n * NCH + c + 1)
                tiles = bass.ds(n * (NT * NCH) + NT * c, NT)
                step(V.tensor_tensor(LT[:], psG[:, c % 2, :, :E], per(RS[:, c % 2], NT), ALU.mult))
                step(V.tensor_tensor(LT[:], LT[:], over(gb[:], NT), ALU.add))
                V.tensor_copy(LALL[:, tiles], LT[:])
                step(V.tensor_reduce(MX[:], LT[:], AX.X, ALU.max))
                step(V.tensor_tensor(EQ[:], LT[:], per(MX[:], NT), ALU.is_equal))
                step(V.tensor_tensor(EQ[:], EQ[:], over(rank[:], NT), ALU.mult))
                step(V.tensor_reduce(FI[:], EQ[:], AX.X, ALU.max))
                V.tensor_tensor(OH[:, :NT], EQ[:], per(FI[:], NT), ALU.is_equal).then_inc(oh_done, 1)
                for _ in between:
                    pass
                dve.wait_ge(oh_done, n * NCH + c + 1)
                V.tensor_copy(OHALL[:, tiles], OH[:, :NT])
                step(V.tensor_tensor(PB[:], OH[:, :NT], over(ebase[:], NT), ALU.mult))
                V.tensor_reduce(ROW[:], PB[:], AX.X, ALU.add)
                dve.wait_ge(c_mm, n * NCH + c + 1)
                step(V.tensor_tensor(PO[:], psC[:, :NT], over(cnt[:], NT), ALU.add))
                step(V.tensor_tensor(PO[:], PO[:], OH[:, :NT], ALU.mult))
                V.tensor_tensor(cnt[:], cnt[:], psC[:, NT], ALU.add)
                step(V.tensor_reduce(POS[:], PO[:], AX.X, ALU.add))
                beside()
                V.tensor_copy(PALL[:, tiles], POS[:])
                V.tensor_scalar(KEEP[:], POS[:], float(CAP), None, ALU.is_lt)
                step(V.tensor_tensor(ROW[:], ROW[:], own[:, tiles], ALU.subtract))
                step(V.tensor_tensor(ROW[:], ROW[:], POS[:], ALU.add))
                step(V.tensor_tensor(ROW[:], ROW[:], KEEP[:], ALU.mult))
                assert done[0] == DCH
                dve.wait_ge(sc_st[c % 2], n * (16 * NT * NCH // 2) + 16 * NT * (c // 2))
                V.tensor_tensor(IDX[:, c % 2], ROW[:], own[:, tiles], ALU.add).then_inc(idx_done, 1)

            def image(n, last):
                for c in range(NCH):
                    following = [] if last and c + 1 == NCH else [(n + (c + 1) // NCH, (c + 1) % NCH)]
                    between = iter(())
                    for at in following:
                        between = statistics(*at)
                    places(n, c, between, lambda: [scales(*at) for at in following])

            for _ in statistics(0, 0):
                pass
            scales(0, 0)
            if B > 1:
                with dve.Fori(0, B - 1) as n:
                    image(n, False)
            image(B - 1, True)

            dve.wait_ge(idx_done, NK)
            done = [0]

            def last(ins):
                done[0] += 1
                ins.then_inc(fin, 1)
                dve.wait_ge(fin, done[0])

            last(V.tensor_reduce(W1[:], LALL[:], AX.X, ALU.max))
            last(V.tensor_tensor(LALL[:], LALL[:], per(W1[:], NTOK), ALU.subtract))
            kept, ntile, first, end = small[:, 0], small[:, 1], small[:, 2], small[:, 3]
            last(V.tensor_scalar(kept, cnt[:], float(CAP), None, ALU.min))
            last(V.tensor_tensor(CMP[:], kept.unsqueeze(2).broadcast_to([P, E, KMAX]),
                                 steps[:].unsqueeze(1).broadcast_to([P, E, KMAX]), ALU.is_gt))
            last(V.tensor_reduce(ntile, CMP[:], AX.X, ALU.add))
            last(V.memset(first, 0.0))
            for e in range(1, E):
                last(V.tensor_tensor(first[:, e:e + 1], first[:, e - 1:e], ntile[:, e - 1:e], ALU.add))
            last(V.tensor_tensor(end, first, ntile, ALU.add))
            last(V.tensor_tensor(JC[:], jota[:].unsqueeze(2).broadcast_to([P, NJ, E]), over(end, NJ), ALU.is_ge))
            last(V.tensor_reduce(JT[:, 0], JC[:], AX.X, ALU.add))
            last(V.tensor_tensor(JC[:], JC[:], over(ntile, NJ), ALU.mult))
            last(V.tensor_reduce(JT[:, 1], JC[:], AX.X, ALU.add))
            last(V.tensor_tensor(JT[:, 1], jota[:], JT[:, 1], ALU.subtract))
            last(V.tensor_scalar(JT[:, 0], JT[:, 0], float(E - 1), None, ALU.min))
            last(V.tensor_scalar(JT[:, 1], JT[:, 1], float(KMAX - 1), float(TM), ALU.min, ALU.mult))
            last(V.scalar_tensor_tensor(JT[:, 2], JT[:, 0], float(CAP), JT[:, 1], ALU.mult, ALU.add))
            last(V.tensor_copy(tables[:, 0], JT[0:1, 0]))
            last(V.tensor_copy(tables[:, 1], JT[0:1, 2]))
            last(V.tensor_tensor(OHALL[:], OHALL[:], over(first, NTOK), ALU.mult))
            last(V.tensor_reduce(own[:], OHALL[:], AX.X, ALU.add))
            last(V.scalar_tensor_tensor(own[:], own[:], float(TM), PALL[:], ALU.mult, ALU.add))
            last(V.tensor_scalar(PALL[:], PALL[:], float(CAP), None, ALU.is_lt))
            last(V.tensor_tensor(yrow[:], own[:], PALL[:], ALU.mult))
            dve.wait_ge(fin_act, 1)
            last(V.tensor_reduce(W1[:], LALL[:], AX.X, ALU.add))
            last(V.reciprocal(W1[:], W1[:]))
            last(V.tensor_tensor(wgt[:], W1[:], PALL[:], ALU.mult))

def experts(nc, xe, w1, b1, w2, b2, ident_d, ye, CAP, NJ, tables, room, passed):
    E, C, FF = w1.shape
    KC = C // P
    FC = FF // P
    NT = TM // P
    assert NJ % 2 == 0
    with ExitStack() as ctx:
        def sb(name, shape, dt=F32):
            return ctx.enter_context(nc.sbuf_tensor(name, shape, dt))

        def ps(name, shape):
            return ctx.enter_context(nc.psum_tensor(name, shape, F32))

        def sem(name):
            return ctx.enter_context(nc.semaphore(name))

        ident = sb("p4_ident", [P, P])
        W1 = sb("w1_sb", [P, 2, KC, FF])
        W2 = sb("w2_sb", [P, 2, FC, C])
        W1S = sb("w1_split", [P, 2, 2, KC, FF], F32R)
        W2S = sb("w2_split", [P, 2, 2, FC, C], F32R)
        B1 = sb("b1_sb", [P, 2, FC])
        B2 = sb("b2_sb", [P, 2, C])
        XR = sb("p4_XR", [P, 2, NT, C])
        XT = sb("p4_XT", [P, KC, TM])
        XS = sb("x_split", [P, 2, KC, TM], F32R)
        HM = sb("HM", [P, 2, TM])
        HS = sb("h_split", [P, 2, FC, TM], F32R)
        W1M = sb("w1_masked", [P, KC, FF])
        W2M = sb("w2_masked", [P, FC, C])
        XM = sb("x_masked", [P, KC, TM])
        HMM = sb("h_masked", [P, 2, TM])
        Y = sb("Y", [P, 2, NT, C])
        ABS = sb("ABS", [P, NT, C])
        ASUM = sb("ASUM", [P, 1])
        psT = ps("p4_psT", [P, KC, TM])
        psH = ps("psH", [P, 2, TM])
        psY = ps("psY", [P, NT, 512])

        id_in, zeroed = sem("id_in"), sem("p4_zeroed")
        w_in = [sem(f"p4_w_in{i}") for i in range(2)]
        b_in = [sem(f"p4_b_in{i}") for i in range(2)]
        x_in = [sem(f"p4_x_in{i}") for i in range(2)]
        y_st = [sem(f"y_st{i}") for i in range(2)]
        t_mm, t_out, x_high, x_low, w_high, w_low, h_mm, h_out, h_high, h_low, y_mm, y_out, abs_out, sum_done = (
            sem(n) for n in ("p4_t_mm", "t_out", "x_high", "x_low", "w_high", "w_low", "h_mm", "h_out", "h_high",
                             "h_low", "y_mm", "y_out", "abs_out", "sum_done"))
        w_mask, x_mask, h_mask = sem("w_mask"), sem("x_mask"), sem("h_mask")
        block = ctx.enter_context(nc.Block())

        def tiles(eng, tile):
            if NJ > 2:
                with eng.Fori(0, NJ // 2 - 1) as i:
                    tile(2 * i, 0, i, False)
                    tile(2 * i + 1, 1, i, False)
            tile(NJ - 2, 0, NJ // 2 - 1, False)
            tile(NJ - 1, 1, NJ // 2 - 1, True)

        @block.sync
        def _(sp):
            sp.dma_start(ident[:], ident_d).then_inc(id_in, 16)

            def load(j, s, before):
                expert = sp.value_load(tables[0:1, 0, bass.ds(j, 1)], min_val=0, max_val=E - 1)
                row = sp.value_load(tables[0:1, 1, bass.ds(j, 1)], min_val=0, max_val=E * CAP - TM)
                if before is not None:
                    sp.wait_ge(t_mm, before)
                    sp.sem_inc(passed, 1)
                sp.dma_start(XR[:, s], xe[bass.ds(row, TM), :].rearrange("(t p) c -> p t c", p=P)) \
                    .then_inc(x_in[s], 16)
                if before is not None:
                    sp.wait_ge(w_low, 2 * before)
                    sp.sem_inc(passed, 1)
                sp.dma_start(W1[:, s], w1[bass.ds(expert, 1)].rearrange("e (h p) f -> p (e h) f", p=P)) \
                    .then_inc(w_in[s], 16)
                sp.dma_start(W2[:, s], w2[bass.ds(expert, 1)].rearrange("e (m p) c -> p (e m) c", p=P)) \
                    .then_inc(w_in[s], 16)
                if before is not None:
                    sp.wait_ge(y_out, before)
                    sp.sem_inc(passed, 1)
                sp.dma_start(B1[:, s], b1[bass.ds(expert, 1)].rearrange("e p m -> p (e m)")).then_inc(b_in[s], 16)
                sp.dma_start(B2[:, s], b2[bass.ds(expert, 1)].rearrange("e c -> (e c)").partition_broadcast(P)) \
                    .then_inc(b_in[s], 16)

            for s in range(2):
                load(s, s, None)
            if NJ > 2:
                with sp.Fori(0, NJ // 2 - 1) as i:
                    for s in range(2):
                        load(2 * i + s + 2, s, 2 * i + s + 1)

        @block.gpsimd
        def _(pool):
            nc.gpsimd.memset(room[:, 0:1], 0.0).then_inc(zeroed, 1)
            nc.gpsimd.memset(Y[:, 1], 0.0).then_inc(zeroed, 1)
            pool.wait_ge(zeroed, 2)

            def add_sum(j):
                pool.wait_ge(abs_out, j + 1)
                pool.wait_ge(sum_done, j)
                nc.gpsimd.tensor_tensor(room[:, 0:1], room[:, 0:1], ASUM[:], ALU.add).then_inc(sum_done, 1)

            def low_weights(j, s):
                for k, (w, masked, parts) in enumerate(((W1, W1M, W1S), (W2, W2M, W2S))):
                    pool.wait_ge(w_mask, 2 * j + k + 1)
                    nc.gpsimd.tensor_tensor(parts[:, s, 1], w[:, s], masked[:], ALU.subtract).then_inc(w_low, 1)

            low_weights(0, 0)

            def tile(j, s, i, last):
                if not last:
                    low_weights(j + 1, 1 - s)
                pool.wait_ge(y_out, j + 1)
                pool.dma_start(ye[bass.ds(j * TM, TM), :].rearrange("(t p) c -> p t c", p=P), Y[:, s]) \
                    .then_inc(y_st[s], 16)
                add_sum(j)

            tiles(pool, tile)
            add_sum(NJ)
            for s in range(2):
                pool.wait_ge(y_st[s], 8 * NJ)

        @block.tensor
        def _(pe):
            def product(out, a, b, start, stop):
                nc.tensor.matmul(out, a[0], b[0], start=start, stop=False)
                nc.tensor.matmul(out, a[0], b[1], start=False, stop=False)
                return nc.tensor.matmul(out, a[1], b[0], start=False, stop=stop)

            def turn(j, s, i):
                pe.wait_ge(x_in[s], i * 16 + 16)
                pe.wait_ge(t_out, j)
                for t in range(NT):
                    for h in range(KC):
                        last = nc.tensor.transpose(psT[:, h, P * t:P * (t + 1)],
                                                   XR[:, s, t, P * h:P * (h + 1)], ident[:])
                last.then_inc(t_mm, 1)

            def hidden(j, s):
                for done, count in ((x_high, j + 1), (x_low, j + 1), (w_high, 2 * j + 1), (w_low, 2 * j + 1)):
                    pe.wait_ge(done, count)
                for m in range(FC):
                    pe.wait_ge(h_out, j * FC + max(m - 1, 0))
                    for h in range(KC):
                        prod = product(psH[:, m % 2], [W1S[:, s, k, h, P * m:P * (m + 1)] for k in range(2)],
                                       [XS[:, k, h] for k in range(2)], h == 0, h == KC - 1)
                    prod.then_inc(h_mm, 1)

            def output(j, s):
                pe.wait_ge(w_high, 2 * j + 2)
                pe.wait_ge(w_low, 2 * j + 2)
                pe.wait_ge(y_out, j)
                for m in range(FC):
                    pe.wait_ge(h_high, j * FC + m + 1)
                    pe.wait_ge(h_low, j * FC + m + 1)
                    for t in range(NT):
                        prod = product(psY[:, t, :C], [HS[:, k, m, P * t:P * (t + 1)] for k in range(2)],
                                       [W2S[:, s, k, m] for k in range(2)], m == 0, m == FC - 1)
                prod.then_inc(y_mm, 1)

            pe.wait_ge(id_in, 16)
            turn(0, 0, 0)

            def tile(j, s, i, last):
                hidden(j, s)
                if not last:
                    turn(j + 1, 1 - s, i + s)
                output(j, s)

            tiles(pe, tile)

        @block.scalar
        def _(act):
            def columns(j):
                act.wait_ge(t_mm, j + 1)
                act.wait_ge(x_low, j)
                nc.scalar.activation(XT[:], psT[:], ACT.Copy).then_inc(t_out, 1)

            def absolute(j, s):
                act.wait_ge(y_out, j)
                act.wait_ge(sum_done, j)
                nc.scalar.activation(ABS[:], Y[:, s], ACT.Abs, accum_out=ASUM[:]).then_inc(abs_out, 1)

            def high_hidden(j, m):
                act.wait_ge(h_mask, j * FC + m + 1)
                nc.scalar.activation(HS[:, 0, m], HMM[:, m % 2], ACT.Copy).then_inc(h_high, 1)

            def high_inputs(j, s):
                for k, (masked, parts) in enumerate(((W1M, W1S), (W2M, W2S))):
                    act.wait_ge(w_mask, 2 * j + k + 1)
                    nc.scalar.activation(parts[:, s, 0], masked[:], ACT.Copy).then_inc(w_high, 1)
                    if k == 0:
                        act.wait_ge(x_mask, j + 1)
                        nc.scalar.activation(XS[:, 0], XM[:], ACT.Copy).then_inc(x_high, 1)

            act.wait_ge(zeroed, 2)
            columns(0)
            high_inputs(0, 0)

            def tile(j, s, i, last):
                act.wait_ge(b_in[s], i * 32 + 32)
                act.wait_ge(y_mm, j)
                for m in range(FC):
                    act.wait_ge(h_mm, j * FC + m + 1)
                    act.wait_ge(h_low, j * FC + max(m - 1, 0))
                    nc.scalar.activation(HM[:, m % 2], psH[:, m % 2], ACT.Relu, bias=B1[:, s, m:m + 1]) \
                        .then_inc(h_out, 1)
                    if m == 0:
                        absolute(j, 1 - s)
                    else:
                        high_hidden(j, m - 1)
                high_hidden(j, FC - 1)
                if not last:
                    columns(j + 1)
                    high_inputs(j + 1, 1 - s)

            tiles(act, tile)
            absolute(NJ, 1)

        @block.vector
        def _(dve):
            def mask(masked, whole):
                return nc.vector.tensor_scalar(masked.bitcast(I32), whole.bitcast(I32), -4096, None, ALU.bitwise_and)

            def mask_weights(j, s, i):
                dve.wait_ge(w_in[s], i * 32 + 32)
                dve.wait_ge(w_high, 2 * j)
                dve.wait_ge(w_low, 2 * j)
                mask(W1M[:], W1[:, s]).then_inc(w_mask, 1)
                mask(W2M[:], W2[:, s]).then_inc(w_mask, 1)

            def split_columns(j):
                dve.wait_ge(t_out, j + 1)
                dve.wait_ge(x_high, j)
                mask(XM[:], XT[:]).then_inc(x_mask, 1)
                dve.wait_ge(x_mask, j + 1)
                nc.vector.tensor_tensor(XS[:, 1], XT[:], XM[:], ALU.subtract).then_inc(x_low, 1)

            mask_weights(0, 0, 0)
            split_columns(0)

            def tile(j, s, i, last):
                dve.wait_ge(y_mm, j)
                for m in range(FC):
                    dve.wait_ge(h_out, j * FC + m + 1)
                    dve.wait_ge(h_high, j * FC + max(m - 1, 0))
                    mask(HMM[:, m % 2], HM[:, m % 2]).then_inc(h_mask, 1)
                    dve.wait_ge(h_mask, j * FC + m + 1)
                    nc.vector.tensor_tensor(HS[:, 1, m], HM[:, m % 2], HMM[:, m % 2], ALU.subtract) \
                        .then_inc(h_low, 1)
                if not last:
                    mask_weights(j + 1, 1 - s, i + s)
                    split_columns(j + 1)
                dve.wait_ge(y_mm, j + 1)
                dve.wait_ge(b_in[s], i * 32 + 32)
                dve.wait_ge(y_st[s], i * 16)
                dve.wait_ge(abs_out, j + 1)
                nc.vector.tensor_tensor(Y[:, s], psY[:, :, :C], B2[:, s].unsqueeze(1).broadcast_to([P, NT, C]), ALU.add) \
                    .then_inc(y_out, 1)

            tiles(dve, tile)


def all_partitions(nc, ident_d, values, flag, op, limit, compare, tag):
    with ExitStack() as ctx:
        ident = ctx.enter_context(nc.sbuf_tensor(f"{tag}_ident", [P, P], F32))
        red = ctx.enter_context(nc.sbuf_tensor(f"{tag}_red", [1, 2], F32))
        row = ctx.enter_context(nc.psum_tensor(f"{tag}_row", [P, P], F32))
        id_in, step = (ctx.enter_context(nc.semaphore(f"{tag}_{n}")) for n in ("in", "step"))
        block = ctx.enter_context(nc.Block())

        @block.sync
        def _(sp):
            sp.dma_start(ident[:], ident_d).then_inc(id_in, 16)

        @block.tensor
        def _(pe):
            pe.wait_ge(id_in, 16)
            nc.tensor.transpose(row[0:1], values, ident[:]).then_inc(step, 1)

        @block.vector
        def _(dve):
            dve.wait_ge(step, 1)
            nc.vector.tensor_reduce(red[:, 0:1], row[0:1], AX.X, op).then_inc(step, 1)
            dve.wait_ge(step, 2)
            nc.vector.tensor_scalar(red[:, 1:2], red[:, 0:1], limit, None, compare).then_inc(step, 1)
            dve.wait_ge(step, 3)
            nc.vector.tensor_copy(flag, red[:, 1:2]).then_inc(step, 1)
            dve.wait_ge(step, 4)


def combine(nc, x1, ye, ident_d, out, yrow, wgt, flag, passed, HUGE=3.4028234663852886e38):
    B, C, HW = x1.shape
    KC = C // P
    N = 512
    NT = N // P
    NCH = HW // N
    with ExitStack() as ctx:
        def sb(name, shape, dt=F32):
            return ctx.enter_context(nc.sbuf_tensor(name, shape, dt))

        def ps(name, shape):
            return ctx.enter_context(nc.psum_tensor(name, shape, F32))

        def sem(name):
            return ctx.enter_context(nc.semaphore(name))

        ident = sb("p5_ident", [P, P])
        YG = sb("YG", [P, 4, NT, C])
        XC = sb("p5_XC", [P, 4, KC, N])
        PART = sb("PART", [P, 2, NT, C])
        TEST = sb("TEST", [P, NT, C])
        IDX = sb("p5_IDX", [P, 4, NT], U32)
        WS = sb("WS", [P, 4, NT])
        psT = ps("p5_psT", [P, 2, KC, N])

        id_in = sem("p5_id_in")
        g_in = [sem(f"g_in{i}") for i in range(4)]
        x_in = [sem(f"p5_x_in{i}") for i in range(4)]
        o_st = [sem(f"o_st{i}") for i in range(4)]
        pick, scaled, clean, t_mm, added, fix = (sem(n) for n in ("pick", "scaled", "clean", "p5_t_mm", "added", "fix"))
        block = ctx.enter_context(nc.Block())
        assert NCH % 4 == 0
        QS = NCH // 4

        @block.sync
        def _(sp):
            sp.dma_start(ident[:], ident_d).then_inc(id_in, 16)
            with sp.Fori(0, B) as n:
                for c in range(NCH):
                    sp.wait_ge(o_st[c % 4], n * (16 * QS) + 16 * (c // 4))
                    sp.dma_start(XC[:, c % 4], x1[n, :, N * c:N * (c + 1)].rearrange("(h p) w -> p h w", p=P)) \
                        .then_inc(x_in[c % 4], 16)

        @block.gpsimd
        def _(pool):
            with pool.Fori(0, B) as n:
                for c in range(NCH):
                    pool.wait_ge(pick, n * NCH + c + 1)
                    pool.wait_ge(t_mm, n * NCH + max(c - 3, 0))
                    pool.sem_inc(passed, 1)
                    for t in range(NT):
                        pool.indirect_dma_start(
                            out=YG[:, c % 4, t], out_offset=None, in_=ye,
                            in_offset=bass.IndirectOffsetOnAxis(ap=IDX[:, c % 4, t:t + 1], axis=0)) \
                            .then_inc(g_in[c % 4], 16)

        def store(act, n, c):
            act.wait_ge(added, n * NCH + c + 1)
            act.dma_start(out[n, :, N * c:N * (c + 1)].rearrange("(h p) w -> p h w", p=P), XC[:, c % 4]) \
                .then_inc(o_st[c % 4], 16)

        @block.scalar
        def _(act):
            with act.Fori(0, B) as n:
                for c in range(NCH):
                    act.wait_ge(g_in[c % 4], n * (16 * NT * QS) + 16 * NT * (c // 4 + 1))
                    for t in range(NT):
                        last = nc.scalar.activation(YG[:, c % 4, t], YG[:, c % 4, t], ACT.Copy,
                                                    scale=WS[:, c % 4, t:t + 1])
                    last.then_inc(scaled, 1)
                    if c >= 1:
                        store(act, n, c - 1)
                store(act, n, NCH - 1)
            for s in range(4):
                act.wait_ge(o_st[s], 16 * QS * B)

        @block.tensor
        def _(pe):
            pe.wait_ge(id_in, 16)
            with pe.Fori(0, B) as n:
                for c in range(NCH):
                    pe.wait_ge(clean, n * NCH + c + 1)
                    pe.wait_ge(added, n * NCH + max(c - 1, 0))
                    for h in range(KC):
                        for t in range(NT):
                            last = nc.tensor.transpose(psT[:, c % 2, h, P * t:P * (t + 1)],
                                                       YG[:, c % 4, t, P * h:P * (h + 1)], ident[:])
                    last.then_inc(t_mm, 1)

        @block.vector
        def _(dve):
            V = nc.vector
            finite = dve.value_load(flag, min_val=0, max_val=1)

            def choose(n, c):
                dve.wait_ge(scaled, n * NCH + max(c - 3, 0))
                tiles = bass.ds(n * (NT * NCH) + NT * c, NT)
                V.tensor_copy(WS[:, c % 4], wgt[:, tiles])
                V.tensor_copy(IDX[:, c % 4], yrow[:, tiles]).then_inc(pick, 1)

            with dve.Fori(0, B) as n:
                for c in range(3):
                    choose(n, c)
                for c in range(NCH):
                    if c + 3 < NCH:
                        choose(n, c + 3)
                    dve.wait_ge(scaled, n * NCH + c + 1)
                    dve.sem_inc(passed, 1)
                    with dve.If(finite < 1):
                        y = YG[:, c % 4]
                        done = [0]

                        def step(ins):
                            done[0] += 1
                            ins.then_inc(fix, 1)
                            dve.wait_ge(fix, n * (10 * NCH) + 10 * c + done[0])

                        for part, keep, cap, beyond, within in ((PART[:, 0], ALU.max, 1.0, ALU.is_gt, ALU.is_le),
                                                                (PART[:, 1], ALU.min, -1.0, ALU.is_lt, ALU.is_ge)):
                            clip = ALU.min if cap > 0 else ALU.max
                            step(V.tensor_scalar(part, y, 0.0, cap * HUGE, keep, clip))
                            step(V.tensor_scalar(TEST[:], y, 0.0, cap * HUGE, keep, within))
                            step(V.tensor_tensor(part, part, TEST[:], ALU.mult))
                            step(V.tensor_scalar(TEST[:], y, 0.0, cap * HUGE, keep, beyond))
                            step(V.scalar_tensor_tensor(part, TEST[:], cap * 1e4, part, ALU.mult, ALU.add))
                        V.tensor_tensor(y, PART[:, 0], PART[:, 1], ALU.add)
                    dve.drain().then_inc(clean, 1)
                    dve.wait_ge(x_in[c % 4], n * (16 * QS) + 16 * (c // 4) + 16)
                    dve.wait_ge(t_mm, n * NCH + c + 1)
                    V.tensor_tensor(XC[:, c % 4], XC[:, c % 4], psT[:, c % 2], ALU.add).then_inc(added, 1)


def metaformer_layer(nc, x, dw_w, dw_b, om_w, om_b, vp_w, vp_b, op_w, op_b, gate_w, gate_b, w1, b1, w2, b2,
                     cst, out):
    B, C, HW = x.shape
    W = 64
    H = HW // W
    T = B * HW
    E = w1.shape[0]
    CAP = -(-5 * T // (4 * E))
    NJ = T // TM + E
    OM = om_w.shape[1]
    rows = BH * -(-H // BH) + 2 * HALO
    assert CAP % TM == 0 and T % TM == 0

    def dram(name, shape, dt=F32):
        return nc.dram_tensor(name, shape, dt, kind="Internal").ap()

    v_pad = dram("v_pad", (B, rows, W + 2 * HALO, C))
    xn = dram("xn", (B, C, HW))
    om_raw = dram("om_raw", (B, HW // P, P, OM))
    taps_t = dram("taps_t", (B, PARTS * C // P, P, HW), BF16)
    sampled = dram("sampled", (T // P, P, C))
    x1 = dram("x1", (B, C, HW))
    xe = dram("xe", (E * CAP + T, C))
    ye = dram("ye", (NJ * TM, C))
    with ExitStack() as ctx:
        def sb(name, shape, dt=F32):
            return ctx.enter_context(nc.sbuf_tensor(name, shape, dt))

        passed = ctx.enter_context(nc.semaphore("passed"))
        room = sb("room", [P, 2])
        near = sb("near", [1, 1], I32)
        finite = sb("finite", [1, 1], I32)
        tables = sb("tables", [1, 2, NJ], I32)
        yrow = sb("yrow", [P, T // P], U32)
        wgt = sb("wgt", [P, T // P])
        conv_features(nc, x, dw_w, dw_b, om_w, om_b, vp_w, vp_b, cst["ident"], cst["mean"],
                      xn, v_pad, om_raw, taps_t, xe[0:E * CAP], room, passed)
        all_partitions(nc, cst["ident"], room[:, 0:1], near[:], ALU.add, 0.0, ALU.is_le, "near")
        deform(nc, x, op_w, op_b, cst["select"], v_pad, taps_t, x1, passed)
        resample(nc, x, op_w, op_b, cst["ident"], cst["pix"], cst["geo"], v_pad, om_raw, sampled, x1, near[:])
        route(nc, x1, gate_w, gate_b, cst, xe, CAP, NJ, tables, yrow, wgt, passed)
        experts(nc, xe, w1, b1, w2, b2, cst["ident"], ye, CAP, NJ, tables, room, passed)
        all_partitions(nc, cst["ident"], room[:, 0:1], finite[:], ALU.add, 3.4028234663852886e38, ALU.is_le, "fin")
        combine(nc, x1, ye, cst["ident"], out, yrow, wgt, finite[:], passed)


def constants(np, B, H, W, C, E):
    T = B * H * W
    cap = -(-5 * T // (4 * E))
    p, q = np.arange(P), np.arange(PT)
    last = (BH - 1) * RW + BW - 1
    select = np.zeros((P, last + P))
    for g in range(P // TAPP):
        for tap in range(TAPS):
            select[TAPP * g + tap, last + tap // 5 * RW + tap % 5] = 1
    pix = np.zeros((P, 2, PT))
    pix[:, 0] = (p % W)[:, None] + HALO - 1 + q // 3
    pix[:, 1] = (p // W)[:, None] + HALO - 1 + q % 3
    tile, g = np.arange(T // P)[:, None], np.arange(G)[None]
    rows = BH * -(-H // BH) + 2 * HALO
    per = H * W // P
    geo = np.stack([P // W * (tile % per) + 0 * g, tile // per * rows * (W + 2 * HALO) * G + g], -1)
    made = {
        "ident": np.eye(P), "mean": np.full((P, P), 1 / C), "select": select, "pix": pix,
        "geo": geo.reshape(-1, 2), "tri": np.triu(np.ones((P, P)), 1), "own": E * cap + np.arange(T // P)[None] * P + p[:, None],
        "rank": E - np.arange(E), "ebase": np.arange(E) * cap, "steps": np.arange(cap // TM) * TM,
        "jota": np.arange(T // TM + E),
    }
    return {k: v.astype(np.float32) for k, v in made.items()}


def kernel(**inputs):
    import numpy as _np
    import concourse.bacc as _bacc
    from concourse.bass_utils import run_bass_kernel_spmd as _run

    nc = _bacc.Bacc("TRN2", target_bir_lowering=False, num_devices=1)
    a = {k: _np.asarray(v) for k, v in inputs.items()}
    B, C, H, W = a["x"].shape
    E, _, FF = a["L0_ffn_w1"].shape
    given = {
        "x": a["x"].reshape(B, C, H * W),
        "dw_w": a["L0_conv_dw_w"].reshape(C, 9), "dw_b": a["L0_conv_dw_b"].reshape(C // P, P).T,
        "om_w": a["L0_conv_om_w"].T, "om_b": a["L0_conv_om_b"],
        "vp_w": a["L0_conv_vp_w"].T, "vp_b": a["L0_conv_vp_b"],
        "op_w": a["L0_conv_op_w"].T, "op_b": a["L0_conv_op_b"].reshape(C // P, P).T,
        "gate_w": a["L0_ffn_gate_w"], "gate_b": a["L0_ffn_gate_b"],
        "w1": a["L0_ffn_w1"], "b1": a["L0_ffn_b1"].reshape(E, FF // P, P).transpose(0, 2, 1),
        "w2": a["L0_ffn_w2"], "b2": a["L0_ffn_b2"],
    }
    tables = constants(_np, B, H, W, C, E)
    arrays = {f"in_{k}": _np.ascontiguousarray(v) for k, v in {**given, **tables}.items()}
    aps = {k: nc.dram_tensor(k, v.shape, F32, kind="ExternalInput").ap() for k, v in arrays.items()}
    out = nc.dram_tensor("out_0", (B, C, H * W), F32, kind="ExternalOutput").ap()
    metaformer_layer(nc, *[aps[f"in_{k}"] for k in given], {k: aps[f"in_{k}"] for k in tables}, out)
    r = _run(nc, [arrays], core_ids=[0])
    return r.results[0]["out_0"].reshape(B, C, H, W)
```
